# Optimizing a Trainium2 kernel written in Bass

```python
import numpy as np
import jax
import jax.numpy as jnp

def _softmax(x, axis=-1):
    return jax.nn.softmax(x, axis=axis)

def _gelu(x):
    return jax.nn.gelu(x, approximate=True)

def _silu(x):
    return jax.nn.silu(x)

def _sigmoid(x):
    return jax.nn.sigmoid(x)

def _layernorm(x, axis=-1, eps=1e-05):
    m = jnp.mean(x, axis=axis, keepdims=True)
    v = jnp.var(x, axis=axis, keepdims=True)
    return (x - m) / jnp.sqrt(v + eps)

def _scatter_add(tgt, idx, src, axis=0):
    return tgt.at[idx].add(src)

def _segment_sum(src, seg, n):
    return jax.ops.segment_sum(src, seg, n)
kernel_name = 'mk_seq_preln_d1_jaxref_r8_8a06d8'

def setup_inputs(seed: int=0):
    np.random.seed(seed)
    _w = jnp.asarray

    def _L0_attn_setup():
        import jax, jax.numpy as jnp
        import numpy as np
        D_MODEL, N_HEADS, D_STATE, N_GROUPS, CHUNK = (256, 32, 64, 1, 32)
        BATCH, SEQLEN = (2, 512)

        def segsum(v):
            cs = jnp.cumsum(v, axis=-1)
            seg = cs[..., :, None] - cs[..., None, :]
            T = v.shape[-1]
            mask = jnp.tril(jnp.ones((T, T), bool))
            return jnp.where(mask, seg, -jnp.inf)

        def _ssd(x, A_log, D, B_w, B_b, C_w, C_b, dt_w, dt_b, out_w, out_b):
            b, t, d = x.shape
            h = A_log.shape[0]
            n = B_w.shape[0] // N_GROUPS
            p = d // h
            l = CHUNK
            c = t // l
            A = -jnp.exp(A_log.astype(jnp.float32))
            B = (x @ B_w.T + B_b).reshape(b, t, N_GROUPS, n)
            C = (x @ C_w.T + C_b).reshape(b, t, N_GROUPS, n)
            B = jnp.broadcast_to(B, (b, t, h, n))
            C = jnp.broadcast_to(C, (b, t, h, n))
            dt = jax.nn.softplus(x @ dt_w.T + dt_b)
            xh = x.reshape(b, t, h, p)
            xc = xh.reshape(b, c, l, h, p)
            Bc = B.reshape(b, c, l, h, n)
            Cc = C.reshape(b, c, l, h, n)
            dtc = dt.reshape(b, c, l, h)
            dA = jnp.transpose(dtc * A, (0, 3, 1, 2))
            A_cumsum = jnp.cumsum(dA, axis=-1)
            L = jnp.exp(segsum(dA))
            xdt = xc * dtc[..., None]
            Y_diag = jnp.einsum('bclhn,bcshn,bhcls,bcshp->bclhp', Cc, Bc, L, xdt)
            decay_states = jnp.exp(A_cumsum[..., -1:] - A_cumsum)
            states = jnp.einsum('bclhn,bhcl,bclhp->bchpn', Bc, decay_states, xdt)
            states = jnp.concatenate([jnp.zeros_like(states[:, :1]), states], axis=1)
            dA_last = jnp.pad(A_cumsum[..., -1], ((0, 0), (0, 0), (1, 0)))
            decay_chunk = jnp.exp(segsum(dA_last))
            new_states = jnp.einsum('bhzc,bchpn->bzhpn', decay_chunk, states)
            prev_states = new_states[:, :-1]
            state_decay_out = jnp.exp(A_cumsum)
            Y_off = jnp.einsum('bclhn,bchpn,bhcl->bclhp', Cc, prev_states, state_decay_out)
            Y = (Y_diag + Y_off).reshape(b, t, h, p) + D[None, None, :, None] * xh
            return Y.reshape(b, t, d) @ out_w.T + out_b
        key = jax.random.key(seed)
        ks = jax.random.split(key, 8)
        s = 0.02
        d, h, n, g = (D_MODEL, N_HEADS, D_STATE, N_GROUPS)
        return {'x': jax.random.normal(ks[0], (BATCH, SEQLEN, d), jnp.float32), 'A_log': jnp.log(jnp.arange(1, h + 1, dtype=jnp.float32)), 'D': jnp.ones((h,), jnp.float32), 'B_w': jax.random.normal(ks[1], (g * n, d), jnp.float32) * s, 'B_b': jnp.zeros((g * n,), jnp.float32), 'C_w': jax.random.normal(ks[2], (g * n, d), jnp.float32) * s, 'C_b': jnp.zeros((g * n,), jnp.float32), 'dt_w': jax.random.normal(ks[3], (h, d), jnp.float32) * s, 'dt_b': jnp.zeros((h,), jnp.float32), 'out_w': jax.random.normal(ks[4], (d, d), jnp.float32) * s, 'out_b': jnp.zeros((d,), jnp.float32)}
    _L0_attn_in = _L0_attn_setup()

    def _L0_ffn_setup():
        import jax, jax.numpy as jnp
        import numpy as np
        B, S, H = (4, 128, 256)
        E, K, I, SI = (16, 4, 176, 704)

        def _silu_mul(gu, inter):
            return jax.nn.silu(gu[:, :inter]) * gu[:, inter:]
        key = jax.random.key(seed)
        ks = jax.random.split(key, 7)
        s = 0.02
        return {'hidden_states': jax.random.normal(ks[0], (B, S, H), jnp.float32), 'gate_w': jax.random.normal(ks[1], (E, H), jnp.float32) * s, 'expert_gate_up': jax.random.normal(ks[2], (E, 2 * I, H), jnp.float32) * s, 'expert_down': jax.random.normal(ks[3], (E, H, I), jnp.float32) * s, 'shared_gate_up': jax.random.normal(ks[4], (2 * SI, H), jnp.float32) * s, 'shared_down': jax.random.normal(ks[5], (H, SI), jnp.float32) * s, 'shared_gate_vec': jax.random.normal(ks[6], (1, H), jnp.float32) * s}
    _L0_ffn_in = _L0_ffn_setup()
    _d = {'L0_attn_x': _L0_attn_in['x'], 'L0_attn_A_log': _L0_attn_in['A_log'], 'L0_attn_D': _L0_attn_in['D'], 'L0_attn_B_w': _L0_attn_in['B_w'], 'L0_attn_B_b': _L0_attn_in['B_b'], 'L0_attn_C_w': _L0_attn_in['C_w'], 'L0_attn_C_b': _L0_attn_in['C_b'], 'L0_attn_dt_w': _L0_attn_in['dt_w'], 'L0_attn_dt_b': _L0_attn_in['dt_b'], 'L0_attn_out_w': _L0_attn_in['out_w'], 'L0_attn_out_b': _L0_attn_in['out_b'], 'L0_ffn_gate_w': _L0_ffn_in['gate_w'], 'L0_ffn_expert_gate_up': _L0_ffn_in['expert_gate_up'], 'L0_ffn_expert_down': _L0_ffn_in['expert_down'], 'L0_ffn_shared_gate_up': _L0_ffn_in['shared_gate_up'], 'L0_ffn_shared_down': _L0_ffn_in['shared_down'], 'L0_ffn_shared_gate_vec': _L0_ffn_in['shared_gate_vec']}
    _x0 = _d['L0_attn_x']
    _d['L0_attn_x'] = jax.random.normal(jax.random.fold_in(jax.random.key(seed), 1), (4, 512, 256), dtype=_x0.dtype)
    del _x0
    return _d

def reference(L0_attn_x, L0_attn_A_log, L0_attn_D, L0_attn_B_w, L0_attn_B_b, L0_attn_C_w, L0_attn_C_b, L0_attn_dt_w, L0_attn_dt_b, L0_attn_out_w, L0_attn_out_b, L0_ffn_gate_w, L0_ffn_expert_gate_up, L0_ffn_expert_down, L0_ffn_shared_gate_up, L0_ffn_shared_down, L0_ffn_shared_gate_vec):

    def _L0_attn_ref(x, A_log, D, B_w, B_b, C_w, C_b, dt_w, dt_b, out_w, out_b):
        import jax, jax.numpy as jnp
        import numpy as np
        D_MODEL, N_HEADS, D_STATE, N_GROUPS, CHUNK = (256, 32, 64, 1, 32)
        BATCH, SEQLEN = (2, 512)

        def segsum(v):
            cs = jnp.cumsum(v, axis=-1)
            seg = cs[..., :, None] - cs[..., None, :]
            T = v.shape[-1]
            mask = jnp.tril(jnp.ones((T, T), bool))
            return jnp.where(mask, seg, -jnp.inf)

        def _ssd(x, A_log, D, B_w, B_b, C_w, C_b, dt_w, dt_b, out_w, out_b):
            b, t, d = x.shape
            h = A_log.shape[0]
            n = B_w.shape[0] // N_GROUPS
            p = d // h
            l = CHUNK
            c = t // l
            A = -jnp.exp(A_log.astype(jnp.float32))
            B = (x @ B_w.T + B_b).reshape(b, t, N_GROUPS, n)
            C = (x @ C_w.T + C_b).reshape(b, t, N_GROUPS, n)
            B = jnp.broadcast_to(B, (b, t, h, n))
            C = jnp.broadcast_to(C, (b, t, h, n))
            dt = jax.nn.softplus(x @ dt_w.T + dt_b)
            xh = x.reshape(b, t, h, p)
            xc = xh.reshape(b, c, l, h, p)
            Bc = B.reshape(b, c, l, h, n)
            Cc = C.reshape(b, c, l, h, n)
            dtc = dt.reshape(b, c, l, h)
            dA = jnp.transpose(dtc * A, (0, 3, 1, 2))
            A_cumsum = jnp.cumsum(dA, axis=-1)
            L = jnp.exp(segsum(dA))
            xdt = xc * dtc[..., None]
            Y_diag = jnp.einsum('bclhn,bcshn,bhcls,bcshp->bclhp', Cc, Bc, L, xdt)
            decay_states = jnp.exp(A_cumsum[..., -1:] - A_cumsum)
            states = jnp.einsum('bclhn,bhcl,bclhp->bchpn', Bc, decay_states, xdt)
            states = jnp.concatenate([jnp.zeros_like(states[:, :1]), states], axis=1)
            dA_last = jnp.pad(A_cumsum[..., -1], ((0, 0), (0, 0), (1, 0)))
            decay_chunk = jnp.exp(segsum(dA_last))
            new_states = jnp.einsum('bhzc,bchpn->bzhpn', decay_chunk, states)
            prev_states = new_states[:, :-1]
            state_decay_out = jnp.exp(A_cumsum)
            Y_off = jnp.einsum('bclhn,bchpn,bhcl->bclhp', Cc, prev_states, state_decay_out)
            Y = (Y_diag + Y_off).reshape(b, t, h, p) + D[None, None, :, None] * xh
            return Y.reshape(b, t, d) @ out_w.T + out_b
        return _ssd(x, A_log, D, B_w, B_b, C_w, C_b, dt_w, dt_b, out_w, out_b)

    def _L0_ffn_ref(hidden_states, gate_w, expert_gate_up, expert_down, shared_gate_up, shared_down, shared_gate_vec):
        import jax, jax.numpy as jnp
        import numpy as np
        B, S, H = (4, 128, 256)
        E, K, I, SI = (16, 4, 176, 704)

        def _silu_mul(gu, inter):
            return jax.nn.silu(gu[:, :inter]) * gu[:, inter:]
        orig_shape = hidden_states.shape
        x = hidden_states.reshape(-1, H)
        router_logits = x @ gate_w.T
        routing_probs = jax.nn.softmax(router_logits.astype(jnp.float32), axis=-1)
        topk_w, topk_idx = jax.lax.top_k(routing_probs, K)
        topk_w = topk_w / topk_w.sum(axis=-1, keepdims=True)
        topk_w = topk_w.astype(x.dtype)
        combine = (jax.nn.one_hot(topk_idx, E, dtype=x.dtype) * topk_w[..., None]).sum(1)
        shared = _silu_mul(x @ shared_gate_up.T, SI) @ shared_down.T
        shared = shared * jax.nn.sigmoid(x @ shared_gate_vec.T)

        def step(acc, ew):
            w_gu, w_d, cw = ew
            h = _silu_mul(x @ w_gu.T, I)
            return (acc + h @ w_d.T * cw[:, None], None)
        acc0 = jnp.zeros_like(x)
        sparse, _ = jax.lax.scan(step, acc0, (expert_gate_up, expert_down, combine.T))
        return (shared + sparse).reshape(orig_shape)
    x = L0_attn_x
    x = x + _L0_attn_ref(_layernorm(x, axis=-1), L0_attn_A_log, L0_attn_D, L0_attn_B_w, L0_attn_B_b, L0_attn_C_w, L0_attn_C_b, L0_attn_dt_w, L0_attn_dt_b, L0_attn_out_w, L0_attn_out_b)
    x = x + _L0_ffn_ref(_layernorm(x, axis=-1), L0_ffn_gate_w, L0_ffn_expert_gate_up, L0_ffn_expert_down, L0_ffn_shared_gate_up, L0_ffn_shared_down, L0_ffn_shared_gate_vec)
    return x

_drawn_inputs = setup_inputs


def setup_inputs(seed=0):
    import zlib

    import numpy as np

    out = dict(_drawn_inputs(seed))
    spreads = {'L0_attn_D': (1.0, 0.2),
     'L0_attn_B_b': (0.0, 0.1),
     'L0_attn_C_b': (0.0, 0.1),
     'L0_attn_dt_b': (0.0, 0.634),
     'L0_attn_out_b': (0.0, 0.1)}
    factors = {'L0_ffn_gate_w': 8.0,
     'L0_ffn_expert_gate_up': 8.0,
     'L0_ffn_expert_down': 8.0,
     'L0_ffn_shared_gate_up': 4.263,
     'L0_ffn_shared_down': 4.268,
     'L0_ffn_shared_gate_vec': 8.0}
    for name, (base, spread) in spreads.items():
        noise = np.random.default_rng([zlib.crc32(name.encode()), seed]).standard_normal(out[name].shape)
        drawn = base * np.exp(spread * noise) if base else spread * noise
        out[name] = jnp.asarray(drawn.astype(out[name].dtype))
    for name, factor in factors.items():
        out[name] = (out[name] * factor).astype(out[name].dtype)
    return out
```

```python
from contextlib import ExitStack

import numpy as np

import concourse.bass as bass
from concourse import mybir

ALU = mybir.AluOpType
ACT = mybir.ActivationFunctionType
AX = mybir.AxisListType
F32 = mybir.dt.float32
F32R = mybir.dt.float32r
I32 = mybir.dt.int32
U32 = mybir.dt.uint32

P = 128
L = 32
C = P // L
BATCH, SEQ, D = 4, 512, 256
GROUPS = SEQ // P
NT = BATCH * GROUPS
T = NT * P
PAIRS = NT // 2
K2 = D // P
H, HD = 32, 8
HQ, HG = 4, 8
N = 64
E, TOPK, EI, SI = 16, 4, 176, 704
EPS = 1e-5
XT = 80
ROWS = T * TOPK
ER = 17

WU = K2 * 2 * EI
WD = 2 * D
WC = WU + WD
SH = E - 4
EK = EI // 2
XG = 4

CONSTS = {}
RCONSTS = {}


def constants():
    r = np.arange(P)
    blk, pos = r // L, r % L
    same = blk[:, None] == blk[None, :]
    parts = {
        "ident": np.eye(P),
        "after": same & (pos[:, None] > pos[None, :]),
        "upto": same & (pos[:, None] <= pos[None, :]),
        "spread": pos[:, None] == pos[None, :],
        "tri": pos[:, None] <= np.arange(L)[None, :],
        "chunk": np.repeat(np.arange(C), N)[None, :] == blk[:, None],
    }
    routing = {
        "ones": np.ones((P, P)),
        "before": r[:, None] < r[None, :],
        "iota_e": np.broadcast_to(np.arange(E), (P, E)),
        "edges": np.broadcast_to(np.arange(NT) * P, (P, NT)),
        "keep": np.broadcast_to((np.arange(E * NT) % NT) != 0, (P, E * NT)),
        "tiles": np.broadcast_to(np.arange(XT + XG), (P, XT + XG)),
    }
    arrays = []
    for where, group in ((CONSTS, parts), (RCONSTS, routing)):
        at = 0
        for name, a in group.items():
            where[name] = (at, a.shape[1])
            at += a.shape[1]
        arrays.append(np.concatenate([np.asarray(a, np.float32) for a in group.values()], 1))
    return arrays


constants()
NC = sum(n for _, n in CONSTS.values())
NRC = sum(n for _, n in RCONSTS.values())
WS = {"bd": (0, N + H), "cc": (N + H, 2 * N), "wo": (N + H + 2 * N, D), "wg": (N + H + 2 * N + D, 32)}
NW = N + H + 2 * N + D + 32


def build(nc, x, w_small, w_bias, a_log, d_row, ob_row, cst_in, rcst_in, w_units, out):
    es = ExitStack()
    with es:
        names = {}

        def sem(name):
            return es.enter_context(nc.semaphore(name))

        def sb(name, shape, dt=F32, stack=None):
            return (stack or es).enter_context(nc.sbuf_tensor(name, shape, dt))

        cst = sb("cst", [P, NC])
        res = sb("res", [P, NT, D])
        lgt = sb("lgt", [P, NT, P])
        xg = lgt[:, :, :].rearrange("p (r u) t -> p r (u t)", u=K2)
        wgt = sb("wgt", [P, NT, TOPK])
        sig = sb("sig", [P, NT])
        pair = sb("pair", [P, NT * TOPK], I32)
        slot_i = sb("slot_i", [P, NT * TOPK], I32)
        tab = sb("tab", [P, XT], I32)
        tok = sb("tok", [P, XT], I32)
        epack = sb("epack", [1, XT // XG], I32)
        bank = [es.enter_context(nc.psum_tensor(f"bank{i}", [P, 512], F32)) for i in range(8)]

        def const(name):
            a, n = CONSTS[name]
            return cst[:, a:a + n]

        st = ExitStack()
        w_raw = sb("w_raw", [P, K2, NW], F32, st)
        w_hi = sb("w_hi", [P, K2, NW], F32R, st)
        w_lo = sb("w_lo", [P, K2, NW], F32R, st)
        bias = sb("bias", [P, 2], F32, st)
        a_sb = sb("a_sb", [P, H], F32, st)
        d_sb = sb("d_sb", [P, H], F32, st)
        ob_sb = sb("ob_sb", [P, D], F32, st)
        ones_col = sb("ones_col", [P, 1], F32, st)
        stat6 = sb("stat6", [P, 2, 2, 6], F32, st)
        mv = sb("mv", [P, 2, 2, 2], F32, st)
        var = sb("var", [P, 2, 2], F32, st)
        lnv = sb("lnv", [P, 2, 2], F32, st)
        y0 = sb("y0", [P, 2, 2], F32, st)
        ya = sb("ya", [P, 2], F32, st)
        yb = sb("yb", [P, 2], F32, st)
        rs = sb("rs", [P, 2], F32, st)
        xn = sb("xn", [P, NT, D], F32, st)
        xt_hi = sb("xt_hi", [P, 2, K2, 2 * P], F32R, st)
        xt_lo = sb("xt_lo", [P, 2, K2, 2 * P], F32R, st)
        bdf = sb("bdf", [N + H, 2, 2 * P], F32, st)
        ct = sb("ct", [P, NT, P], F32, st)
        bz = sb("bz", [P, 4, 2, N + H], F32, st)
        gmd = sb("gmd", [P, 2, 2 * P], F32, st)
        gp = sb("gp", [P, NT, P], F32, st)
        na = sb("na", [P, 2, H], F32, st)
        sp_e = sb("sp_e", [P, 2, H], F32, st)
        sp_l = sb("sp_l", [P, 2, H], F32, st)
        dt = sb("dt", [P, 2, 2, H], F32, st)
        da = sb("da", [P, 2, 2, H], F32, st)
        daq = sb("daq", [P, 2, 2, C, HG], F32, st)
        daq_hi = sb("daq_hi", [P, NT, C, HG], F32R, st)
        daq_lo = sb("daq_lo", [P, NT, C, HG], F32R, st)
        ecs = sb("ecs", [P, NT, H], F32, st)
        dec = sb("dec", [P, 2, 2, H], F32, st)
        dch = sb("dch", [P, 4, C, H], F32, st)
        xdt = sb("xdt", [P, 2, 2, D], F32, st)
        xd = sb("xd", [P, 2, 2, D], F32, st)
        bm = sb("bm", [P, 2, 2, C, N], F32, st)
        tmp_s = sb("tmp_s", [P, D], F32, st)
        state = sb("state", [P, GROUPS, 2, C, D], F32, st)
        rr_hi = sb("rr_hi", [P, 2, C * HG, L], F32R, st)
        rr_lo = sb("rr_lo", [P, 2, C * HG, L], F32R, st)
        after_r = sb("after_r", [P, P], F32R, st)
        ex = sb("ex", [P, 2, C * HG, L], F32, st)
        mm = sb("mm", [P, 2, C * HG, L], F32, st)
        xb = sb("xb", [P, 2, C, D], F32, st)
        t1 = sb("t1", [P, D], F32, st)
        t2 = sb("t2", [P, D], F32, st)
        yy = sb("yy", [P, 2, D], F32, st)
        yt_hi = sb("yt_hi", [P, 2, D], F32R, st)
        yt_lo = sb("yt_lo", [P, 2, D], F32R, st)
        stat6b = sb("stat6b", [P, 6], F32, st)
        mvb = sb("mvb", [P, 2], F32, st)
        varb = sb("varb", [P, 1], F32, st)
        lnvb = sb("lnvb", [P, 1], F32, st)
        y0b = sb("y0b", [P, 1], F32, st)
        yab = sb("yab", [P, 1], F32, st)
        ybb = sb("ybb", [P, 1], F32, st)
        rsb = sb("rsb", [P, 1], F32, st)
        xn2 = sb("xn2", [P, 2, D], F32, st)
        x2t = sb("x2t", [P, D], F32, st)

        st.close()

        rt = ExitStack()
        rcst = sb("rcst", [P, NRC], F32, rt)
        lg = sb("lg", [P, NT, 32], F32, rt)
        mx = sb("mx", [P, NT], F32, rt)
        shl = sb("shl", [P, NT, E], F32, rt)
        pe_ = sb("pexp", [P, NT, E], F32, rt)
        sgx = sb("sgx", [P, NT], F32, rt)
        sgy = sb("sgy", [P, NT], F32, rt)
        sm = sb("sm", [P, NT], F32, rt)
        rc = sb("rc", [P, NT], F32, rt)
        prob = sb("prob", [P, NT, E], F32, rt)
        m8 = sb("m8", [P, NT, 8], F32, rt)
        i8 = sb("i8", [P, NT, 8], U32, rt)
        sw = sb("sw", [P, NT], F32, rt)
        rw = sb("rw", [P, NT], F32, rt)
        idf = sb("idf", [P, NT, TOPK], F32, rt)
        oh = sb("oh", [P, NT, TOPK, E], F32, rt)
        msk = sb("msk", [P, E, NT], F32, rt)
        inc = sb("inc", [P, E, NT], F32, rt)
        exc = sb("exc", [P, E, NT], F32, rt)
        gt = sb("gt", [P, E, NT], F32, rt)
        tl = sb("tl", [P, E], F32, rt)
        incl = sb("incl", [P, E], F32, rt)
        base = sb("base", [P, E], F32, rt)
        sl = sb("sl", [P, E, NT], F32, rt)
        sl2 = sb("sl2", [P, E, NT], F32, rt)
        so = sb("so", [P, NT, TOPK, E], F32, rt)
        slf = sb("slf", [P, NT * TOPK], F32, rt)
        si = sb("si", [P, NT * TOPK], I32, rt)
        s_hi7 = sb("s_hi7", [P, NT * TOPK], I32, rt)
        s_lo7 = sb("s_lo7", [P, NT * TOPK], I32, rt)
        le = sb("le", [1, XT + XG, E], F32, rt)
        ef = sb("ef", [1, XT + XG], F32, rt)
        em = sb("em", [1, XT + XG], F32, rt)
        ep = sb("ep", [1, 2, XT // XG], F32, rt)
        init = sb("init", [P, XT], I32, rt)
        rt.close()

        wu_hi = sb("wu_hi", [P, E, WC], F32R)
        wu_lo = sb("wu_lo", [P, E, WC], F32R)
        stage_w = sb("stage_w", [P, 2, WC])
        tx_hi = sb("tx_hi", [P, D], F32R)
        tx_lo = sb("tx_lo", [P, D], F32R)
        act_s = sb("act_s", [P, SI])
        act_h = sb("act_h", [P, 6 * P])
        th_hi = sb("th_hi", [P, 6, P], F32R)
        th_lo = sb("th_lo", [P, 6, P], F32R)
        y_sb = sb("y_sb", [P, 2, D])
        yl = stage_w[:, :, 0:TOPK * D]

        table_d = nc.dram_tensor("table_dram", (P * XT, 1), I32, kind="Internal").ap()
        y_d = nc.dram_tensor("y_dram", (ROWS + P * XT, D), F32, kind="Internal").ap()
        out_v = out.rearrange("b (g p) d -> g b p d", p=P)

        xdt_d = nc.dram_tensor("xdt_dram", (NT, P, D), F32, kind="Internal").ap()
        xn2_d = nc.dram_tensor("xn2_dram", (T, D), F32, kind="Internal").ap()
        x_v = x.rearrange("b (g p) d -> g p b d", p=P)

        s_c = sem("s_const")
        s_x = [sem(f"s_x_in{g}") for g in range(GROUPS)]
        s_w = sem("s_w")
        s_small = sem("s_small")
        s_whi, s_wlo = sem("s_whi"), sem("s_wlo")
        s_zero = sem("s_zero")
        s_ea, s_aneg = sem("s_ea"), sem("s_aneg")
        s_st, s_mv, s_var = sem("s_st"), sem("s_mv"), sem("s_var")
        s_ln, s_y0 = sem("s_ln"), sem("s_y0")
        s_nw = sem("s_nw")
        s_xn = sem("s_xn")
        s_xt, s_xth, s_xtl = sem("s_xt"), sem("s_xth"), sem("s_xtl")
        s_pbd, s_pcc, s_bdf, s_ct = sem("s_pbd"), sem("s_pcc"), sem("s_bdf"), sem("s_ct")
        s_pbz, s_pg, s_bz, s_gmd = sem("s_pbz"), sem("s_pg"), sem("s_bz"), sem("s_gmd")
        s_na, s_spe, s_spl = sem("s_na"), sem("s_spe"), sem("s_spl")
        s_dt, s_da, s_daq, s_dqh, s_dql, s_aft = sem("s_dt"), sem("s_da"), sem("s_daq"), sem("s_dqh"), sem("s_dql"), sem("s_aft")
        s_pd, s_pgp = sem("s_pd"), sem("s_pgp")
        s_dec, s_gp = sem("s_dec"), sem("s_gp")
        s_xdt, s_xd, s_bm, s_xdtw = sem("s_xdt"), sem("s_xd"), sem("s_bm"), [sem("s_xdtw0"), sem("s_xdtw1")]
        s_ps, s_rm, s_ra = sem("s_ps"), sem("s_rm"), sem("s_ra")
        s_rr, s_e, s_ex, s_mm = sem("s_rr"), sem("s_e"), sem("s_ex"), sem("s_mm")
        s_xb = [sem("s_xb0"), sem("s_xb1")]
        s_xnd, s_xob = sem("s_xnd"), sem("s_xob")
        s_yd, s_t1, s_t2, s_y = sem("s_yd"), sem("s_t1"), sem("s_t2"), sem("s_y")
        s_yt, s_yth, s_ytl, s_po, s_x1 = sem("s_yt"), sem("s_yth"), sem("s_ytl"), sem("s_po"), sem("s_x1")
        s_st2, s_mv2, s_var2, s_ln2, s_y02, s_nw2, s_xn2 = (sem("s_st2"), sem("s_mv2"), sem("s_var2"), sem("s_ln2"),
                                                           sem("s_y02"), sem("s_nw2"), sem("s_xn2"))
        s_x2d = [sem("s_x2d0"), sem("s_x2d1")]
        s_x2t, s_x2c, s_lg, s_lgt = sem("s_x2t"), sem("s_x2c"), sem("s_lg"), sem("s_lgt")
        s_out = [sem("s_out0"), sem("s_out1")]
        s_rc, s_iota, s_init = sem("s_rc"), sem("s_iota"), sem("s_init")
        s_plg, s_lgc, s_r, s_pex, s_cnt, s_msk = sem("s_plg"), sem("s_lgc"), sem("s_r"), sem("s_pex"), sem("s_cnt"), sem("s_msk")
        s_idx, s_tabw, s_tab, s_tok, s_routed = sem("s_idx"), sem("s_tabw"), sem("s_tab"), sem("s_tok"), sem("s_routed")
        s_ws, s_uh, s_ul = [sem("s_ws0"), sem("s_ws1")], sem("s_uh"), sem("s_ul")
        s_sx = [sem("s_sx0"), sem("s_sx1")]
        s_stx, s_stxh, s_stxl, s_sgu, s_ssi, s_sh = sem("s_stx"), sem("s_stxh"), sem("s_stxl"), sem("s_sgu"), sem("s_ssi"), sem("s_sh")
        s_sth, s_sthh, s_sthl, s_sdn, s_sacc = sem("s_sth"), sem("s_sthh"), sem("s_sthl"), sem("s_sdn"), sem("s_sacc")
        s_xg = [sem(f"s_xg{i}") for i in range(XG)]
        s_etx, s_etxh, s_etxl, s_egu, s_esi, s_eh = sem("s_etx"), sem("s_etxh"), sem("s_etxl"), sem("s_egu"), sem("s_esi"), sem("s_eh")
        s_eth, s_ethh, s_ethl, s_edn, s_ey = sem("s_eth"), sem("s_ethh"), sem("s_ethl"), sem("s_edn"), sem("s_ey")
        s_sc = [sem("s_sc0"), sem("s_sc1")]
        s_yl, s_fin, s_pad = [sem("s_yl0"), sem("s_yl1")], sem("s_fin"), sem("s_pad")

        def rconst(name):
            a, n = RCONSTS[name]
            return rcst[:, a:a + n]

        def up(w, slot, k):
            return w[:, slot, k * 2 * EI:(k + 1) * 2 * EI]

        def down(w, slot, k, rows=P):
            return w[0:rows, slot, WU + k * D:WU + (k + 1) * D]

        def tiles_in_turn(eng, n, unroll, step):
            rounds = (n - 1) // unroll
            with eng.Fori(0, rounds) as i:
                for j in range(1, unroll + 1):
                    step(i * unroll + j, i + j // unroll, j % unroll)
            for k in range(rounds * unroll + 1, n):
                step(k, k // unroll, k % unroll)

        def split3(out_ap, pairs):
            n = 3 * len(pairs)
            i = 0
            for (lh, ll), (rh, rl) in pairs:
                for a, b in ((lh, rl), (ll, rh), (lh, rh)):
                    last = nc.tensor.matmul(out_ap, a, b, start=(i == 0), stop=(i == n - 1))
                    i += 1
            return last

        MSTART = 14
        STEPS = MSTART + NT + 7

        def adds(u):
            return 1 + C * u - max(0, u - (PAIRS - 2))

        def wcol(w, name, k):
            a, n = WS[name]
            return w[:, k, a:a + n]

        def by_head(ap):
            return ap.rearrange("p (h e) -> p h e", e=HD)

        block = es.enter_context(nc.Block())

        @block.sync
        def _(sp):
            for g in range(GROUPS):
                sp.dma_start(res[:, g * BATCH:(g + 1) * BATCH, :], x_v[g]).then_inc(s_x[g], 16)
                if g == 0:
                    sp.dma_start(cst[:, :], cst_in).then_inc(s_c, 16)
            for step in range(-PAIRS, NT + 5):
                u = step + PAIRS
                if u < PAIRS:
                    sp.wait_ge(s_xdt, u + 1)
                    sp.dma_start(xdt_d[2 * u:2 * u + 2].rearrange("b p d -> p b d"),
                                 xdt[:, u % 2]).then_inc(s_xdtw[u % 2], 16)
                q = step
                if 0 <= q < NT:
                    u = q // 2
                    sp.wait_ge(s_xdtw[u % 2], 16 * (u // 2 + 1))
                    if q >= 2:
                        sp.wait_ge(s_yd, q - 1)
                    else:
                        sp.wait_ge(s_zero, 3)
                    for a in range(HQ):
                        src = xdt_d[q].rearrange("(c s) (a e) -> a s c e", c=C, a=HQ)[a]
                        sp.dma_start(xb[L * a:L * a + L, q % 2, :, a * N:(a + 1) * N], src).then_inc(s_xb[q % 2], 16)
                q = step - 5
                if 0 <= q < NT:
                    sp.wait_ge(s_xn2, q + 1)
                    sp.dma_start(xn2_d[q * P:(q + 1) * P, :], xn2[:, q % 2, :]).then_inc(s_x2d[q % 2], 16)
            for i in range(2):
                sp.wait_ge(s_x2d[i], 16 * NT // 2)
            sp.wait_ge(s_lgt, NT)
            sp.dma_start(rcst[:, :], rcst_in).then_inc(s_rc, 16)
            sp.wait_ge(s_iota, 2)
            sp.dma_start(table_d.rearrange("(p t) o -> p (t o)", t=XT), init[:, :]).then_inc(s_init, 16)

            def load_unit(u, n, par):
                sp.dma_start(stage_w[:, par, :], w_units[u]).then_inc(s_ws[par], 16)

            for u in range(4):
                if u >= 2:
                    sp.wait_ge(s_ul, u - 1)
                load_unit(u, u // 2, u % 2)

            def shared_rows(k, par):
                sp.dma_start(xg[:, par, :], xn2_d.rearrange("(q p) d -> q p d", p=P)[k]).then_inc(s_sx[par], 16)

            sp.wait_ge(s_lgc, 1)
            shared_rows(0, 0)
            shared_rows(1, 1)
            with sp.Fori(0, 6) as i:
                for j in range(2):
                    k = 2 * i + j + 2
                    sp.wait_ge(s_stx, k - 1)
                    shared_rows(k, j)
                    sp.wait_ge(s_ul, k + 1)
                    load_unit(k + 2, 0, j)
            for k in range(14, NT):
                sp.wait_ge(s_stx, k - 1)
                shared_rows(k, k % 2)
            sp.wait_ge(s_sdn, NT)
            for u in range(16, 20):
                sp.wait_ge(s_ul, u - 1)
                load_unit(u, 0, u % 2)


            for i in range(2):
                sp.wait_ge(s_sc[i], 16 * XT // 2)
            sp.wait_ge(s_ul, 20)
            y_v = y_d[0:ROWS, :].rearrange("(q p j) d -> q p (j d)", p=P, j=TOPK)
            for q in range(NT + 1):
                if q < NT:
                    if q >= 2:
                        sp.wait_ge(s_fin, q - 1)
                    sp.dma_start(yl[:, q % 2, :], y_v[q]).then_inc(s_yl[q % 2], 16)
                if q >= 1:
                    sp.wait_ge(s_fin, q)
                    sp.dma_start(out_v[(q - 1) // BATCH, (q - 1) % BATCH], res[:, q - 1, :]).then_inc(s_out[(q - 1) % 2], 16)
            for i in range(2):
                sp.wait_ge(s_out[i], 16 * NT // 2)
        @block.gpsimd
        def _(pool):
            nc.gpsimd.memset(ones_col[:, :], 1.0).then_inc(s_zero, 1)
            nc.gpsimd.memset(xb[:, 0], 0.0).then_inc(s_zero, 1)
            nc.gpsimd.memset(xb[:, 1], 0.0).then_inc(s_zero, 1)
            nc.gpsimd.memset(bm[:, :, :, :, :], 0.0).then_inc(s_bm, 1)
            pool.wait_ge(s_c, 16)
            nc.gpsimd.tensor_copy(after_r[:, :], const("after")).then_inc(s_aft, 1)
            pool.wait_ge(s_small, 64)

            def with_bias(u):
                pool.wait_ge(s_xn, 2 * (u + 1))
                nc.gpsimd.tensor_tensor(res[:, 2 * u:2 * u + 2], res[:, 2 * u:2 * u + 2],
                                        ob_sb[:, :].unsqueeze(1).to_broadcast([P, 2, D]), ALU.add).then_inc(s_xob, 1)

            def inputs(u):
                if u >= 2:
                    pool.wait_ge(s_xdtw[u % 2], 16 * (u // 2))
                pool.wait_ge(s_dt, u + 1)
                for j in range(2):
                    i = nc.gpsimd.tensor_tensor(by_head(xdt[:, u % 2, j]), by_head(xn[:, 2 * u + j]),
                                                dt[:, u % 2, j].unsqueeze(2).to_broadcast([P, H, HD]), ALU.mult)
                i.then_inc(s_xdt, 1)
                if u >= 2:
                    pool.wait_ge(s_ps, u - 1)
                pool.wait_ge(s_xdt, u + 1)
                pool.wait_ge(s_dec, 3 * u + 1)
                for j in range(2):
                    i = nc.gpsimd.tensor_tensor(by_head(xd[:, u % 2, j]), by_head(xdt[:, u % 2, j]),
                                                dec[:, u % 2, j].unsqueeze(2).to_broadcast([P, H, HD]), ALU.mult)
                i.then_inc(s_xd, 1)
                pool.wait_ge(s_daq, 16 * (u + 1))
                dq = slice(2 * u, 2 * u + 2)
                nc.gpsimd.tensor_copy(daq_hi[:, dq], daq[:, u % 2]).then_inc(s_dqh, 1)
                pool.wait_ge(s_dqh, u + 1)
                nc.gpsimd.tensor_tensor(daq_lo[:, dq], daq[:, u % 2], daq_hi[:, dq], ALU.subtract).then_inc(s_dql, 1)
                for j in range(2):
                    i = nc.gpsimd.tensor_tensor(by_head(xn[:, 2 * u + j]), by_head(xn[:, 2 * u + j]),
                                                d_sb[:, :].unsqueeze(2).to_broadcast([P, H, HD]), ALU.mult)
                i.then_inc(s_xnd, 1)

            def increments(q):
                if q >= 2:
                    pool.wait_ge(s_e, q - 1)
                pool.wait_ge(s_dql, q // 2 + 1)
                for part, of in ((rr_hi, daq_hi), (rr_lo, daq_lo)):
                    last = nc.gpsimd.tensor_tensor(
                        part[:, q % 2], of[:, q].rearrange("p c a -> p (c a)").unsqueeze(2).to_broadcast([P, C * HG, L]),
                        const("tri").unsqueeze(1).to_broadcast([P, C * HG, L]), ALU.mult)
                last.then_inc(s_rr, 1)

            for step in range(STEPS):
                for u, stage in ((step - 8, inputs), (step - 2, with_bias)):
                    if 0 <= u < PAIRS:
                        stage(u)
                if 0 <= step - MSTART < NT:
                    increments(step - MSTART)
            pool.wait_ge(s_lgt, NT)
            nc.gpsimd.iota(pair[:, :], [[TOPK * P, NT], [1, TOPK]], base=0, channel_multiplier=TOPK).then_inc(s_iota, 1)
            nc.gpsimd.iota(init[:, :], [[1, XT]], base=ROWS, channel_multiplier=XT).then_inc(s_iota, 1)
            pool.wait_ge(s_iota, 2)
            pool.wait_ge(s_init, 16)
            pool.wait_ge(s_idx, 1)
            for i in range(NT * TOPK):
                pool.indirect_dma_start(out=table_d, out_offset=bass.IndirectOffsetOnAxis(ap=slot_i[:, i:i + 1], axis=0),
                                        in_=pair[:, i:i + 1], in_offset=None).then_inc(s_tabw, 16)

            def gather(k):
                if k >= XG:
                    pool.wait_ge(s_etx, k - XG + 1)
                pool.indirect_dma_start(out=xg[:, k % XG, :], out_offset=None, in_=xn2_d,
                                        in_offset=bass.IndirectOffsetOnAxis(ap=tok[:, k:k + 1], axis=0)).then_inc(s_xg[k % XG], 16)

            pool.wait_ge(s_tok, 1)
            pool.wait_ge(s_stx, NT)
            for k in range(XG):
                gather(k)
            for k in range(XT):
                if k + XG < XT:
                    gather(k + XG)
                pool.wait_ge(s_ey, k + 1)
                pool.indirect_dma_start(out=y_d, out_offset=bass.IndirectOffsetOnAxis(ap=tab[:, k:k + 1], axis=0),
                                        in_=y_sb[:, k % 2, :], in_offset=None).then_inc(s_sc[k % 2], 16)

        @block.scalar
        def _(act):
            nc.scalar.preload_act_table_set("natural_log_exp_and_others")
            act.dma_start(w_raw[:, :, :], w_small).then_inc(s_w, 16)
            act.dma_start(bias[:, :], w_bias).then_inc(s_small, 16)
            act.dma_start(a_sb[:, :], a_log.to_broadcast([P, H])).then_inc(s_small, 16)
            act.dma_start(d_sb[:, :], d_row.to_broadcast([P, H])).then_inc(s_small, 16)
            act.dma_start(ob_sb[:, :], ob_row.to_broadcast([P, D])).then_inc(s_small, 16)
            act.wait_ge(s_w, 16)
            nc.scalar.copy(w_hi[:, :, :], w_raw[:, :, :]).then_inc(s_whi, 1)
            act.wait_ge(s_small, 64)
            nc.scalar.activation(a_sb[:, :], a_sb[:, :], ACT.Exp).then_inc(s_ea, 1)
            act.wait_ge(s_zero, 1)

            def rstd_guess(u):
                act.wait_ge(s_var, u + 1)
                nc.scalar.activation(lnv[:, u % 2], var[:, u % 2], ACT.Ln).then_inc(s_ln, 1)
                act.wait_ge(s_ln, u + 1)
                nc.scalar.activation(y0[:, u % 2], lnv[:, u % 2], ACT.Exp, scale=-0.5).then_inc(s_y0, 1)

            def high_parts(u):
                act.wait_ge(s_xt, u + 1)
                if u >= 2:
                    act.wait_ge(s_pcc, u - 1)
                nc.scalar.copy(xt_hi[:, u % 2].rearrange("p k t -> p (k t)"), bank[0][:, :]).then_inc(s_xth, 1)

            def projected(u):
                act.wait_ge(s_pcc, u + 1)
                if u >= 2:
                    act.wait_ge(s_pg, u - 1)
                nc.scalar.activation(bdf[:, u % 2], bank[1][0:N + H, 0:2 * P], ACT.Identity,
                                     bias=bias[0:N + H, 0:1]).then_inc(s_bdf, 1)
                nc.scalar.activation(ct[:, 2 * u:2 * u + 2, :].rearrange("p b t -> p (b t)"), bank[1][:, 2 * P:4 * P],
                                     ACT.Identity, bias=bias[:, 1:2]).then_inc(s_ct, 1)

            def token_major(u):
                act.wait_ge(s_pg, u + 1)
                if u >= 4:
                    act.wait_ge(s_bm, u - 2)
                    act.wait_ge(s_dt, u - 3)
                nc.scalar.copy(bz[:, u % 4].rearrange("p b j -> p (b j)"), bank[2][:, 0:2 * (N + H)]).then_inc(s_bz, 1)

            def softplus(u):
                act.wait_ge(s_na, u + 1)
                nc.scalar.activation(sp_e[:, :, :], na[:, :, :], ACT.Exp).then_inc(s_spe, 1)
                act.wait_ge(s_spe, u + 1)
                if u:
                    act.wait_ge(s_dt, u)
                nc.scalar.activation(sp_l[:, :, :], sp_e[:, :, :], ACT.Ln, bias=ones_col[:, 0:1]).then_inc(s_spl, 1)

            def blocks(u):
                if u >= 2:
                    act.wait_ge(s_ps, u - 1)
                act.wait_ge(s_bm, u + 1)
                for c in range(C):
                    i = nc.scalar.copy(bm[L * c:L * c + L, u % 2, :, c, :], bz[L * c:L * c + L, u % 4, :, 0:N])
                i.then_inc(s_bm, 1)

            def by_quarter(u):
                act.wait_ge(s_da, u + 1)
                if u >= 2:
                    act.wait_ge(s_dql, u - 1)
                for a in range(HQ):
                    for c in range(C):
                        nc.scalar.copy(daq[L * a:L * a + L, u % 2, :, c, :],
                                       da[L * c:L * c + L, u % 2, :, a * HG:(a + 1) * HG]).then_inc(s_daq, 1)

            def decays(u):
                act.wait_ge(s_pd, u + 1)
                if u >= 2:
                    act.wait_ge(s_xd, u - 1)
                if u >= 4:
                    act.wait_ge(s_ra, adds(u - 3))
                nc.scalar.activation(dec[:, u % 2].rearrange("p b h -> p (b h)"), bank[3][:, 0:2 * H], ACT.Exp).then_inc(s_dec, 1)
                nc.scalar.activation(ecs[:, 2 * u:2 * u + 2, :].rearrange("p b h -> p (b h)"),
                                     bank[3][:, 2 * H:4 * H], ACT.Exp).then_inc(s_dec, 1)
                nc.scalar.activation(dch[:, u % 4].rearrange("p c h -> p (c h)"), bank[3][:, 4 * H:4 * H + C * H],
                                     ACT.Exp).then_inc(s_dec, 1)
                nc.scalar.copy(gp[:, 2 * u:2 * u + 2, :].rearrange("p b t -> p (b t)"), bank[3][:, 2 * P:4 * P]).then_inc(s_gp, 1)

            def expo(q):
                act.wait_ge(s_e, q + 1)
                if q >= 2:
                    act.wait_ge(s_mm, q - 1)
                for i in range(2):
                    nc.scalar.activation(ex[:, q % 2, 16 * i:16 * i + 16, :].rearrange("p a l -> p (a l)"),
                                         bank[i][:, :], ACT.Exp).then_inc(s_ex, 1)

            def y_high(q):
                act.wait_ge(s_yt, q + 1)
                if q >= 2:
                    act.wait_ge(s_po, q - 1)
                nc.scalar.copy(yt_hi[:, q % 2], bank[4][:, 0:D]).then_inc(s_yth, 1)

            def rstd2(q):
                act.wait_ge(s_var2, q + 1)
                nc.scalar.activation(lnvb[:, :], varb[:, :], ACT.Ln).then_inc(s_ln2, 1)
                act.wait_ge(s_ln2, q + 1)
                nc.scalar.activation(y0b[:, :], lnvb[:, :], ACT.Exp, scale=-0.5).then_inc(s_y02, 1)

            def x2_copy(q):
                act.wait_ge(s_x2t, q + 1)
                if q:
                    act.wait_ge(s_lg, q)
                nc.scalar.copy(x2t[:, :], bank[6][:, 0:D]).then_inc(s_x2c, 1)

            def logits_copy(q):
                act.wait_ge(s_lg, q + 1)
                nc.scalar.copy(lgt[0:32, q, :], bank[7][0:32, 0:P]).then_inc(s_lgt, 1)

            for step in range(STEPS):
                for k, stage in ((1, rstd_guess), (2, high_parts), (4, projected), (5, token_major), (6, softplus),
                                 (7, decays), (7, by_quarter), (8, blocks)):
                    if 0 <= step - k < PAIRS:
                        stage(step - k)
                for k, stage in ((5, rstd2), (0, expo), (3, y_high), (6, logits_copy), (5, x2_copy)):
                    if 0 <= step - MSTART - k < NT:
                        stage(step - MSTART - k)

            act.wait_ge(s_plg, 1)
            nc.scalar.copy(lg[:, :, :].rearrange("p q e -> p (q e)"), bank[0][:, :]).then_inc(s_lgc, 1)
            act.wait_ge(s_lgc, 1)
            nc.scalar.activation(sgx[:, :], lg[:, :, E], ACT.Exp, scale=-1.0).then_inc(s_pex, 1)
            act.wait_ge(s_r, 2)
            nc.scalar.activation(pe_[:, :, :].rearrange("p q e -> p (q e)"), shl[:, :, :].rearrange("p q e -> p (q e)"),
                                 ACT.Exp).then_inc(s_pex, 1)

            def split_high(u, slot, par, uses):
                act.wait_ge(s_ws[par], 16 * uses)
                nc.scalar.copy(wu_hi[:, slot, :], stage_w[:, par, :]).then_inc(s_uh, 1)

            for u in range(4):
                split_high(u, SH + u, u % 2, u // 2 + 1)

            def s_thigh(k):
                act.wait_ge(s_sth, k + 1)
                if not isinstance(k, int) or k >= 1:
                    act.wait_ge(s_sdn, k)
                nc.scalar.copy(th_hi[:, 0:4, :].rearrange("p c t -> p (c t)"), bank[5][:, :]).then_inc(s_sthh, 1)
                nc.scalar.copy(th_hi[:, 4:6, :].rearrange("p c t -> p (c t)"), bank[6][:, 0:2 * P]).then_inc(s_sthh, 1)

            def s_silu(k):
                for c in range(2):
                    act.wait_ge(s_sgu, 4 * k + c + 1)
                    if not isinstance(k, int) or k >= 1:
                        act.wait_ge(s_sh, 2 * k + c - 1)
                    nc.scalar.activation(act_s[:, c * 352:(c + 1) * 352], bank[1 + c][:, 0:352], ACT.Silu).then_inc(s_ssi, 1)

            def s_xhigh(k):
                act.wait_ge(s_stx, k + 1)
                if not isinstance(k, int) or k >= 1:
                    act.wait_ge(s_sgu, 4 * k)
                nc.scalar.copy(tx_hi[:, :], bank[0][:, 0:D]).then_inc(s_stxh, 1)

            s_xhigh(0)
            s_silu(0)
            s_xhigh(1)
            with act.Fori(0, 6) as i:
                for j in range(2):
                    k = 2 * i + j + 1
                    s_thigh(k - 1)
                    s_silu(k)
                    s_xhigh(k + 1)
                    split_high(0, k - 1, j, i + 3)
            for k in range(13, NT):
                s_thigh(k - 1)
                s_silu(k)
                if k + 1 < NT:
                    s_xhigh(k + 1)
            s_thigh(NT - 1)
            act.wait_ge(s_tabw, 16 * NT * TOPK)
            act.dma_start(tab[:, :], table_d.rearrange("(p t) o -> p (t o)", t=XT)).then_inc(s_tab, 16)
            for u in range(16, 20):
                split_high(u, u - 4, u % 2, u // 2 + 1)

            def e_thigh(k):
                act.wait_ge(s_eth, k + 1)
                if not isinstance(k, int) or k >= 1:
                    act.wait_ge(s_edn, k)
                nc.scalar.copy(th_hi[0:EK, 0:2, :].rearrange("p c t -> p (c t)"), bank[5][0:EK, 0:2 * P]).then_inc(s_ethh, 1)

            def e_silu(k, par):
                act.wait_ge(s_egu, k + 1)
                if not isinstance(k, int) or k >= 1:
                    act.wait_ge(s_eh, k)
                nc.scalar.activation(act_s[:, 0:EI], bank[1 + par][:, 0:EI], ACT.Silu).then_inc(s_esi, 1)

            def e_xhigh(k):
                act.wait_ge(s_etx, k + 1)
                if not isinstance(k, int) or k >= 1:
                    act.wait_ge(s_egu, k)
                nc.scalar.copy(tx_hi[:, :], bank[0][:, 0:D]).then_inc(s_etxh, 1)

            def e_result(k, par, uses):
                act.wait_ge(s_edn, k + 1)
                if not isinstance(uses, int) or uses >= 1:
                    act.wait_ge(s_sc[par], 16 * uses)
                nc.scalar.copy(y_sb[:, par, :], bank[7][:, 0:D]).then_inc(s_ey, 1)

            act.wait_ge(s_sthl, 2 * NT)
            e_xhigh(0)
            e_silu(0, 0)
            e_xhigh(1)

            def e_step(k, n, j):
                e_thigh(k - 1)
                e_silu(k, j % 2)
                if not isinstance(k, int) or k + 1 < XT:
                    e_xhigh(k + 1)
                e_result(k - 1, (j - 1) % 2, (n * XG + j - 1) // 2 if isinstance(n, int) else n * (XG // 2) + (j - 1) // 2)

            for k in range(1, 1 + XG):
                e_step(k, k // XG, k % XG)
            with act.Fori(1, (XT - 1) // XG) as i:
                for j in range(1, XG + 1):
                    e_step(i * XG + j, i + j // XG, j % XG)
            for k in range((XT - 1) // XG * XG + 1, XT):
                e_step(k, k // XG, k % XG)
            e_thigh(XT - 1)
            e_result(XT - 1, (XT - 1) % 2, (XT - 1) // 2)

        @block.vector
        def _(dve):
            dve.wait_ge(s_whi, 1)
            nc.vector.tensor_tensor(w_lo[:, :, :], w_raw[:, :, :], w_hi[:, :, :], ALU.subtract).then_inc(s_wlo, 1)
            nc.vector.memset(state[:, 0, :, 0, :], 0.0).then_inc(s_ra, 1)
            nw = [0]

            def newton(v, y, a, b, r, s):
                ops = (lambda: nc.vector.tensor_tensor(a, y, y, ALU.mult),
                       lambda: nc.vector.tensor_tensor(b, a, v, ALU.mult),
                       lambda: nc.vector.tensor_scalar(a, b, -0.5, 1.5, ALU.mult, ALU.add),
                       lambda: nc.vector.tensor_tensor(r, a, y, ALU.mult))
                for op in ops:
                    op().then_inc(s_nw, 1)
                    nw[0] += 1
                    dve.wait_ge(s_nw, nw[0])

            def stats(u):
                if u % 2 == 0:
                    dve.wait_ge(s_x[u // 2], 16)
                for j in range(2):
                    nc.vector.bn_stats(stat6[:, u % 2, j], res[:, 2 * u + j]).then_inc(s_st, 1)
                for j in range(2):
                    dve.wait_ge(s_st, 2 * u + j + 1)
                    nc.vector.bn_aggr(mv[:, u % 2, j], stat6[:, u % 2, j]).then_inc(s_mv, 1)
                dve.wait_ge(s_mv, 2 * (u + 1))
                nc.vector.tensor_scalar(var[:, u % 2], mv[:, u % 2, :, 1], EPS, None, ALU.add).then_inc(s_var, 1)

            def normalise(u):
                dve.wait_ge(s_y0, u + 1)
                newton(var[:, u % 2], y0[:, u % 2], ya[:, :], yb[:, :], rs[:, :], s_nw)
                for j in range(2):
                    nc.vector.tensor_scalar(xn[:, 2 * u + j], res[:, 2 * u + j], mv[:, u % 2, j, 0:1],
                                            rs[:, j:j + 1], ALU.subtract, ALU.mult).then_inc(s_xn, 1)

            def low_parts(u):
                dve.wait_ge(s_xth, u + 1)
                if u >= 2:
                    dve.wait_ge(s_pcc, u - 1)
                nc.vector.tensor_tensor(xt_lo[:, u % 2].rearrange("p k t -> p (k t)"), bank[0][:, :],
                                        xt_hi[:, u % 2].rearrange("p k t -> p (k t)"), ALU.subtract).then_inc(s_xtl, 1)

            def masks(u):
                dve.wait_ge(s_bz, u + 1)
                if u >= 2:
                    dve.wait_ge(s_pgp, u - 1)
                nc.vector.tensor_tensor(gmd[:, u % 2].rearrange("p (b t) -> p b t", b=2),
                                        bank[2][:, 2 * P:4 * P].rearrange("p (b t) -> p b t", b=2),
                                        const("upto").unsqueeze(1).to_broadcast([P, 2, P]), ALU.mult).then_inc(s_gmd, 1)
                z = bz[:, u % 4, :, N:N + H]
                nc.vector.scalar_tensor_tensor(out=na[:, :, :], in0=z, scalar=-1.0, in1=z, op0=ALU.mult,
                                               op1=ALU.min).then_inc(s_na, 1)

            def steps(u):
                dve.wait_ge(s_spl, u + 1)
                if u >= 2:
                    dve.wait_ge(s_xdt, u - 1)
                nc.vector.scalar_tensor_tensor(out=dt[:, u % 2], in0=bz[:, u % 4, :, N:N + H], scalar=0.0, in1=sp_l[:, :, :],
                                               op0=ALU.max, op1=ALU.add).then_inc(s_dt, 1)
                dve.wait_ge(s_dt, u + 1)
                dve.wait_ge(s_ea, 1)
                if u >= 2:
                    dve.wait_ge(s_pd, u - 1)
                    dve.wait_ge(s_daq, 16 * (u - 1))
                nc.vector.scalar_tensor_tensor(out=da[:, u % 2], in0=dt[:, u % 2], scalar=-1.0,
                                               in1=a_sb[:, :].unsqueeze(1).to_broadcast([P, 2, H]),
                                               op0=ALU.mult, op1=ALU.mult).then_inc(s_da, 1)

            def recur(u):
                g, i = u // 2, u % 2
                dve.wait_ge(s_ps, u + 1)
                dve.wait_ge(s_dec, 3 * u + 3)
                for c in range(C):
                    if (g, c) == (GROUPS - 1, C - 1):
                        continue
                    dve.wait_ge(s_ra, adds(u) + c)
                    nc.vector.tensor_tensor(by_head(tmp_s[:, :]), by_head(state[:, g, i, c]),
                                            dch[:, u % 4, c].unsqueeze(2).to_broadcast([P, H, HD]), ALU.mult).then_inc(s_rm, 1)
                    dve.wait_ge(s_rm, adds(u) + c)
                    nxt = (g, c + 1) if c + 1 < C else (g + 1, 0)
                    nc.vector.tensor_tensor(state[:, nxt[0], i, nxt[1]], tmp_s[:, :],
                                            bank[4 + 2 * i + c // 2][:, D * (c % 2):D * (c % 2) + D],
                                            ALU.add).then_inc(s_ra, 1)

            def weigh(q):
                dve.wait_ge(s_ex, 2 * (q + 1))
                if q >= 2:
                    dve.wait_ge(s_yd, q - 1)
                dve.wait_ge(s_gp, q // 2 + 1)
                g4 = gp[:, q].rearrange("p (c l) -> p c l", c=C)
                for c in range(C):
                    i = nc.vector.tensor_tensor(mm[:, q % 2, c * HG:(c + 1) * HG, :], ex[:, q % 2, c * HG:(c + 1) * HG, :],
                                                g4[:, c].unsqueeze(1).to_broadcast([P, HG, L]), ALU.mult)
                i.then_inc(s_mm, 1)

            def combine(q):
                pb = bank[2 + q % 2]
                dve.wait_ge(s_yd, q + 1)
                nc.vector.tensor_tensor(by_head(t1[:, :]), by_head(pb[:, D:2 * D]),
                                        ecs[:, q].unsqueeze(2).to_broadcast([P, H, HD]), ALU.mult).then_inc(s_t1, 1)
                dve.wait_ge(s_t1, q + 1)
                dve.wait_ge(s_xnd, q // 2 + 1)
                nc.vector.tensor_tensor(t2[:, :], t1[:, :], xn[:, q], ALU.add).then_inc(s_t2, 1)
                dve.wait_ge(s_t2, q + 1)
                if q >= 2:
                    dve.wait_ge(s_yt, q - 1)
                nc.vector.tensor_tensor(yy[:, q % 2], t2[:, :], pb[:, 0:D], ALU.add).then_inc(s_y, 1)

            def y_low(q):
                dve.wait_ge(s_yth, q + 1)
                if q >= 2:
                    dve.wait_ge(s_po, q - 1)
                nc.vector.tensor_tensor(yt_lo[:, q % 2], bank[4][:, 0:D], yt_hi[:, q % 2], ALU.subtract).then_inc(s_ytl, 1)

            def residual(q):
                dve.wait_ge(s_po, q + 1)
                dve.wait_ge(s_xob, q // 2 + 1)
                nc.vector.tensor_tensor(res[:, q], bank[5][:, 0:D], res[:, q], ALU.add).then_inc(s_x1, 1)
                dve.wait_ge(s_x1, q + 1)
                nc.vector.bn_stats(stat6b[:, :], res[:, q]).then_inc(s_st2, 1)
                dve.wait_ge(s_st2, q + 1)
                nc.vector.bn_aggr(mvb[:, :], stat6b[:, :]).then_inc(s_mv2, 1)
                dve.wait_ge(s_mv2, q + 1)
                nc.vector.tensor_scalar(varb[:, :], mvb[:, 1:2], EPS, None, ALU.add).then_inc(s_var2, 1)

            def normalise2(q):
                dve.wait_ge(s_y02, q + 1)
                newton(varb[:, :], y0b[:, :], yab[:, :], ybb[:, :], rsb[:, :], s_nw)
                if q >= 2:
                    dve.wait_ge(s_x2d[q % 2], 16 * (q // 2))
                    dve.wait_ge(s_x2t, q - 1)
                nc.vector.tensor_scalar(xn2[:, q % 2], res[:, q], mvb[:, 0:1], rsb[:, 0:1], ALU.subtract,
                                        ALU.mult).then_inc(s_xn2, 1)

            for step in range(STEPS):
                for k, stage in ((3, low_parts), (7, steps), (6, masks), (10, recur), (1, normalise), (0, stats)):
                    if 0 <= step - k < PAIRS:
                        stage(step - k)
                for k, stage in ((5, residual), (1, weigh), (5, normalise2), (2, combine), (3, y_low)):
                    if 0 <= step - MSTART - k < NT:
                        stage(step - MSTART - k)

            nr = [0]

            def r_(ins):
                ins.then_inc(s_r, 1)
                nr[0] += 1
                dve.wait_ge(s_r, nr[0])

            def wide(ap, n):
                return ap.unsqueeze(2).to_broadcast([P, ap.shape[1], n])

            dve.wait_ge(s_lgc, 1)
            r_(nc.vector.tensor_reduce(mx[:, :], lg[:, :, 0:E], AX.X, ALU.max))
            r_(nc.vector.tensor_tensor(shl[:, :, :], lg[:, :, 0:E], wide(mx[:, :], E), ALU.subtract))
            dve.wait_ge(s_pex, 2)
            r_(nc.vector.tensor_scalar(sgy[:, :], sgx[:, :], 1.0, None, ALU.add))
            r_(nc.vector.reciprocal(sig[:, :], sgy[:, :]))
            r_(nc.vector.tensor_reduce(sm[:, :], pe_[:, :, :], AX.X, ALU.add))
            r_(nc.vector.reciprocal(rc[:, :], sm[:, :]))
            r_(nc.vector.tensor_tensor(prob[:, :, :], pe_[:, :, :], wide(rc[:, :], E), ALU.mult))
            for q in range(NT):
                last = nc.vector.max(m8[:, q, :], prob[:, q, :])
            r_(last)
            for q in range(NT):
                last = nc.vector.max_index(i8[:, q, :], m8[:, q, :], prob[:, q, :])
            r_(last)
            r_(nc.vector.tensor_reduce(sw[:, :], m8[:, :, 0:TOPK], AX.X, ALU.add))
            r_(nc.vector.reciprocal(rw[:, :], sw[:, :]))
            r_(nc.vector.tensor_tensor(wgt[:, :, :], m8[:, :, 0:TOPK], wide(rw[:, :], TOPK), ALU.mult))
            r_(nc.vector.tensor_copy(idf[:, :, :], i8[:, :, 0:TOPK]))
            dve.wait_ge(s_rc, 16)
            r_(nc.vector.tensor_tensor(oh[:, :, :, :].rearrange("p q j e -> p (q j) e"),
                                       wide(idf[:, :, :].rearrange("p q j -> p (q j)"), E),
                                       rconst("iota_e").unsqueeze(1).to_broadcast([P, NT * TOPK, E]), ALU.is_equal))
            nc.vector.tensor_reduce(msk[:, :, :].rearrange("p e q -> p q e"), oh[:, :, :, :].rearrange("p q j e -> p q e j"),
                                    AX.X, ALU.add).then_inc(s_msk, 1)
            dve.wait_ge(s_cnt, 1)
            rank, tot = bank[1][:, 0:E * NT], bank[1][:, E * NT:2 * E * NT]
            flat = lambda t: t[:, :, :].rearrange("p e q -> p (e q)")
            r_(nc.vector.tensor_tensor_scan(flat(inc), rconst("keep"), tot, 0.0, ALU.mult, ALU.add))
            r_(nc.vector.tensor_tensor(flat(exc), flat(inc), tot, ALU.subtract))
            r_(nc.vector.tensor_tensor(gt[:, :, :], inc[:, :, NT - 1].unsqueeze(2).to_broadcast([P, E, NT]),
                                       rconst("edges").unsqueeze(1).to_broadcast([P, E, NT]), ALU.is_gt))
            r_(nc.vector.tensor_reduce(tl[:, :], gt[:, :, :], AX.X, ALU.add))
            r_(nc.vector.tensor_tensor_scan(incl[:, :], rconst("ones")[:, 0:E], tl[:, :], 0.0, ALU.mult, ALU.add))
            r_(nc.vector.tensor_tensor(base[:, :], incl[:, :], tl[:, :], ALU.subtract))
            r_(nc.vector.tensor_tensor(flat(sl), flat(exc), rank, ALU.add))
            r_(nc.vector.scalar_tensor_tensor(out=sl2[:, :, :], in0=wide(base[:, :], NT), scalar=float(P), in1=sl[:, :, :],
                                              op0=ALU.mult, op1=ALU.add))
            r_(nc.vector.tensor_tensor(so[:, :, :, :], oh[:, :, :, :],
                                       sl2[:, :, :].rearrange("p e q -> p q e").unsqueeze(2).to_broadcast([P, NT, TOPK, E]), ALU.mult))
            r_(nc.vector.tensor_reduce(slf[:, :], so[:, :, :, :].rearrange("p q j e -> p (q j) e"), AX.X, ALU.add))
            r_(nc.vector.tensor_copy(si[:, :], slf[:, :]))
            r_(nc.vector.tensor_scalar(s_hi7[:, :], si[:, :], 7, None, ALU.logical_shift_right))
            r_(nc.vector.tensor_scalar(s_lo7[:, :], si[:, :], P - 1, None, ALU.bitwise_and))
            nc.vector.scalar_tensor_tensor(out=slot_i[:, :], in0=s_lo7[:, :], scalar=float(XT), in1=s_hi7[:, :],
                                           op0=ALU.mult, op1=ALU.add).then_inc(s_idx, 1)
            nx = XT + XG
            r_(nc.vector.tensor_tensor(le[:, :, :], incl[0:1, :].unsqueeze(1).to_broadcast([1, nx, E]),
                                       rconst("tiles")[0:1, :].unsqueeze(2).to_broadcast([1, nx, E]), ALU.is_le))
            r_(nc.vector.tensor_reduce(ef[:, :], le[:, :, :], AX.X, ALU.add))
            r_(nc.vector.tensor_scalar(em[:, :], ef[:, :], float(E - 1), None, ALU.min))
            e4 = em[:, :].rearrange("o (i j) -> o i j", j=XG)
            np_ = XT // XG
            r_(nc.vector.tensor_copy(ep[:, 0, :], e4[:, 0:np_, 0]))
            for j in range(1, XG + 1):
                dst = ep[:, j % 2, :] if j < XG else epack[:, :]
                src = e4[:, 0:np_, j] if j < XG else e4[:, 1:np_ + 1, 0]
                ins = nc.vector.scalar_tensor_tensor(out=dst, in0=src, scalar=float(E ** j), in1=ep[:, (j - 1) % 2, :],
                                                     op0=ALU.mult, op1=ALU.add)
                if j < XG:
                    r_(ins)
            ins.then_inc(s_routed, 1)
            dve.wait_ge(s_routed, 1)
            dve.wait_ge(s_idx, 1)

            def split_low(slot, n):
                dve.wait_ge(s_uh, n)
                nc.vector.tensor_tensor(wu_lo[:, slot, :], stage_w[:, n_par[0], :], wu_hi[:, slot, :], ALU.subtract).then_inc(s_ul, 1)

            n_par = [0]
            for u in range(4):
                n_par[0] = u % 2
                split_low(SH + u, u + 1)
            nc.vector.memset(act_h[:, SI:6 * P], 0.0).then_inc(s_pad, 1)

            def s_tlow(k):
                dve.wait_ge(s_sthh, 2 * k + 2)
                if not isinstance(k, int) or k >= 1:
                    dve.wait_ge(s_sdn, k)
                nc.vector.tensor_tensor(th_lo[:, 0:4, :].rearrange("p c t -> p (c t)"), bank[5][:, :],
                                        th_hi[:, 0:4, :].rearrange("p c t -> p (c t)"), ALU.subtract).then_inc(s_sthl, 1)
                nc.vector.tensor_tensor(th_lo[:, 4:6, :].rearrange("p c t -> p (c t)"), bank[6][:, 0:2 * P],
                                        th_hi[:, 4:6, :].rearrange("p c t -> p (c t)"), ALU.subtract).then_inc(s_sthl, 1)

            def s_gated(k):
                for c in range(2):
                    dve.wait_ge(s_ssi, 2 * k + c + 1)
                    dve.wait_ge(s_sgu, 4 * k + c + 3)
                    if not isinstance(k, int) or k >= 1:
                        dve.wait_ge(s_sth, k)
                    nc.vector.tensor_tensor(act_h[:, c * 352:(c + 1) * 352], act_s[:, c * 352:(c + 1) * 352],
                                            bank[3 + c][:, 0:352], ALU.mult).then_inc(s_sh, 1)

            def s_xlow(k):
                dve.wait_ge(s_stxh, k + 1)
                if not isinstance(k, int) or k >= 1:
                    dve.wait_ge(s_sgu, 4 * k)
                nc.vector.tensor_tensor(tx_lo[:, :], bank[0][:, 0:D], tx_hi[:, :], ALU.subtract).then_inc(s_stxl, 1)

            def s_add(k):
                dve.wait_ge(s_sdn, k + 1)
                nc.vector.scalar_tensor_tensor(out=res[:, k, :], in0=bank[7][:, 0:D], scalar=sig[:, bass.ds(k, 1)],
                                               in1=res[:, k, :], op0=ALU.mult, op1=ALU.add).then_inc(s_sacc, 1)

            s_xlow(0)
            s_gated(0)
            s_xlow(1)
            with dve.Fori(0, 6) as i:
                for j in range(2):
                    k = 2 * i + j + 1
                    s_tlow(k - 1)
                    s_gated(k)
                    s_xlow(k + 1)
                    s_add(k - 1)
                    n_par[0] = j
                    split_low(k - 1, k + 4)
            for k in range(13, NT):
                s_tlow(k - 1)
                s_gated(k)
                if k + 1 < NT:
                    s_xlow(k + 1)
                s_add(k - 1)
            s_tlow(NT - 1)
            s_add(NT - 1)
            for u in range(16, 20):
                n_par[0] = u % 2
                split_low(u - 4, u + 1)
            dve.wait_ge(s_tab, 16)
            nc.vector.tensor_scalar(tok[:, :], tab[:, :], 2, T - 1, ALU.logical_shift_right, ALU.bitwise_and).then_inc(s_tok, 1)

            def e_tlow(k):
                dve.wait_ge(s_ethh, k + 1)
                if not isinstance(k, int) or k >= 1:
                    dve.wait_ge(s_edn, k)
                nc.vector.tensor_tensor(th_lo[0:EK, 0:2, :].rearrange("p c t -> p (c t)"), bank[5][0:EK, 0:2 * P],
                                        th_hi[0:EK, 0:2, :].rearrange("p c t -> p (c t)"), ALU.subtract).then_inc(s_ethl, 1)

            def e_gated(k, par):
                dve.wait_ge(s_esi, k + 1)
                if not isinstance(k, int) or k >= 1:
                    dve.wait_ge(s_eth, k)
                nc.vector.tensor_tensor(act_h[:, 0:EI], act_s[:, 0:EI], bank[1 + par][:, EI:2 * EI], ALU.mult).then_inc(s_eh, 1)

            def e_xlow(k):
                dve.wait_ge(s_etxh, k + 1)
                if not isinstance(k, int) or k >= 1:
                    dve.wait_ge(s_egu, k)
                nc.vector.tensor_tensor(tx_lo[:, :], bank[0][:, 0:D], tx_hi[:, :], ALU.subtract).then_inc(s_etxl, 1)

            e_xlow(0)
            e_gated(0, 0)
            e_xlow(1)

            def e_step(k, n, j):
                e_tlow(k - 1)
                e_gated(k, j % 2)
                if not isinstance(k, int) or k + 1 < XT:
                    e_xlow(k + 1)

            tiles_in_turn(dve, XT, XG, e_step)
            e_tlow(XT - 1)

            dve.wait_ge(s_sacc, NT)
            for q in range(NT):
                dve.wait_ge(s_yl[q % 2], 16 * (q // 2 + 1))
                for j in range(TOPK):
                    last = nc.vector.scalar_tensor_tensor(out=res[:, q, :], in0=yl[:, q % 2, j * D:(j + 1) * D],
                                                          scalar=wgt[:, q, j:j + 1], in1=res[:, q, :],
                                                          op0=ALU.mult, op1=ALU.add)
                    if j < TOPK - 1:
                        r_(last)
                last.then_inc(s_fin, 1)

        @block.tensor
        def _(pe):
            pe.wait_ge(s_c, 16)
            ident = const("ident")

            def transposes(u):
                if u:
                    pe.wait_ge(s_xtl, u)
                for j in range(2):
                    pe.wait_ge(s_xn, 2 * u + j + 1)
                    for k in range(K2):
                        last = nc.tensor.transpose(bank[0][:, (2 * k + j) * P:(2 * k + j + 1) * P],
                                                   xn[:, 2 * u + j, k * P:(k + 1) * P], ident)
                last.then_inc(s_xt, 1)

            def project(u):
                pe.wait_ge(s_wlo, 1)
                pe.wait_ge(s_xtl, u + 1)
                if u:
                    pe.wait_ge(s_bdf, u)
                    pe.wait_ge(s_ct, u)
                xs = [(xt_hi[:, u % 2, k], xt_lo[:, u % 2, k]) for k in range(K2)]
                split3(bank[1][0:N + H, 0:2 * P], [((wcol(w_hi, "bd", k), wcol(w_lo, "bd", k)), xs[k]) for k in range(K2)])
                split3(bank[1][:, 2 * P:4 * P], [((wcol(w_hi, "cc", k), wcol(w_lo, "cc", k)), xs[k])
                                                 for k in range(K2)]).then_inc(s_pcc, 1)

            def chunk_products(u):
                pe.wait_ge(s_bdf, u + 1)
                pe.wait_ge(s_ct, u + 1)
                if u:
                    pe.wait_ge(s_bz, u)
                    pe.wait_ge(s_gmd, u)
                for j in range(2):
                    nc.tensor.transpose(bank[2][:, j * (N + H):(j + 1) * (N + H)], bdf[:, u % 2, j * P:(j + 1) * P],
                                        const("ident")[0:N + H, 0:N + H])
                for j in range(2):
                    last = nc.tensor.matmul(bank[2][:, (2 + j) * P:(3 + j) * P], bdf[0:N, u % 2, j * P:(j + 1) * P],
                                            ct[0:N, 2 * u + j, :], start=True, stop=True)
                last.then_inc(s_pg, 1)

            def sums(u):
                pe.wait_ge(s_gmd, u + 1)
                if u:
                    pe.wait_ge(s_dec, 3 * u)
                    pe.wait_ge(s_gp, u)
                nc.tensor.matmul(bank[3][:, 2 * P:4 * P], const("spread"), gmd[:, u % 2], start=True, stop=True).then_inc(s_pgp, 1)
                pe.wait_ge(s_da, u + 1)
                d2 = da[:, u % 2].rearrange("p b h -> p (b h)")
                nc.tensor.matmul(bank[3][:, 0:2 * H], const("after"), d2, start=True, stop=True)
                nc.tensor.matmul(bank[3][:, 2 * H:4 * H], const("upto"), d2, start=True, stop=True)
                for c in range(C):
                    for j in range(2):
                        col = (4 + c) * H
                        last = nc.tensor.matmul(bank[3][N * j:N * j + N, col:col + H],
                                                const("chunk")[:, c * N:(c + 1) * N], da[:, u % 2, j, :],
                                                start=True, stop=True)
                last.then_inc(s_pd, 1)

            def states(u):
                pe.wait_ge(s_xd, u + 1)
                pe.wait_ge(s_bm, u + 2)
                if u >= 2:
                    pe.wait_ge(s_ra, adds(u - 1))
                for c in range(C):
                    if u >= PAIRS - 2 and c == C - 1:
                        continue
                    for j in range(2):
                        last = nc.tensor.matmul(bank[4 + 2 * (u % 2) + c // 2][N * j:N * j + N, D * (c % 2):D * (c % 2) + D],
                                                bm[:, u % 2, j, c, :], xd[:, u % 2, j, :], start=True, stop=True)
                last.then_inc(s_ps, 1)

            def exponents(q):
                pe.wait_ge(s_rr, q + 1)
                pe.wait_ge(s_aft, 1)
                if q >= 1:
                    pe.wait_ge(s_ex, 2 * q)
                else:
                    pe.wait_ge(s_ct, PAIRS)
                for i in range(2):
                    for part in (rr_lo, rr_hi):
                        last = nc.tensor.matmul(bank[i][:, :], after_r[:, :],
                                                part[:, q % 2, 16 * i:16 * i + 16, :].rearrange("p a l -> p (a l)"),
                                                start=(part is rr_lo), stop=(part is rr_hi))
                last.then_inc(s_e, 1)

            def outputs(q):
                g, i, j = q // BATCH, q % BATCH // 2, q % 2
                pb = bank[2 + q % 2]
                if q >= 2:
                    pe.wait_ge(s_y, q - 1)
                else:
                    pe.wait_ge(s_dec, 3 * PAIRS)
                    pe.wait_ge(s_gp, PAIRS)
                pe.wait_ge(s_ra, adds(q // 2 + 1))
                for c in range(C):
                    nc.tensor.matmul(pb[L * c:L * c + L, D:2 * D], ct[N * j:N * j + N, q, L * c:L * c + L],
                                     state[N * j:N * j + N, g, i, c, :], start=True, stop=True)
                pe.wait_ge(s_mm, q + 1)
                pe.wait_ge(s_xb[q % 2], 16 * HQ * (q // 2 + 1))
                for a in range(HG):
                    for c in range(C):
                        o = pb[L * c:L * c + L, 0:D].rearrange("p (a g e) -> p g a e", g=HG, e=HD)[:, a]
                        r = xb[:, q % 2, c].rearrange("p (a g e) -> p g a e", g=HG, e=HD)[:, a]
                        last = nc.tensor.matmul(o, mm[:, q % 2, c * HG + a, :], r, start=True, stop=True)
                last.then_inc(s_yd, 1)

            def turn_y(q):
                pe.wait_ge(s_y, q + 1)
                if q:
                    pe.wait_ge(s_ytl, q)
                else:
                    pe.wait_ge(s_ra, adds(PAIRS))
                for k in range(K2):
                    last = nc.tensor.transpose(bank[4][:, k * P:(k + 1) * P], yy[:, q % 2, k * P:(k + 1) * P], ident)
                last.then_inc(s_yt, 1)

            def project_out(q):
                pe.wait_ge(s_ytl, q + 1)
                if q:
                    pe.wait_ge(s_x1, q)
                split3(bank[5][:, 0:D], [((yt_hi[:, q % 2, k * P:(k + 1) * P], yt_lo[:, q % 2, k * P:(k + 1) * P]),
                                         (wcol(w_hi, "wo", k), wcol(w_lo, "wo", k))) for k in range(K2)]).then_inc(s_po, 1)

            def turn_x2(q):
                pe.wait_ge(s_xn2, q + 1)
                if q:
                    pe.wait_ge(s_x2c, q)
                for k in range(K2):
                    last = nc.tensor.transpose(bank[6][:, k * P:(k + 1) * P], xn2[:, q % 2, k * P:(k + 1) * P], ident)
                last.then_inc(s_x2t, 1)

            def logits(q):
                pe.wait_ge(s_x2c, q + 1)
                if q:
                    pe.wait_ge(s_lgt, q)
                for k in range(K2):
                    last = nc.tensor.matmul(bank[7][0:32, 0:P], wcol(w_raw, "wg", k), x2t[:, k * P:(k + 1) * P],
                                            start=(k == 0), stop=(k == K2 - 1))
                last.then_inc(s_lg, 1)

            for step in range(STEPS):
                for k, stage in ((4, project), (2, transposes), (5, chunk_products), (7, sums), (9, states)):
                    if 0 <= step - k < PAIRS:
                        stage(step - k)
                for k, stage in ((0, exponents), (2, outputs), (3, turn_y), (4, project_out), (6, logits), (5, turn_x2)):
                    if 0 <= step - MSTART - k < NT:
                        stage(step - MSTART - k)

            pe.wait_ge(s_lgt, NT)
            for q in range(NT):
                last = nc.tensor.transpose(bank[0][:, q * 32:(q + 1) * 32], lgt[0:32, q, :], const("ident")[0:32, 0:32])
            last.then_inc(s_plg, 1)
            pe.wait_ge(s_msk, 1)
            pe.wait_ge(s_rc, 16)
            m = msk[:, :, :].rearrange("p e q -> p (e q)")
            nc.tensor.matmul(bank[1][:, 0:E * NT], rconst("before"), m, start=True, stop=True)
            nc.tensor.matmul(bank[1][:, E * NT:2 * E * NT], rconst("ones"), m, start=True, stop=True).then_inc(s_cnt, 1)

            xs = [(tx_hi[:, k * P:(k + 1) * P], tx_lo[:, k * P:(k + 1) * P]) for k in range(K2)]

            def s_turn_x(k, par, uses):
                pe.wait_ge(s_sx[par], 16 * uses)
                if isinstance(k, int) and k == 0:
                    pe.wait_ge(s_lgc, 1)
                else:
                    pe.wait_ge(s_stxl, k)
                for c in range(K2):
                    last = nc.tensor.transpose(bank[0][:, c * P:(c + 1) * P], xg[:, par, c * P:(c + 1) * P], ident)
                last.then_inc(s_stx, 1)

            def s_up(k):
                pe.wait_ge(s_stxl, k + 1)
                for c in range(4):
                    if isinstance(k, int) and k == 0:
                        pe.wait_ge(s_ul, c + 1)
                        pe.wait_ge(s_idx, 1)
                    elif c % 2 == 0:
                        pe.wait_ge(s_sh, 2 * k)
                    split3(bank[1 + c][:, 0:2 * EI],
                           [(xs[b], (up(wu_hi, SH + c, b), up(wu_lo, SH + c, b))) for b in range(K2)]).then_inc(s_sgu, 1)

            def s_turn_h(k):
                pe.wait_ge(s_sh, 2 * k + 2)
                if isinstance(k, int) and k == 0:
                    pe.wait_ge(s_pad, 1)
                else:
                    pe.wait_ge(s_sthl, 2 * k)
                for c in range(6):
                    last = nc.tensor.transpose(bank[5 + c // 4][:, c % 4 * P:(c % 4 + 1) * P], act_h[:, c * P:(c + 1) * P], ident)
                last.then_inc(s_sth, 1)

            def s_down(k):
                pe.wait_ge(s_sthl, 2 * k + 2)
                if not isinstance(k, int) or k >= 1:
                    pe.wait_ge(s_sacc, k)
                split3(bank[7][:, 0:D], [((th_hi[:, c, :], th_lo[:, c, :]),
                                         (down(wu_hi, SH + c // 2, c % 2), down(wu_lo, SH + c // 2, c % 2)))
                                         for c in range(6)]).then_inc(s_sdn, 1)

            s_turn_x(0, 0, 1)
            s_up(0)
            s_turn_x(1, 1, 1)

            def s_step(k, n, j):
                s_turn_h(k - 1)
                s_up(k)
                if not isinstance(k, int) or k + 1 < NT:
                    s_turn_x(k + 1, (j + 1) % 2, n + (j + 1) // 2 + 1)
                s_down(k - 1)

            tiles_in_turn(pe, NT, 2, s_step)
            s_turn_h(NT - 1)
            s_down(NT - 1)

            def experts(i):
                w = pe.value_load(epack[0:1, bass.ds(i, 1)] if not isinstance(i, int) else epack[0:1, i:i + 1],
                                  min_val=0, max_val=E ** (XG + 1) - 1)
                return [w // E ** j % E for j in range(XG + 1)]

            def e_turn_x(k, slot, uses):
                pe.wait_ge(s_xg[slot], 16 * uses)
                if not isinstance(k, int) or k >= 1:
                    pe.wait_ge(s_etxl, k)
                for c in range(K2):
                    last = nc.tensor.transpose(bank[0][:, c * P:(c + 1) * P], xg[:, slot, c * P:(c + 1) * P], ident)
                last.then_inc(s_etx, 1)

            def e_up(k, par, e):
                pe.wait_ge(s_etxl, k + 1)
                if not isinstance(k, int) or k >= 2:
                    pe.wait_ge(s_eh, k - 1)
                split3(bank[1 + par][:, 0:2 * EI],
                       [(xs[b], (up(wu_hi[:, bass.ds(e, 1), :], 0, b), up(wu_lo[:, bass.ds(e, 1), :], 0, b)))
                        for b in range(K2)]).then_inc(s_egu, 1)

            def e_turn_h(k):
                pe.wait_ge(s_eh, k + 1)
                if not isinstance(k, int) or k >= 1:
                    pe.wait_ge(s_ethl, k)
                for c in range(2):
                    last = nc.tensor.transpose(bank[5][0:EK, c * P:(c + 1) * P], act_h[:, c * EK:(c + 1) * EK], ident)
                last.then_inc(s_eth, 1)

            def e_down(k, e):
                pe.wait_ge(s_ethl, k + 1)
                if not isinstance(k, int) or k >= 1:
                    pe.wait_ge(s_ey, k)
                split3(bank[7][:, 0:D], [((th_hi[0:EK, c, :], th_lo[0:EK, c, :]),
                                         (down(wu_hi[:, bass.ds(e, 1), :], 0, c, EK), down(wu_lo[:, bass.ds(e, 1), :], 0, c, EK)))
                                         for c in range(2)]).then_inc(s_edn, 1)

            pe.wait_ge(s_routed, 1)
            pe.wait_ge(s_sacc, NT)
            e_turn_x(0, 0, 1)
            pe.wait_ge(s_ul, 20)
            e_up(0, 0, experts(0)[0])
            e_turn_x(1, 1, 1)

            def e_round(i, count):
                e = experts(i)
                for j in range(1, count + 1):
                    k = i * XG + j
                    e_turn_h(k - 1)
                    e_up(k, j % 2, e[j])
                    if not isinstance(k, int) or k + 1 < XT:
                        e_turn_x(k + 1, (j + 1) % XG, i + (j + 1) // XG + 1)
                    e_down(k - 1, e[j - 1])
                return e

            rounds = (XT - 1) // XG
            with pe.Fori(0, rounds) as i:
                e_round(i, XG)
            e = e_round(rounds, XT - 1 - rounds * XG)
            e_turn_h(XT - 1)
            e_down(XT - 1, e[XT - 1 - rounds * XG])


def kernel(**inputs):
    import concourse.bacc as _bacc
    from concourse.bass_utils import run_bass_kernel_spmd as _run

    nc = _bacc.Bacc("TRN2", target_bir_lowering=False, num_devices=1)
    arrays, args = {}, {}
    for name, a in layout(inputs).items():
        a = np.ascontiguousarray(a)
        arrays[f"in_{name}"] = a
        args[name] = nc.dram_tensor(f"in_{name}", a.shape, mybir.dt.from_np(a.dtype), kind="ExternalInput").ap()
    out = nc.dram_tensor("out_0", (BATCH, SEQ, D), F32, kind="ExternalOutput").ap()
    build(nc, out=out, **args)
    r = _run(nc, [arrays], core_ids=[0])
    return r.results[0]["out_0"]


def layout(inputs):
    g = {k: np.asarray(v) for k, v in inputs.items()}

    def blocks(w):
        return w.T.reshape(w.shape[1] // P, P, w.shape[0]).transpose(1, 0, 2)

    cw = g["L0_attn_C_w"]
    router = np.concatenate([g["L0_ffn_gate_w"], g["L0_ffn_shared_gate_vec"], np.zeros((32 - ER, D), np.float32)])
    small = np.concatenate([g["L0_attn_B_w"], g["L0_attn_dt_w"], cw, cw, g["L0_attn_out_w"], router])
    bias = np.zeros((P, 2), np.float32)
    bias[:N, 0] = g["L0_attn_B_b"]
    bias[N:N + H, 0] = g["L0_attn_dt_b"]
    bias[:N, 1] = bias[N:, 1] = g["L0_attn_C_b"]
    units = np.zeros((4 + E, P, WC), np.float32)
    units[:4, :, :WU] = (g["L0_ffn_shared_gate_up"].reshape(4, 2 * EI, K2, P).transpose(0, 3, 2, 1)).reshape(4, P, WU)
    shared_down = np.zeros((6 * P, D), np.float32)
    shared_down[:SI] = g["L0_ffn_shared_down"].T
    units[:3, :, WU:] = shared_down.reshape(3, 2, P, D).transpose(0, 2, 1, 3).reshape(3, P, WD)
    units[4:, :, :WU] = g["L0_ffn_expert_gate_up"].reshape(E, 2 * EI, K2, P).transpose(0, 3, 2, 1).reshape(E, P, WU)
    units[4:, :EK, WU:] = g["L0_ffn_expert_down"].reshape(E, D, 2, EK).transpose(0, 3, 2, 1).reshape(E, EK, WD)
    cst, rcst = constants()
    return {
        "x": g["L0_attn_x"], "w_small": blocks(small), "w_bias": bias,
        "a_log": g["L0_attn_A_log"].reshape(1, H), "d_row": g["L0_attn_D"].reshape(1, H),
        "ob_row": g["L0_attn_out_b"].reshape(1, D), "cst_in": cst,
        "rcst_in": rcst, "w_units": units,
    }
```

```python
from contextlib import ExitStack

import numpy as np

import concourse.bass as bass
from concourse import mybir

ALU = mybir.AluOpType
ACT = mybir.ActivationFunctionType
AX = mybir.AxisListType
F32 = mybir.dt.float32
F32R = mybir.dt.float32r
I32 = mybir.dt.int32
U32 = mybir.dt.uint32

P = 128
L = 32
C = P // L
BATCH, SEQ, D = 4, 512, 256
GROUPS = SEQ // P
NT = BATCH * GROUPS
T = NT * P
PAIRS = NT // 2
K2 = D // P
H, HD = 32, 8
HQ, HG = 4, 8
N = 64
E, TOPK, EI, SI = 16, 4, 176, 704
EPS = 1e-5
XT = 80
ROWS = T * TOPK
ER = 17

WU = K2 * 2 * EI
WD = 2 * D
WC = WU + WD
SH = 4
EK = EI // 2
XG = 4

CONSTS = {}
RCONSTS = {}


def constants():
    r = np.arange(P)
    blk, pos = r // L, r % L
    same = blk[:, None] == blk[None, :]
    parts = {
        "ident": np.eye(P),
        "after": same & (pos[:, None] > pos[None, :]),
        "upto": same & (pos[:, None] <= pos[None, :]),
        "spread": pos[:, None] == pos[None, :],
        "tri": pos[:, None] <= np.arange(L)[None, :],
        "chunk": np.repeat(np.arange(C), N)[None, :] == blk[:, None],
    }
    routing = {
        "ones": np.ones((P, P)),
        "before": r[:, None] < r[None, :],
        "iota_e": np.broadcast_to(np.arange(E), (P, E)),
        "edges": np.broadcast_to(np.arange(NT) * P, (P, NT)),
        "keep": np.broadcast_to((np.arange(E * NT) % NT) != 0, (P, E * NT)),
        "tiles": np.broadcast_to(np.arange(XT + XG), (P, XT + XG)),
    }
    arrays = []
    for where, group in ((CONSTS, parts), (RCONSTS, routing)):
        at = 0
        for name, a in group.items():
            where[name] = (at, a.shape[1])
            at += a.shape[1]
        arrays.append(np.concatenate([np.asarray(a, np.float32) for a in group.values()], 1))
    return arrays


constants()
NC = sum(n for _, n in CONSTS.values())
NRC = sum(n for _, n in RCONSTS.values())
WS = {"bd": (0, N + H), "cc": (N + H, 2 * N), "wo": (0, D), "wg": (D, 32)}
NW1, NW2 = N + H + 2 * N, D + 32


def build(nc, x, w_small, w_bias, a_log, d_row, ob_row, cst_in, rcst_in, w_units, out):
    es = ExitStack()
    with es:
        def sem(name):
            return es.enter_context(nc.semaphore(name))

        def sb(name, shape, dt=F32, stack=None):
            return (stack or es).enter_context(nc.sbuf_tensor(name, shape, dt))

        cst = sb("cst", [P, NC])
        res = sb("res", [P, NT, D])
        rcst = sb("rcst", [P, NRC])
        xg = sb("xg", [P, XG, D])
        wgt = sb("wgt", [P, NT, TOPK])
        sig = sb("sig", [P, NT])
        pair = sb("pair", [P, NT * TOPK], I32)
        init = sb("init", [P, XT], I32)
        incl = sb("incl", [P, E])
        ef = sb("ef", [1, 2, XT + XG])
        em = sb("em", [1, XT + XG])
        ep = sb("ep", [1, 2, XT // XG])
        eq = sb("eq", [1, XT // XG])
        slot_i = sb("slot_i", [P, NT * TOPK], I32)
        tab = sb("tab", [P, XT], I32)
        tok = sb("tok", [P, XT], I32)
        epack = sb("epack", [1, XT // XG], I32)
        bank = [es.enter_context(nc.psum_tensor(f"bank{i}", [P, 512], F32)) for i in range(8)]

        def const(name):
            a, n = CONSTS[name]
            return cst[:, a:a + n]

        st = ExitStack()
        w1_raw = sb("w1_raw", [P, K2, NW1], F32, st)
        w1_hi = sb("w1_hi", [P, K2, NW1], F32R, st)
        w1_lo = sb("w1_lo", [P, K2, NW1], F32R, st)
        bias = sb("bias", [P, 2], F32, st)
        a_sb = sb("a_sb", [P, H], F32, st)
        ob_sb = sb("ob_sb", [P, D], F32, st)
        ones_col = sb("ones_col", [P, 1], F32, st)
        stat6 = sb("stat6", [P, 2, 2, 6], F32, st)
        mv = sb("mv", [P, 2, 2, 2], F32, st)
        var = sb("var", [P, 2, 2], F32, st)
        lnv = sb("lnv", [P, 2, 2], F32, st)
        y0 = sb("y0", [P, 2, 2], F32, st)
        ya = sb("ya", [P, 2], F32, st)
        yb = sb("yb", [P, 2], F32, st)
        rs = sb("rs", [P, 2], F32, st)
        xt_hi = sb("xt_hi", [P, 2, K2, 2 * P], F32R, st)
        xt_lo = sb("xt_lo", [P, 2, K2, 2 * P], F32R, st)
        bdf = sb("bdf", [N + H, 2, 2 * P], F32, st)
        bz = sb("bz", [P, 4, 2, N + H], F32, st)
        gmd = sb("gmd", [P, 2, 2 * P], F32, st)
        na = sb("na", [P, 2, H], F32, st)
        sp_e = sb("sp_e", [P, 2, H], F32, st)
        sp_l = sb("sp_l", [P, 2, H], F32, st)
        dt = sb("dt", [P, 2, 2, H], F32, st)
        da = sb("da", [P, 2, 2, H], F32, st)
        daq = sb("daq", [P, 2, 2, C, HG], F32, st)
        dec = sb("dec", [P, 2, 2, H], F32, st)
        dch = sb("dch", [P, 4, C, H], F32, st)
        xdt = sb("xdt", [P, 2, 2, D], F32, st)
        xd = sb("xd", [P, 2, 2, D], F32, st)
        bm = sb("bm", [P, 2, 2, C, N], F32, st)
        tmp_s = sb("tmp_s", [P, D], F32, st)
        state = sb("state", [P, GROUPS, 2, C, D], F32, st)
        lg = sb("lg", [P, 2, BATCH, 32], F32, st)
        mx = sb("mx", [P, BATCH], F32, st)
        shl = sb("shl", [P, BATCH, E], F32, st)
        pe_ = sb("pexp", [P, BATCH, E], F32, st)
        sgx = sb("sgx", [P, BATCH], F32, st)
        sgy = sb("sgy", [P, BATCH], F32, st)
        sm = sb("sm", [P, BATCH], F32, st)
        rc = sb("rc", [P, BATCH], F32, st)
        prob = sb("prob", [P, BATCH, E], F32, st)
        m8 = sb("m8", [P, BATCH, 8], F32, st)
        i8 = sb("i8", [P, BATCH, 8], U32, st)
        sw = sb("sw", [P, BATCH], F32, st)
        rw = sb("rw", [P, BATCH], F32, st)
        idf = sb("idf", [P, NT, TOPK], F32, st)
        xn = sb("xn", [P, NT, D], F32, st)
        ct = sb("ct", [P, NT, P], F32, st)
        gp = sb("gp", [P, NT, P], F32, st)
        d_sb = sb("d_sb", [P, H], F32, st)
        w2_raw = sb("w2_raw", [P, K2, NW2], F32, st)
        w2_hi = sb("w2_hi", [P, K2, NW2], F32R, st)
        w2_lo = sb("w2_lo", [P, K2, NW2], F32R, st)
        daq_hi = sb("daq_hi", [P, NT, C, HG], F32R, st)
        daq_lo = sb("daq_lo", [P, NT, C, HG], F32R, st)
        ecs = sb("ecs", [P, NT, H], F32, st)
        t1 = sb("t1", [P, D], F32, st)
        yy = sb("yy", [P, 2, D], F32, st)
        yt_hi = sb("yt_hi", [P, 2, D], F32R, st)
        yt_lo = sb("yt_lo", [P, 2, D], F32R, st)
        stat6b = sb("stat6b", [P, 6], F32, st)
        mvb = sb("mvb", [P, 2], F32, st)
        varb = sb("varb", [P, 1], F32, st)
        lnvb = sb("lnvb", [P, 1], F32, st)
        y0b = sb("y0b", [P, 1], F32, st)
        yab = sb("yab", [P, 1], F32, st)
        ybb = sb("ybb", [P, 1], F32, st)
        rsb = sb("rsb", [P, 1], F32, st)
        xn2 = sb("xn2", [P, 2, D], F32, st)
        x2t = sb("x2t", [P, D], F32, st)
        after_r = sb("after_r", [P, P], F32R, st)
        rr_hi = sb("rr_hi", [P, 2, C * HG, L], F32R, st)
        rr_lo = sb("rr_lo", [P, 2, C * HG, L], F32R, st)
        ex = sb("ex", [P, 2, C * HG, L], F32, st)
        mm = sb("mm", [P, 2, C * HG, L], F32, st)
        xb = sb("xb", [P, 2, C, D], F32, st)
        st.close()

        rw4 = ExitStack()
        sb("under_raw", [P, SH, 2, WC], F32, rw4)
        raw = sb("raw", [P, SH * WC - WD], F32, rw4)
        rw4.close()

        rt = ExitStack()
        sb("under_routing", [P, E - 4, 2, WC], F32, rt)
        oh = sb("oh", [P, NT, TOPK, E], F32, rt)
        msk = sb("msk", [P, E, NT], F32, rt)
        inc = sb("inc", [P, E, NT], F32, rt)
        exc = sb("exc", [P, E, NT], F32, rt)
        gt = sb("gt", [P, E, NT], F32, rt)
        tl = sb("tl", [P, E], F32, rt)
        base = sb("base", [P, E], F32, rt)
        sl = sb("sl", [P, E, NT], F32, rt)
        sl2 = sb("sl2", [P, E, NT], F32, rt)
        so = sb("so", [P, NT, TOPK, E], F32, rt)
        slf = sb("slf", [P, NT * TOPK], F32, rt)
        si = sb("si", [P, NT * TOPK], I32, rt)
        s_hi7 = sb("s_hi7", [P, NT * TOPK], I32, rt)
        s_lo7 = sb("s_lo7", [P, NT * TOPK], I32, rt)
        rt.close()

        fin = ExitStack()
        yl = sb("yl", [P, NT, TOPK * D], F32, fin)
        fin.close()

        pl = ExitStack()
        sb("under_places", [P, 2, 2, WC], F32, pl)
        place23 = sb("place23", [P, 2, 2, WC], F32, pl)
        pl.close()

        wu = sb("wu", [P, E, 2, WC], F32R)
        stage_w = sb("stage_w", [P, 2, WC])
        tx_hi = sb("tx_hi", [P, D], F32R)
        tx_lo = sb("tx_lo", [P, D], F32R)
        act_s = sb("act_s", [P, SI])
        act_h = sb("act_h", [P, 6 * P])
        th_hi = sb("th_hi", [P, 6, P], F32R)
        th_lo = sb("th_lo", [P, 6, P], F32R)
        y_sb = sb("y_sb", [P, 2, D])
        xt2_hi = [tx_hi[:, :], th_hi[:, 2:4, :].rearrange("p c t -> p (c t)")]
        xt2_lo = [tx_lo[:, :], th_lo[:, 2:4, :].rearrange("p c t -> p (c t)")]
        et_hi = [th_hi[0:EK, 4 * h:4 * h + 2, :] for h in range(2)]
        et_lo = [th_lo[0:EK, 4 * h:4 * h + 2, :] for h in range(2)]
        stage_d = y_sb[:, :, :].rearrange("p a d -> p (a d)")

        table_d = nc.dram_tensor("table_dram", (P * XT, 1), I32, kind="Internal").ap()
        y_d = nc.dram_tensor("y_dram", (ROWS + P * XT, D), F32, kind="Internal").ap()
        out_v = out.rearrange("b (g p) d -> g b p d", p=P)

        xdt_d = nc.dram_tensor("xdt_dram", (NT, P, D), F32, kind="Internal").ap()
        xn2_d = nc.dram_tensor("xn2_dram", (T, D), F32, kind="Internal").ap()
        x_v = x.rearrange("b (g p) d -> g p b d", p=P)

        s_c = sem("s_const")
        s_x = [sem(f"s_x_in{g}") for g in range(GROUPS)]
        s_w, s_w2 = sem("s_w"), sem("s_w2")
        s_small = sem("s_small")
        s_whi, s_wlo = sem("s_whi"), sem("s_wlo")
        s_zero = sem("s_zero")
        s_ea = sem("s_ea")
        s_st, s_mv, s_var = sem("s_st"), sem("s_mv"), sem("s_var")
        s_ln, s_y0 = sem("s_ln"), sem("s_y0")
        s_nw = sem("s_nw")
        s_xn = sem("s_xn")
        s_xt, s_xth, s_xtl = sem("s_xt"), sem("s_xth"), sem("s_xtl")
        s_pcc, s_bdf, s_ct = sem("s_pcc"), sem("s_bdf"), sem("s_ct")
        s_pg, s_bz, s_gmd = sem("s_pg"), sem("s_bz"), sem("s_gmd")
        s_na, s_spe, s_spl = sem("s_na"), sem("s_spe"), sem("s_spl")
        s_dt, s_da, s_daq, s_dqh, s_dql, s_aft = sem("s_dt"), sem("s_da"), sem("s_daq"), sem("s_dqh"), sem("s_dql"), sem("s_aft")
        s_pd, s_pgp = sem("s_pd"), sem("s_pgp")
        s_dec, s_gp = sem("s_dec"), sem("s_gp")
        s_xdt, s_xd, s_bm, s_xdtw = sem("s_xdt"), sem("s_xd"), sem("s_bm"), [sem("s_xdtw0"), sem("s_xdtw1")]
        s_ps, s_rm, s_ra = sem("s_ps"), sem("s_rm"), sem("s_ra")
        s_rr, s_rl, s_e, s_ex, s_mm = sem("s_rr"), sem("s_rl"), sem("s_e"), sem("s_ex"), sem("s_mm")
        s_xb = [sem("s_xb0"), sem("s_xb1")]
        s_xnd, s_xob = sem("s_xnd"), sem("s_xob")
        s_yd, s_t1, s_y = sem("s_yd"), sem("s_t1"), sem("s_y")
        s_yt, s_yth, s_ytl, s_po, s_x1 = sem("s_yt"), sem("s_yth"), sem("s_ytl"), sem("s_po"), sem("s_x1")
        s_st2, s_mv2, s_var2, s_ln2, s_y02, s_xn2 = (sem("s_st2"), sem("s_mv2"), sem("s_var2"), sem("s_ln2"),
                                                           sem("s_y02"), sem("s_xn2"))
        s_x2d = [sem("s_x2d0"), sem("s_x2d1")]
        s_x2t, s_x2c, s_lg, s_lgt = sem("s_x2t"), sem("s_x2c"), sem("s_lg"), sem("s_lgt")
        s_out = [sem("s_out0"), sem("s_out1")]
        s_shl, s_gex, s_gate = sem("s_shl"), sem("s_gex"), sem("s_gate")
        s_rc, s_iota, s_init = sem("s_rc"), sem("s_iota"), sem("s_init")
        s_r, s_cnt, s_msk = sem("s_r"), sem("s_cnt"), sem("s_msk")
        s_idx, s_tabw, s_tab, s_tok, s_routed = sem("s_idx"), sem("s_tabw"), sem("s_tab"), sem("s_tok"), sem("s_routed")
        s_raw, s_rawh, s_rawl = sem("s_raw"), sem("s_rawh"), sem("s_rawl")
        s_last = [sem(f"s_last{i}") for i in range(4)]
        s_ws, s_uh, s_ul = [sem("s_ws0"), sem("s_ws1")], sem("s_uh"), sem("s_ul")
        s_sx = [sem("s_sx0"), sem("s_sx1")]
        s_stx, s_stxh, s_stxl, s_sgu, s_ssi, s_sh = sem("s_stx"), sem("s_stxh"), sem("s_stxl"), sem("s_sgu"), sem("s_ssi"), sem("s_sh")
        s_sth, s_sthh, s_sthl, s_sdn, s_sacc = sem("s_sth"), sem("s_sthh"), sem("s_sthl"), sem("s_sdn"), sem("s_sacc")
        s_xg = [sem(f"s_xg{i}") for i in range(XG)]
        s_etx, s_etxh, s_etxl, s_egu, s_esi, s_eh = sem("s_etx"), sem("s_etxh"), sem("s_etxl"), sem("s_egu"), sem("s_esi"), sem("s_eh")
        s_eth, s_ethh, s_ethl, s_edn, s_ey = sem("s_eth"), sem("s_ethh"), sem("s_ethl"), sem("s_edn"), sem("s_ey")
        s_sc = [sem("s_sc0"), sem("s_sc1")]
        s_yl, s_fin, s_pad = [sem(f"s_yl{q}") for q in range(NT)], sem("s_fin"), sem("s_pad")
        s_ef = sem("s_ef")

        def rconst(name):
            a, n = RCONSTS[name]
            return rcst[:, a:a + n]

        def last_part(place, up_part):
            cols = slice(0, WU) if up_part else slice(WU, WC)
            if place < 2:
                return place, cols, stage_w[:, place, cols], s_ws[place], 16 * (E - SH + 2) // 2
            if place == 2 and not up_part:
                return place, cols, stage_d, s_last[0], 16
            return place, cols, place23[:, place - 2, 1, cols], s_last[place if up_part else 1], 16

        LAST = [last_part(3, False), last_part(0, True), last_part(1, True), last_part(2, True), last_part(3, True),
                last_part(0, False), last_part(1, False), last_part(2, False)]

        def unit_width(u):
            return WC if u < SH - 1 else WU

        def up(slot, k):
            return [wu[:, slot, i, k * 2 * EI:(k + 1) * 2 * EI] for i in range(2)]

        def down(slot, k, rows=P):
            return [wu[0:rows, slot, i, WU + k * D:WU + (k + 1) * D] for i in range(2)]

        def expert_tiles(eng, step):
            rounds = (XT - 2) // XG
            for k in range(1, XG + 2):
                step(k, k // XG, k % XG)
            with eng.Fori(1, rounds) as i:
                for j in range(2, XG + 2):
                    step(i * XG + j, i + j // XG, j % XG)
            for k in range(rounds * XG + 2, XT):
                step(k, k // XG, k % XG)

        def split3(out_ap, pairs):
            n = 3 * len(pairs)
            i = 0
            for (lh, ll), (rh, rl) in pairs:
                for a, b in ((lh, rl), (ll, rh), (lh, rh)):
                    last = nc.tensor.matmul(out_ap, a, b, start=(i == 0), stop=(i == n - 1))
                    i += 1
            return last

        MSTART = 13
        STEPS = MSTART + NT + 10
        ROUTE = 11
        EARLY = 4
        SPLIT = NT - 3

        def adds(u):
            return 1 + C * u - max(0, u - (PAIRS - 2))

        def wcol(w, name, k):
            a, n = WS[name]
            return w[:, k, a:a + n]

        def by_head(ap):
            return ap.rearrange("p (h e) -> p h e", e=HD)

        def shared_rows(eng, k, par):
            eng.dma_start(xg[:, par, :], xn2_d.rearrange("(q p) d -> q p d", p=P)[k]).then_inc(s_sx[par], 16)

        def masked(eng, part, of, q):
            return eng.tensor_tensor(part[:, q % 2], of[:, q].rearrange("p c a -> p (c a)").unsqueeze(2).to_broadcast([P, C * HG, L]),
                                     const("tri").unsqueeze(1).to_broadcast([P, C * HG, L]), ALU.mult)

        block = es.enter_context(nc.Block())

        @block.sync
        def _(sp):
            for g in range(GROUPS):
                sp.dma_start(res[:, g * BATCH:(g + 1) * BATCH, :], x_v[g]).then_inc(s_x[g], 16)
                if g == 0:
                    sp.dma_start(cst[:, :], cst_in).then_inc(s_c, 16)
            sp.dma_start(rcst[:, :], rcst_in).then_inc(s_rc, 16)
            sp.wait_ge(s_iota, 2)
            sp.dma_start(table_d.rearrange("(p t) o -> p (t o)", t=XT), init[:, :]).then_inc(s_init, 16)
            for step in range(-PAIRS, NT + 5):
                u = step + PAIRS
                if u < PAIRS:
                    sp.wait_ge(s_xdt, u + 1)
                    sp.dma_start(xdt_d[2 * u:2 * u + 2].rearrange("b p d -> p b d"),
                                 xdt[:, u % 2]).then_inc(s_xdtw[u % 2], 16)
                q = step
                if 0 <= q < NT:
                    u = q // 2
                    sp.wait_ge(s_xdtw[u % 2], 16 * (u // 2 + 1))
                    if q >= 2:
                        sp.wait_ge(s_yd, q - 1)
                    else:
                        sp.wait_ge(s_zero, 3)
                    for a in range(HQ):
                        src = xdt_d[q].rearrange("(c s) (a e) -> a s c e", c=C, a=HQ)[a]
                        sp.dma_start(xb[L * a:L * a + L, q % 2, :, a * N:(a + 1) * N], src).then_inc(s_xb[q % 2], 16)
                q = step - 5
                if step == 2 * BATCH + 2:
                    sp.wait_ge(s_yd, 2 * BATCH)
                    sp.wait_ge(s_ra, adds(PAIRS))
                    sp.wait_ge(s_dql, PAIRS)
                    sp.wait_ge(s_xdtw[1], 16 * PAIRS // 2)
                    for u in range(SH):
                        n = unit_width(u)
                        sp.dma_start(raw[:, u * WC:u * WC + n], w_units[u, :, 0:n]).then_inc(s_raw, 16)
                if 0 <= q < NT:
                    sp.wait_ge(s_xn2, q + 1)
                    sp.dma_start(xn2_d[q * P:(q + 1) * P, :], xn2[:, q % 2, :]).then_inc(s_x2d[q % 2], 16)
                if q == NT - 2:
                    for k in range(2):
                        shared_rows(sp, k, k)
            def load_unit(n, par):
                sp.dma_start(stage_w[:, par, :], w_units[n + SH]).then_inc(s_ws[par], 16)

            sp.wait_ge(s_yd, NT)
            load_unit(0, 0)
            load_unit(1, 1)
            with sp.Fori(0, (E - SH) // 2) as i:
                for j in range(2):
                    k = 2 * i + j + 2
                    sp.wait_ge(s_ul, k - 1)
                    load_unit(k, j)
            sp.dma_start(stage_d, w_units[SH + E - 2, :, WU:WC]).then_inc(s_last[0], 16)
            sp.dma_start(place23[:, 1, 1, WU:WC], w_units[SH + E - 1, :, WU:WC]).then_inc(s_last[1], 16)
            sp.wait_ge(s_tabw, 16 * NT * TOPK)
            sp.dma_start(tab[:, :], table_d.rearrange("(p t) o -> p (t o)", t=XT)).then_inc(s_tab, 16)
            sp.wait_ge(s_sgu, 4 * NT)
            for i in range(2):
                sp.dma_start(place23[:, i, 1, 0:WU], w_units[SH + E - 2 + i, :, 0:WU]).then_inc(s_last[2 + i], 16)

            y_v = y_d[0:ROWS, :].rearrange("(q p j) d -> q p (j d)", p=P, j=TOPK)
            sp.wait_ge(s_edn, XT)
            for i in range(2):
                sp.wait_ge(s_sc[i], 16 * XT // 2)
            for q in range(NT):
                sp.dma_start(yl[:, q, :], y_v[q]).then_inc(s_yl[q], 16)
            for q in range(NT):
                sp.wait_ge(s_fin, q + 1)
                sp.dma_start(out_v[q // BATCH, q % BATCH], res[:, q, :]).then_inc(s_out[q % 2], 16)
            for i in range(2):
                sp.wait_ge(s_out[i], 16 * NT // 2)

        @block.gpsimd
        def _(pool):
            nc.gpsimd.iota(pair[:, :], [[TOPK * P, NT], [1, TOPK]], base=0, channel_multiplier=TOPK).then_inc(s_iota, 1)
            nc.gpsimd.iota(init[:, :], [[1, XT]], base=ROWS, channel_multiplier=XT).then_inc(s_iota, 1)
            nc.gpsimd.memset(ones_col[:, :], 1.0).then_inc(s_zero, 1)
            nc.gpsimd.memset(xb[:, 0], 0.0).then_inc(s_zero, 1)
            nc.gpsimd.memset(xb[:, 1], 0.0).then_inc(s_zero, 1)
            nc.gpsimd.memset(bm[:, :, :, :, :], 0.0).then_inc(s_bm, 1)
            pool.wait_ge(s_c, 16)
            nc.gpsimd.tensor_copy(after_r[:, :], const("after")).then_inc(s_aft, 1)
            pool.wait_ge(s_small, 64)

            def with_bias(u):
                pool.wait_ge(s_xn, 2 * (u + 1))
                nc.gpsimd.tensor_tensor(res[:, 2 * u:2 * u + 2], res[:, 2 * u:2 * u + 2],
                                        ob_sb[:, :].unsqueeze(1).to_broadcast([P, 2, D]), ALU.add).then_inc(s_xob, 1)

            def inputs(u):
                if u >= 2:
                    pool.wait_ge(s_xdtw[u % 2], 16 * (u // 2))
                pool.wait_ge(s_dt, u + 1)
                for j in range(2):
                    i = nc.gpsimd.tensor_tensor(by_head(xdt[:, u % 2, j]), by_head(xn[:, 2 * u + j]),
                                                dt[:, u % 2, j].unsqueeze(2).to_broadcast([P, H, HD]), ALU.mult)
                i.then_inc(s_xdt, 1)
                if u >= 2:
                    pool.wait_ge(s_ps, u - 1)
                pool.wait_ge(s_xdt, u + 1)
                pool.wait_ge(s_dec, 3 * u + 1)
                for j in range(2):
                    i = nc.gpsimd.tensor_tensor(by_head(xd[:, u % 2, j]), by_head(xdt[:, u % 2, j]),
                                                dec[:, u % 2, j].unsqueeze(2).to_broadcast([P, H, HD]), ALU.mult)
                i.then_inc(s_xd, 1)
                pool.wait_ge(s_daq, C * HQ * (u + 1))
                dq = slice(2 * u, 2 * u + 2)
                nc.gpsimd.tensor_copy(daq_hi[:, dq], daq[:, u % 2]).then_inc(s_dqh, 1)
                pool.wait_ge(s_dqh, u + 1)
                nc.gpsimd.tensor_tensor(daq_lo[:, dq], daq[:, u % 2], daq_hi[:, dq], ALU.subtract).then_inc(s_dql, 1)

            def skip_part(u):
                for j in range(2):
                    i = nc.gpsimd.tensor_tensor(by_head(xn[:, 2 * u + j]), by_head(xn[:, 2 * u + j]),
                                                d_sb[:, :].unsqueeze(2).to_broadcast([P, H, HD]), ALU.mult)
                i.then_inc(s_xnd, 1)

            def increments(q):
                if q >= 2:
                    pool.wait_ge(s_e, q - 1)
                pool.wait_ge(s_dql, q // 2 + 1)
                last = masked(nc.gpsimd, rr_hi, daq_hi, q)
                if q >= EARLY:
                    last = masked(nc.gpsimd, rr_lo, daq_lo, q)
                last.then_inc(s_rr, 1)

            for step in range(STEPS):
                for u, stage in ((step - 8, inputs), (step - 2, with_bias)):
                    if 0 <= u < PAIRS:
                        stage(u)
                m = step - MSTART
                if 0 <= m < NT:
                    increments(m)
                    if m % 2 == 1:
                        skip_part(m // 2)
            for u in range(SH):
                pool.wait_ge(s_rawh, u + 1)
                n = unit_width(u)
                nc.gpsimd.tensor_tensor(wu[:, u, 1, 0:n], raw[:, u * WC:u * WC + n], wu[:, u, 0, 0:n],
                                        ALU.subtract).then_inc(s_rawl, 1)
            pool.wait_ge(s_iota, 2)
            pool.wait_ge(s_init, 16)
            pool.wait_ge(s_idx, 1)
            for i in range(NT * TOPK):
                pool.indirect_dma_start(out=table_d, out_offset=bass.IndirectOffsetOnAxis(ap=slot_i[:, i:i + 1], axis=0),
                                        in_=pair[:, i:i + 1], in_offset=None).then_inc(s_tabw, 16)

            pool.wait_ge(s_rc, 16)
            n_ef = [0]

            def small(ins):
                ins.then_inc(s_ef, 1)
                n_ef[0] += 1
                pool.wait_ge(s_ef, n_ef[0])

            small(nc.gpsimd.tensor_scalar(ef[:, 0, :], rconst("tiles")[0:1, :], incl[0:1, 0:1], None, ALU.is_ge))
            for e in range(1, E):
                small(nc.gpsimd.tensor_scalar(em[:, :], rconst("tiles")[0:1, :], incl[0:1, e:e + 1], None, ALU.is_ge))
                small(nc.gpsimd.tensor_tensor(ef[:, e % 2, :], ef[:, (e - 1) % 2, :], em[:, :], ALU.add))
            small(nc.gpsimd.tensor_scalar(em[:, :], ef[:, (E - 1) % 2, :], float(E - 1), None, ALU.min))
            e4 = em[:, :].rearrange("o (i j) -> o i j", j=XG)
            np_ = XT // XG
            for j in range(1, XG + 2):
                src = e4[:, j // XG:np_ + j // XG, j % XG]
                low = ep[:, (j - 1) % 2, :] if j > 1 else e4[:, 0:np_, 0]
                small(nc.gpsimd.tensor_scalar(eq[:, :], src, float(E ** j), None, ALU.mult))
                small(nc.gpsimd.tensor_tensor(ep[:, j % 2, :], eq[:, :], low, ALU.add))
            nc.gpsimd.tensor_copy(epack[:, :], ep[:, (XG + 1) % 2, :]).then_inc(s_routed, 1)

            def gather(k):
                if k >= XG:
                    pool.wait_ge(s_etx, k - XG + 1)
                pool.indirect_dma_start(out=xg[:, k % XG, :], out_offset=None, in_=xn2_d,
                                        in_offset=bass.IndirectOffsetOnAxis(ap=tok[:, k:k + 1], axis=0)).then_inc(s_xg[k % XG], 16)

            pool.wait_ge(s_tok, 1)
            pool.wait_ge(s_stx, NT)
            for k in range(XG):
                gather(k)
            for k in range(XT + 2):
                if k + XG < XT:
                    gather(k + XG)
                if k >= 2:
                    pool.wait_ge(s_ey, k - 1)
                    pool.indirect_dma_start(out=y_d, out_offset=bass.IndirectOffsetOnAxis(ap=tab[:, k - 2:k - 1], axis=0),
                                            in_=y_sb[:, k % 2, :], in_offset=None).then_inc(s_sc[k % 2], 16)

        @block.scalar
        def _(act):
            nc.scalar.preload_act_table_set("natural_log_exp_and_others")
            act.dma_start(w1_raw[:, :, :], w_small[:, :, 0:NW1]).then_inc(s_w, 16)
            act.dma_start(bias[:, :], w_bias).then_inc(s_small, 16)
            act.dma_start(a_sb[:, :], a_log.to_broadcast([P, H])).then_inc(s_small, 16)
            act.dma_start(d_sb[:, :], d_row.to_broadcast([P, H])).then_inc(s_small, 16)
            act.dma_start(ob_sb[:, :], ob_row.to_broadcast([P, D])).then_inc(s_small, 16)
            act.dma_start(w2_raw[:, :, :], w_small[:, :, NW1:NW1 + NW2]).then_inc(s_w2, 16)
            act.wait_ge(s_w, 16)
            nc.scalar.copy(w1_hi[:, :, :], w1_raw[:, :, :]).then_inc(s_whi, 1)
            act.wait_ge(s_zero, 1)

            def rstd_guess(u):
                act.wait_ge(s_var, u + 1)
                nc.scalar.activation(lnv[:, u % 2], var[:, u % 2], ACT.Ln).then_inc(s_ln, 1)
                act.wait_ge(s_ln, u + 1)
                nc.scalar.activation(y0[:, u % 2], lnv[:, u % 2], ACT.Exp, scale=-0.5).then_inc(s_y0, 1)

            def high_parts(u):
                act.wait_ge(s_xt, u + 1)
                if u >= 2:
                    act.wait_ge(s_pcc, u - 1)
                nc.scalar.copy(xt_hi[:, u % 2].rearrange("p k t -> p (k t)"), bank[0][:, :]).then_inc(s_xth, 1)

            def projected(u):
                act.wait_ge(s_pcc, u + 1)
                if u == 0:
                    act.wait_ge(s_small, 64)
                if u >= 2:
                    act.wait_ge(s_pg, u - 1)
                nc.scalar.activation(bdf[:, u % 2], bank[1][0:N + H, 0:2 * P], ACT.Identity,
                                     bias=bias[0:N + H, 0:1]).then_inc(s_bdf, 1)
                nc.scalar.activation(ct[:, 2 * u:2 * u + 2, :].rearrange("p b t -> p (b t)"), bank[1][:, 2 * P:4 * P],
                                     ACT.Identity, bias=bias[:, 1:2]).then_inc(s_ct, 1)

            def token_major(u):
                act.wait_ge(s_pg, u + 1)
                if u >= 4:
                    act.wait_ge(s_bm, u - 2)
                    act.wait_ge(s_dt, u - 3)
                nc.scalar.copy(bz[:, u % 4].rearrange("p b j -> p (b j)"), bank[2][:, 0:2 * (N + H)]).then_inc(s_bz, 1)

            def softplus(u):
                act.wait_ge(s_na, u + 1)
                nc.scalar.activation(sp_e[:, :, :], na[:, :, :], ACT.Exp).then_inc(s_spe, 1)
                act.wait_ge(s_spe, u + 1)
                if u:
                    act.wait_ge(s_dt, u)
                nc.scalar.activation(sp_l[:, :, :], sp_e[:, :, :], ACT.Ln, bias=ones_col[:, 0:1]).then_inc(s_spl, 1)

            def blocks(u):
                if u >= 2:
                    act.wait_ge(s_ps, u - 1)
                act.wait_ge(s_bm, u + 1)
                for c in range(C):
                    i = nc.scalar.copy(bm[L * c:L * c + L, u % 2, :, c, :], bz[L * c:L * c + L, u % 4, :, 0:N])
                i.then_inc(s_bm, 1)

            def by_quarter(u):
                act.wait_ge(s_da, u + 1)
                if u >= 2:
                    act.wait_ge(s_dql, u - 1)
                for a in range(HQ):
                    for c in range(C):
                        nc.scalar.copy(daq[L * a:L * a + L, u % 2, :, c, :],
                                       da[L * c:L * c + L, u % 2, :, a * HG:(a + 1) * HG]).then_inc(s_daq, 1)

            def decays(u):
                act.wait_ge(s_pd, u + 1)
                if u >= 2:
                    act.wait_ge(s_xd, u - 1)
                if u >= 4:
                    act.wait_ge(s_ra, adds(u - 3))
                nc.scalar.activation(dec[:, u % 2].rearrange("p b h -> p (b h)"), bank[3][:, 0:2 * H], ACT.Exp).then_inc(s_dec, 1)
                nc.scalar.activation(ecs[:, 2 * u:2 * u + 2, :].rearrange("p b h -> p (b h)"),
                                     bank[3][:, 2 * H:4 * H], ACT.Exp).then_inc(s_dec, 1)
                nc.scalar.activation(dch[:, u % 4].rearrange("p c h -> p (c h)"), bank[3][:, 4 * H:4 * H + C * H],
                                     ACT.Exp).then_inc(s_dec, 1)
                nc.scalar.copy(gp[:, 2 * u:2 * u + 2, :].rearrange("p b t -> p (b t)"), bank[3][:, 2 * P:4 * P]).then_inc(s_gp, 1)

            def expo(q):
                act.wait_ge(s_e, q + 1)
                if q >= 2:
                    act.wait_ge(s_mm, q - 1)
                for i in range(2):
                    nc.scalar.activation(ex[:, q % 2, 16 * i:16 * i + 16, :].rearrange("p a l -> p (a l)"),
                                         bank[i][:, :], ACT.Exp).then_inc(s_ex, 1)

            def y_high(q):
                act.wait_ge(s_yt, q + 1)
                if q >= 2:
                    act.wait_ge(s_po, q - 1)
                nc.scalar.copy(yt_hi[:, q % 2], bank[4][:, 0:D]).then_inc(s_yth, 1)

            def rstd2(q):
                act.wait_ge(s_var2, q + 1)
                nc.scalar.activation(lnvb[:, :], varb[:, :], ACT.Ln).then_inc(s_ln2, 1)
                act.wait_ge(s_ln2, q + 1)
                nc.scalar.activation(y0b[:, :], lnvb[:, :], ACT.Exp, scale=-0.5).then_inc(s_y02, 1)

            def x2_copy(q):
                act.wait_ge(s_x2t, q + 1)
                if q:
                    act.wait_ge(s_lg, q)
                nc.scalar.copy(x2t[:, :], bank[6][:, 0:D]).then_inc(s_x2c, 1)

            def logits_copy(q):
                act.wait_ge(s_lg, q + 1)
                g = q // BATCH
                if g >= 2:
                    act.wait_ge(s_gate, g - 1)
                nc.scalar.copy(lg[:, g % 2, q % BATCH, :], bank[7][:, 0:32]).then_inc(s_lgt, 1)

            def gate_exps(g):
                act.wait_ge(s_lgt, BATCH * (g + 1))
                if g:
                    act.wait_ge(s_gate, g)
                nc.scalar.activation(sgx[:, :], lg[:, g % 2, :, E], ACT.Exp, scale=-1.0).then_inc(s_gex, 1)
                act.wait_ge(s_shl, g + 1)
                nc.scalar.activation(pe_[:, :, :].rearrange("p q e -> p (q e)"), shl[:, :, :].rearrange("p q e -> p (q e)"),
                                     ACT.Exp).then_inc(s_gex, 1)

            def raw_high(u):
                act.wait_ge(s_raw, 16 * SH)
                n = unit_width(u)
                nc.scalar.copy(wu[:, u, 0, 0:n], raw[:, u * WC:u * WC + n]).then_inc(s_rawh, 1)

            def s_xhigh(k):
                act.wait_ge(s_stx, k + 1)
                if not isinstance(k, int) or k >= 1:
                    act.wait_ge(s_sgu, 4 * k)
                nc.scalar.copy(tx_hi[:, :], bank[0][:, 0:D]).then_inc(s_stxh, 1)

            for step in range(STEPS):
                for k, stage in ((1, rstd_guess), (2, high_parts), (4, projected), (5, token_major), (6, softplus),
                                 (7, decays), (7, by_quarter), (8, blocks)):
                    if 0 <= step - k < PAIRS:
                        stage(step - k)
                if step == 5:
                    act.wait_ge(s_small, 64)
                    nc.scalar.activation(a_sb[:, :], a_sb[:, :], ACT.Exp).then_inc(s_ea, 1)
                m = step - MSTART
                if m == 0:
                    act.wait_ge(s_w2, 16)
                    nc.scalar.copy(w2_hi[:, :, :], w2_raw[:, :, :]).then_inc(s_whi, 1)
                for k, stage in ((0, expo), (5, rstd2), (3, y_high), (7, logits_copy), (6, x2_copy)):
                    if 0 <= m - k < NT:
                        stage(m - k)
                if m >= ROUTE and (m - ROUTE) % BATCH == 0:
                    gate_exps((m - ROUTE) // BATCH)
                if 0 <= m - SPLIT < SH:
                    raw_high(m - SPLIT)
                if m == NT + 5:
                    s_xhigh(0)

            def split_high(slot, n, par, uses):
                act.wait_ge(s_ws[par], 16 * uses)
                nc.scalar.copy(wu[:, slot, 0, :], stage_w[:, par, :]).then_inc(s_uh, 1)

            def s_thigh(k):
                act.wait_ge(s_sth, k + 1)
                if not isinstance(k, int) or k >= 1:
                    act.wait_ge(s_sdn, k)
                nc.scalar.copy(th_hi[:, 0:4, :].rearrange("p c t -> p (c t)"), bank[5][:, :]).then_inc(s_sthh, 1)
                nc.scalar.copy(th_hi[:, 4:6, :].rearrange("p c t -> p (c t)"), bank[6][:, 0:2 * P]).then_inc(s_sthh, 1)

            def s_silu(k):
                for c in range(2):
                    act.wait_ge(s_sgu, 4 * k + c + 1)
                    if not isinstance(k, int) or k >= 1:
                        act.wait_ge(s_sh, 2 * k + c - 1)
                    nc.scalar.activation(act_s[:, c * 352:(c + 1) * 352], bank[1 + c][:, 0:352], ACT.Silu).then_inc(s_ssi, 1)

            for i in range(2):
                act.wait_ge(s_x2d[i], 16 * NT // 2)
            shared_rows(act, 2, 0)
            s_silu(0)
            s_xhigh(1)
            shared_rows(act, 3, 1)
            def s_step(i, j):
                k = 2 * i + j + 1
                s_thigh(k - 1)
                s_silu(k)
                s_xhigh(k + 1)
                shared_rows(act, k + 3, j)
                split_high(k + 3, k - 1, j, i + 1)

            for j in range(2):
                s_step(0, j)
            with act.Fori(1, (E - SH) // 2) as i:
                for j in range(2):
                    s_step(i, j)
            def last_high(i):
                place, cols, src, loaded, n = LAST[i]
                act.wait_ge(loaded, n)
                if i >= 5:
                    act.wait_ge(s_sdn, NT)
                elif i >= 1:
                    act.wait_ge(s_sgu, 4 * NT)
                nc.scalar.copy(wu[:, place, 0, cols], src).then_inc(s_uh, 1)

            for k in range(E - SH + 1, NT):
                s_thigh(k - 1)
                s_silu(k)
                if k + 1 < NT:
                    s_xhigh(k + 1)
            for i in range(3):
                last_high(i)
            s_thigh(NT - 1)
            for i in range(3, 5):
                last_high(i)
            def e_thigh(k, par):
                act.wait_ge(s_eth, k + 1)
                if not isinstance(k, int) or k >= 2:
                    act.wait_ge(s_edn, k - 1)
                nc.scalar.copy(et_hi[par].rearrange("p c t -> p (c t)"), bank[5][0:EK, 0:2 * P]).then_inc(s_ethh, 1)

            def e_silu(k, par):
                act.wait_ge(s_egu, k + 1)
                if not isinstance(k, int) or k >= 1:
                    act.wait_ge(s_eh, k)
                nc.scalar.activation(act_s[:, 0:EI], bank[1 + par][:, 0:EI], ACT.Silu).then_inc(s_esi, 1)

            def e_xhigh(k, par):
                act.wait_ge(s_etx, k + 1)
                if not isinstance(k, int) or k >= 2:
                    act.wait_ge(s_egu, k - 1)
                nc.scalar.copy(xt2_hi[par], bank[0][:, 0:D]).then_inc(s_etxh, 1)

            def e_result(k, par, uses):
                act.wait_ge(s_edn, k + 1)
                if not isinstance(uses, int) or uses >= 1:
                    act.wait_ge(s_sc[par], 16 * uses)
                nc.scalar.copy(y_sb[:, par, :], bank[7][:, 0:D]).then_inc(s_ey, 1)

            act.wait_ge(s_sthl, 2 * NT)
            e_xhigh(0, 0)
            for i in range(5, 8):
                last_high(i)
            e_xhigh(1, 1)
            e_silu(0, 0)
            e_xhigh(2, 0)

            def e_step(k, n, j):
                e_silu(k, j % 2)
                if not isinstance(k, int) or k + 2 < XT:
                    e_xhigh(k + 2, j % 2)
                e_thigh(k - 1, (j - 1) % 2)
                if not isinstance(k, int) or k >= 2:
                    e_result(k - 2, j % 2, n * (XG // 2) + j // 2 - 1)

            expert_tiles(act, e_step)
            e_thigh(XT - 1, (XT - 1) % 2)
            for k in (XT - 2, XT - 1):
                e_result(k, k % 2, k // 2)

        @block.vector
        def _(dve):
            dve.wait_ge(s_whi, 1)
            nc.vector.tensor_tensor(w1_lo[:, :, :], w1_raw[:, :, :], w1_hi[:, :, :], ALU.subtract).then_inc(s_wlo, 1)
            nc.vector.memset(state[:, 0, :, 0, :], 0.0).then_inc(s_ra, 1)
            nw = [0]

            def newton(v, y, a, b, r):
                ops = (lambda: nc.vector.tensor_tensor(a, y, y, ALU.mult),
                       lambda: nc.vector.scalar_tensor_tensor(out=b, in0=a, scalar=-0.5, in1=v, op0=ALU.mult, op1=ALU.mult),
                       lambda: nc.vector.scalar_tensor_tensor(out=r, in0=b, scalar=1.5, in1=y, op0=ALU.add, op1=ALU.mult))
                for op in ops:
                    op().then_inc(s_nw, 1)
                    nw[0] += 1
                    dve.wait_ge(s_nw, nw[0])

            def stats(u):
                if u % 2 == 0:
                    dve.wait_ge(s_x[u // 2], 16)
                for j in range(2):
                    nc.vector.bn_stats(stat6[:, u % 2, j], res[:, 2 * u + j]).then_inc(s_st, 1)
                for j in range(2):
                    dve.wait_ge(s_st, 2 * u + j + 1)
                    nc.vector.bn_aggr(mv[:, u % 2, j], stat6[:, u % 2, j]).then_inc(s_mv, 1)
                dve.wait_ge(s_mv, 2 * (u + 1))
                nc.vector.tensor_scalar(var[:, u % 2], mv[:, u % 2, :, 1], EPS, None, ALU.add).then_inc(s_var, 1)

            def normalise(u):
                dve.wait_ge(s_y0, u + 1)
                newton(var[:, u % 2], y0[:, u % 2], ya[:, :], yb[:, :], rs[:, :])
                for j in range(2):
                    nc.vector.tensor_scalar(xn[:, 2 * u + j], res[:, 2 * u + j], mv[:, u % 2, j, 0:1],
                                            rs[:, j:j + 1], ALU.subtract, ALU.mult).then_inc(s_xn, 1)

            def low_parts(u):
                dve.wait_ge(s_xth, u + 1)
                if u >= 2:
                    dve.wait_ge(s_pcc, u - 1)
                nc.vector.tensor_tensor(xt_lo[:, u % 2].rearrange("p k t -> p (k t)"), bank[0][:, :],
                                        xt_hi[:, u % 2].rearrange("p k t -> p (k t)"), ALU.subtract).then_inc(s_xtl, 1)

            def masks(u):
                dve.wait_ge(s_bz, u + 1)
                if u >= 2:
                    dve.wait_ge(s_pgp, u - 1)
                nc.vector.tensor_tensor(gmd[:, u % 2].rearrange("p (b t) -> p b t", b=2),
                                        bank[2][:, 2 * P:4 * P].rearrange("p (b t) -> p b t", b=2),
                                        const("upto").unsqueeze(1).to_broadcast([P, 2, P]), ALU.mult).then_inc(s_gmd, 1)
                z = bz[:, u % 4, :, N:N + H]
                nc.vector.scalar_tensor_tensor(out=na[:, :, :], in0=z, scalar=-1.0, in1=z, op0=ALU.mult,
                                               op1=ALU.min).then_inc(s_na, 1)

            def steps(u):
                dve.wait_ge(s_spl, u + 1)
                if u >= 2:
                    dve.wait_ge(s_xdt, u - 1)
                nc.vector.scalar_tensor_tensor(out=dt[:, u % 2], in0=bz[:, u % 4, :, N:N + H], scalar=0.0, in1=sp_l[:, :, :],
                                               op0=ALU.max, op1=ALU.add).then_inc(s_dt, 1)
                dve.wait_ge(s_dt, u + 1)
                dve.wait_ge(s_ea, 1)
                if u >= 2:
                    dve.wait_ge(s_pd, u - 1)
                    dve.wait_ge(s_daq, C * HQ * (u - 1))
                nc.vector.scalar_tensor_tensor(out=da[:, u % 2], in0=dt[:, u % 2], scalar=-1.0,
                                               in1=a_sb[:, :].unsqueeze(1).to_broadcast([P, 2, H]),
                                               op0=ALU.mult, op1=ALU.mult).then_inc(s_da, 1)

            def recur(u):
                g, i = u // 2, u % 2
                dve.wait_ge(s_ps, u + 1)
                dve.wait_ge(s_dec, 3 * u + 3)
                for c in range(C):
                    if (g, c) == (GROUPS - 1, C - 1):
                        continue
                    dve.wait_ge(s_ra, adds(u) + c)
                    nc.vector.tensor_tensor(by_head(tmp_s[:, :]), by_head(state[:, g, i, c]),
                                            dch[:, u % 4, c].unsqueeze(2).to_broadcast([P, H, HD]), ALU.mult).then_inc(s_rm, 1)
                    dve.wait_ge(s_rm, adds(u) + c)
                    nxt = (g, c + 1) if c + 1 < C else (g + 1, 0)
                    nc.vector.tensor_tensor(state[:, nxt[0], i, nxt[1]], tmp_s[:, :],
                                            bank[4 + 2 * i + c // 2][:, D * (c % 2):D * (c % 2) + D],
                                            ALU.add).then_inc(s_ra, 1)

            def weigh(q):
                dve.wait_ge(s_ex, 2 * (q + 1))
                if q >= 2:
                    dve.wait_ge(s_yd, q - 1)
                dve.wait_ge(s_gp, q // 2 + 1)
                g4 = gp[:, q].rearrange("p (c l) -> p c l", c=C)
                nc.vector.tensor_tensor(mm[:, q % 2].rearrange("p (c a) l -> p c a l", c=C),
                                        ex[:, q % 2].rearrange("p (c a) l -> p c a l", c=C),
                                        g4.unsqueeze(2).to_broadcast([P, C, HG, L]), ALU.mult).then_inc(s_mm, 1)

            def combine(q):
                pb = bank[2 + q % 2]
                dve.wait_ge(s_yd, q + 1)
                nc.vector.tensor_tensor(by_head(t1[:, :]), by_head(pb[:, D:2 * D]),
                                        ecs[:, q].unsqueeze(2).to_broadcast([P, H, HD]), ALU.mult).then_inc(s_t1, 1)
                dve.wait_ge(s_t1, q + 1)
                if q >= 2:
                    dve.wait_ge(s_yt, q - 1)
                nc.vector.tensor_tensor(yy[:, q % 2], t1[:, :], pb[:, 0:D], ALU.add).then_inc(s_y, 1)

            def other_weights():
                dve.wait_ge(s_whi, 2)
                nc.vector.tensor_tensor(w2_lo[:, :, :], w2_raw[:, :, :], w2_hi[:, :, :], ALU.subtract).then_inc(s_wlo, 1)

            def low_increments(q):
                if q >= 2:
                    dve.wait_ge(s_e, q - 1)
                dve.wait_ge(s_dql, q // 2 + 1)
                dve.wait_ge(s_c, 16)
                masked(nc.vector, rr_lo, daq_lo, q).then_inc(s_rl, 1)

            def y_low(q):
                dve.wait_ge(s_yth, q + 1)
                if q >= 2:
                    dve.wait_ge(s_po, q - 1)
                nc.vector.tensor_tensor(yt_lo[:, q % 2], bank[4][:, 0:D], yt_hi[:, q % 2], ALU.subtract).then_inc(s_ytl, 1)

            def residual(q):
                dve.wait_ge(s_po, q + 1)
                dve.wait_ge(s_xob, q // 2 + 1)
                nc.vector.tensor_tensor(res[:, q], bank[5][:, 0:D], res[:, q], ALU.add).then_inc(s_x1, 1)
                dve.wait_ge(s_x1, q + 1)
                nc.vector.bn_stats(stat6b[:, :], res[:, q]).then_inc(s_st2, 1)
                dve.wait_ge(s_st2, q + 1)
                nc.vector.bn_aggr(mvb[:, :], stat6b[:, :]).then_inc(s_mv2, 1)
                dve.wait_ge(s_mv2, q + 1)
                nc.vector.tensor_scalar(varb[:, :], mvb[:, 1:2], EPS, None, ALU.add).then_inc(s_var2, 1)

            def normalise2(q):
                dve.wait_ge(s_y02, q + 1)
                newton(varb[:, :], y0b[:, :], yab[:, :], ybb[:, :], rsb[:, :])
                if q >= 2:
                    dve.wait_ge(s_x2d[q % 2], 16 * (q // 2))
                    dve.wait_ge(s_x2t, q - 1)
                nc.vector.tensor_scalar(xn2[:, q % 2], res[:, q], mvb[:, 0:1], rsb[:, 0:1], ALU.subtract,
                                        ALU.mult).then_inc(s_xn2, 1)

            nr = [0]

            def r_(ins):
                ins.then_inc(s_r, 1)
                nr[0] += 1
                dve.wait_ge(s_r, nr[0])

            def wide(ap, n):
                return ap.unsqueeze(2).to_broadcast([P, ap.shape[1], n])

            def shifted(g):
                dve.wait_ge(s_lgt, BATCH * (g + 1))
                r_(nc.vector.tensor_reduce(mx[:, :], lg[:, g % 2, :, 0:E], AX.X, ALU.max))
                nc.vector.tensor_tensor(shl[:, :, :], lg[:, g % 2, :, 0:E], wide(mx[:, :], E), ALU.subtract).then_inc(s_shl, 1)

            def choose(g):
                qs = slice(g * BATCH, (g + 1) * BATCH)
                dve.wait_ge(s_gex, 2 * (g + 1))
                r_(nc.vector.tensor_reduce(sm[:, :], pe_[:, :, :], AX.X, ALU.add))
                r_(nc.vector.reciprocal(rc[:, :], sm[:, :]))
                r_(nc.vector.tensor_tensor(prob[:, :, :], pe_[:, :, :], wide(rc[:, :], E), ALU.mult))
                for b in range(BATCH):
                    last = nc.vector.max(m8[:, b, :], prob[:, b, :])
                r_(last)
                for b in range(BATCH):
                    last = nc.vector.max_index(i8[:, b, :], m8[:, b, :], prob[:, b, :])
                nc.vector.tensor_scalar(sgy[:, :], sgx[:, :], 1.0, None, ALU.add).then_inc(s_gate, 1)
                r_(nc.vector.tensor_reduce(sw[:, :], m8[:, :, 0:TOPK], AX.X, ALU.add))
                dve.wait_ge(s_gate, g + 1)
                nc.vector.reciprocal(sig[:, qs], sgy[:, :])
                r_(nc.vector.reciprocal(rw[:, :], sw[:, :]))
                nc.vector.tensor_tensor(wgt[:, qs, :], m8[:, :, 0:TOPK], wide(rw[:, :], TOPK), ALU.mult)
                r_(nc.vector.tensor_copy(idf[:, qs, :], i8[:, :, 0:TOPK]))

            def s_xlow(k):
                dve.wait_ge(s_stxh, k + 1)
                if not isinstance(k, int) or k >= 1:
                    dve.wait_ge(s_sgu, 4 * k)
                nc.vector.tensor_tensor(tx_lo[:, :], bank[0][:, 0:D], tx_hi[:, :], ALU.subtract).then_inc(s_stxl, 1)

            for step in range(STEPS):
                for k, stage in ((3, low_parts), (7, steps), (6, masks), (10, recur), (1, normalise), (0, stats)):
                    if 0 <= step - k < PAIRS:
                        stage(step - k)
                m = step - MSTART
                for k, stage in ((5, residual), (1, weigh), (5, normalise2), (2, combine), (3, y_low)):
                    if 0 <= m - k < NT:
                        stage(m - k)
                if 0 <= m + 1 < EARLY:
                    low_increments(m + 1)
                if m == 0:
                    other_weights()
                if m > ROUTE and (m - ROUTE) % BATCH == 1:
                    choose((m - ROUTE) // BATCH)
                if m >= ROUTE and (m - ROUTE) % BATCH == 0:
                    shifted((m - ROUTE) // BATCH)
                if m == NT + 5:
                    s_xlow(0)

            def s_gated(k):
                for c in range(2):
                    dve.wait_ge(s_ssi, 2 * k + c + 1)
                    dve.wait_ge(s_sgu, 4 * k + c + 3)
                    if not isinstance(k, int) or k >= 1:
                        dve.wait_ge(s_sth, k)
                    nc.vector.tensor_tensor(act_h[:, c * 352:(c + 1) * 352], act_s[:, c * 352:(c + 1) * 352],
                                            bank[3 + c][:, 0:352], ALU.mult).then_inc(s_sh, 1)

            for i in range(2):
                dve.wait_ge(s_x2d[i], 16 * NT // 2)
            dve.wait_ge(s_lg, NT)
            dve.wait_ge(s_rc, 16)
            r_(nc.vector.tensor_tensor(oh[:, :, :, :].rearrange("p q j e -> p (q j) e"),
                                       wide(idf[:, :, :].rearrange("p q j -> p (q j)"), E),
                                       rconst("iota_e").unsqueeze(1).to_broadcast([P, NT * TOPK, E]), ALU.is_equal))
            nc.vector.tensor_reduce(msk[:, :, :].rearrange("p e q -> p q e"), oh[:, :, :, :].rearrange("p q j e -> p q e j"),
                                    AX.X, ALU.add).then_inc(s_msk, 1)
            nc.vector.memset(act_h[:, SI:6 * P], 0.0).then_inc(s_pad, 1)
            s_gated(0)
            s_xlow(1)
            dve.wait_ge(s_cnt, 1)
            rank, tot = bank[7][:, 0:E * NT], bank[7][:, E * NT:2 * E * NT]
            flat = lambda t: t[:, :, :].rearrange("p e q -> p (e q)")
            r_(nc.vector.tensor_tensor_scan(flat(inc), rconst("keep"), tot, 0.0, ALU.mult, ALU.add))
            r_(nc.vector.tensor_tensor(flat(exc), flat(inc), tot, ALU.subtract))
            r_(nc.vector.tensor_tensor(gt[:, :, :], inc[:, :, NT - 1].unsqueeze(2).to_broadcast([P, E, NT]),
                                       rconst("edges").unsqueeze(1).to_broadcast([P, E, NT]), ALU.is_gt))
            r_(nc.vector.tensor_reduce(tl[:, :], gt[:, :, :], AX.X, ALU.add))
            r_(nc.vector.tensor_tensor_scan(incl[:, :], rconst("ones")[:, 0:E], tl[:, :], 0.0, ALU.mult, ALU.add))
            r_(nc.vector.tensor_tensor(base[:, :], incl[:, :], tl[:, :], ALU.subtract))
            r_(nc.vector.tensor_tensor(flat(sl), flat(exc), rank, ALU.add))
            r_(nc.vector.scalar_tensor_tensor(out=sl2[:, :, :], in0=wide(base[:, :], NT), scalar=float(P), in1=sl[:, :, :],
                                              op0=ALU.mult, op1=ALU.add))
            r_(nc.vector.tensor_tensor(so[:, :, :, :], oh[:, :, :, :],
                                       sl2[:, :, :].rearrange("p e q -> p q e").unsqueeze(2).to_broadcast([P, NT, TOPK, E]), ALU.mult))
            r_(nc.vector.tensor_reduce(slf[:, :], so[:, :, :, :].rearrange("p q j e -> p (q j) e"), AX.X, ALU.add))
            r_(nc.vector.tensor_copy(si[:, :], slf[:, :]))
            r_(nc.vector.tensor_scalar(s_hi7[:, :], si[:, :], 7, None, ALU.logical_shift_right))
            r_(nc.vector.tensor_scalar(s_lo7[:, :], si[:, :], P - 1, None, ALU.bitwise_and))
            nc.vector.scalar_tensor_tensor(out=slot_i[:, :], in0=s_lo7[:, :], scalar=float(XT), in1=s_hi7[:, :],
                                           op0=ALU.mult, op1=ALU.add).then_inc(s_idx, 1)

            def split_low(slot, n, par):
                dve.wait_ge(s_uh, n + 1)
                nc.vector.tensor_tensor(wu[:, slot, 1, :], stage_w[:, par, :], wu[:, slot, 0, :], ALU.subtract).then_inc(s_ul, 1)

            def s_tlow(k):
                dve.wait_ge(s_sthh, 2 * k + 2)
                if not isinstance(k, int) or k >= 1:
                    dve.wait_ge(s_sdn, k)
                nc.vector.tensor_tensor(th_lo[:, 0:4, :].rearrange("p c t -> p (c t)"), bank[5][:, :],
                                        th_hi[:, 0:4, :].rearrange("p c t -> p (c t)"), ALU.subtract).then_inc(s_sthl, 1)
                nc.vector.tensor_tensor(th_lo[:, 4:6, :].rearrange("p c t -> p (c t)"), bank[6][:, 0:2 * P],
                                        th_hi[:, 4:6, :].rearrange("p c t -> p (c t)"), ALU.subtract).then_inc(s_sthl, 1)

            def s_add(k):
                dve.wait_ge(s_sdn, k + 1)
                nc.vector.scalar_tensor_tensor(out=res[:, k, :], in0=bank[7][:, 0:D], scalar=sig[:, bass.ds(k, 1)],
                                               in1=res[:, k, :], op0=ALU.mult, op1=ALU.add).then_inc(s_sacc, 1)

            def s_step(i, j):
                k = 2 * i + j + 1
                s_tlow(k - 1)
                s_gated(k)
                s_xlow(k + 1)
                s_add(k - 1)
                split_low(k + 3, k - 1, j)

            for j in range(2):
                s_step(0, j)
            with dve.Fori(1, (E - SH) // 2) as i:
                for j in range(2):
                    s_step(i, j)
            for k in range(E - SH + 1, NT):
                s_tlow(k - 1)
                s_gated(k)
                if k + 1 < NT:
                    s_xlow(k + 1)
                s_add(k - 1)
            def last_low(i):
                place, cols, src, _, _ = LAST[i]
                dve.wait_ge(s_uh, E - SH + 1 + i)
                nc.vector.tensor_tensor(wu[:, place, 1, cols], src, wu[:, place, 0, cols], ALU.subtract).then_inc(s_ul, 1)

            dve.wait_ge(s_tab, 16)
            nc.vector.tensor_scalar(tok[:, :], tab[:, :], 2, T - 1, ALU.logical_shift_right, ALU.bitwise_and).then_inc(s_tok, 1)
            last_low(0)
            s_tlow(NT - 1)
            for i in range(1, 5):
                last_low(i)
            s_add(NT - 1)

            def e_tlow(k, par):
                dve.wait_ge(s_ethh, k + 1)
                if not isinstance(k, int) or k >= 2:
                    dve.wait_ge(s_edn, k - 1)
                nc.vector.tensor_tensor(et_lo[par].rearrange("p c t -> p (c t)"), bank[5][0:EK, 0:2 * P],
                                        et_hi[par].rearrange("p c t -> p (c t)"), ALU.subtract).then_inc(s_ethl, 1)

            def e_gated(k, par):
                dve.wait_ge(s_esi, k + 1)
                if not isinstance(k, int) or k >= 2:
                    dve.wait_ge(s_eth, k - 1)
                nc.vector.tensor_tensor(act_h[:, par * EI:(par + 1) * EI], act_s[:, 0:EI], bank[1 + par][:, EI:2 * EI], ALU.mult).then_inc(s_eh, 1)

            def e_xlow(k, par):
                dve.wait_ge(s_etxh, k + 1)
                if not isinstance(k, int) or k >= 2:
                    dve.wait_ge(s_egu, k - 1)
                nc.vector.tensor_tensor(xt2_lo[par], bank[0][:, 0:D], xt2_hi[par], ALU.subtract).then_inc(s_etxl, 1)

            e_xlow(0, 0)
            for i in range(5, 8):
                last_low(i)
            e_xlow(1, 1)
            e_gated(0, 0)
            e_xlow(2, 0)

            def e_step(k, n, j):
                e_gated(k, j % 2)
                if not isinstance(k, int) or k + 2 < XT:
                    e_xlow(k + 2, j % 2)
                e_tlow(k - 1, (j - 1) % 2)

            expert_tiles(dve, e_step)
            e_tlow(XT - 1, (XT - 1) % 2)

            dve.wait_ge(s_sacc, NT)
            summed = {}

            def join(q, j):
                dve.wait_ge(s_yl[q], 16) if j == 0 else dve.wait_ge(s_r, summed[q])
                ins = nc.vector.scalar_tensor_tensor(out=res[:, q, :], in0=yl[:, q, j * D:(j + 1) * D],
                                                     scalar=wgt[:, q, j:j + 1], in1=res[:, q, :],
                                                     op0=ALU.mult, op1=ALU.add)
                if j == TOPK - 1:
                    ins.then_inc(s_fin, 1)
                else:
                    ins.then_inc(s_r, 1)
                    nr[0] += 1
                    summed[q] = nr[0]

            for q in range(NT + 1):
                for j in range(TOPK // 2):
                    if q >= 1:
                        join(q - 1, TOPK // 2 + j)
                    if q < NT:
                        join(q, j)

        @block.tensor
        def _(pe):
            pe.wait_ge(s_c, 16)
            ident = const("ident")

            def transposes(u):
                if u:
                    pe.wait_ge(s_xtl, u)
                for j in range(2):
                    pe.wait_ge(s_xn, 2 * u + j + 1)
                    for k in range(K2):
                        last = nc.tensor.transpose(bank[0][:, (2 * k + j) * P:(2 * k + j + 1) * P],
                                                   xn[:, 2 * u + j, k * P:(k + 1) * P], ident)
                last.then_inc(s_xt, 1)

            def project(u):
                pe.wait_ge(s_wlo, 1)
                pe.wait_ge(s_xtl, u + 1)
                if u:
                    pe.wait_ge(s_bdf, u)
                    pe.wait_ge(s_ct, u)
                xs = [(xt_hi[:, u % 2, k], xt_lo[:, u % 2, k]) for k in range(K2)]
                split3(bank[1][0:N + H, 0:2 * P], [((wcol(w1_hi, "bd", k), wcol(w1_lo, "bd", k)), xs[k]) for k in range(K2)])
                split3(bank[1][:, 2 * P:4 * P], [((wcol(w1_hi, "cc", k), wcol(w1_lo, "cc", k)), xs[k])
                                                 for k in range(K2)]).then_inc(s_pcc, 1)

            def chunk_products(u):
                pe.wait_ge(s_bdf, u + 1)
                pe.wait_ge(s_ct, u + 1)
                if u:
                    pe.wait_ge(s_bz, u)
                    pe.wait_ge(s_gmd, u)
                for j in range(2):
                    nc.tensor.transpose(bank[2][:, j * (N + H):(j + 1) * (N + H)], bdf[:, u % 2, j * P:(j + 1) * P],
                                        const("ident")[0:N + H, 0:N + H])
                for j in range(2):
                    last = nc.tensor.matmul(bank[2][:, (2 + j) * P:(3 + j) * P], bdf[0:N, u % 2, j * P:(j + 1) * P],
                                            ct[0:N, 2 * u + j, :], start=True, stop=True)
                last.then_inc(s_pg, 1)

            def sums(u):
                pe.wait_ge(s_gmd, u + 1)
                if u:
                    pe.wait_ge(s_dec, 3 * u)
                    pe.wait_ge(s_gp, u)
                nc.tensor.matmul(bank[3][:, 2 * P:4 * P], const("spread"), gmd[:, u % 2], start=True, stop=True).then_inc(s_pgp, 1)
                pe.wait_ge(s_da, u + 1)
                d2 = da[:, u % 2].rearrange("p b h -> p (b h)")
                nc.tensor.matmul(bank[3][:, 0:2 * H], const("after"), d2, start=True, stop=True)
                nc.tensor.matmul(bank[3][:, 2 * H:4 * H], const("upto"), d2, start=True, stop=True)
                for c in range(C):
                    for j in range(2):
                        col = (4 + c) * H
                        last = nc.tensor.matmul(bank[3][N * j:N * j + N, col:col + H],
                                                const("chunk")[:, c * N:(c + 1) * N], da[:, u % 2, j, :],
                                                start=True, stop=True)
                last.then_inc(s_pd, 1)

            def states(u):
                pe.wait_ge(s_xd, u + 1)
                pe.wait_ge(s_bm, u + 2)
                if u >= 2:
                    pe.wait_ge(s_ra, adds(u - 1))
                for c in range(C):
                    if u >= PAIRS - 2 and c == C - 1:
                        continue
                    for j in range(2):
                        last = nc.tensor.matmul(bank[4 + 2 * (u % 2) + c // 2][N * j:N * j + N, D * (c % 2):D * (c % 2) + D],
                                                bm[:, u % 2, j, c, :], xd[:, u % 2, j, :], start=True, stop=True)
                last.then_inc(s_ps, 1)

            def exponents(q):
                pe.wait_ge(s_rr, q + 1)
                if q < EARLY:
                    pe.wait_ge(s_rl, q + 1)
                pe.wait_ge(s_aft, 1)
                if q >= 1:
                    pe.wait_ge(s_ex, 2 * q)
                else:
                    pe.wait_ge(s_ct, PAIRS)
                for i in range(2):
                    for part in (rr_lo, rr_hi):
                        last = nc.tensor.matmul(bank[i][:, :], after_r[:, :],
                                                part[:, q % 2, 16 * i:16 * i + 16, :].rearrange("p a l -> p (a l)"),
                                                start=(part is rr_lo), stop=(part is rr_hi))
                last.then_inc(s_e, 1)

            def outputs(q):
                g, i, j = q // BATCH, q % BATCH // 2, q % 2
                pb = bank[2 + q % 2]
                if q >= 2:
                    pe.wait_ge(s_y, q - 1)
                elif q == 0:
                    pe.wait_ge(s_gmd, PAIRS)
                    pe.wait_ge(s_bz, PAIRS)
                else:
                    pe.wait_ge(s_dec, 3 * PAIRS)
                    pe.wait_ge(s_gp, PAIRS)
                pe.wait_ge(s_ra, adds(q // 2 + 1))
                for c in range(C):
                    nc.tensor.matmul(pb[L * c:L * c + L, D:2 * D], ct[N * j:N * j + N, q, L * c:L * c + L],
                                     state[N * j:N * j + N, g, i, c, :], start=True, stop=True)
                pe.wait_ge(s_xnd, q // 2 + 1)
                nc.tensor.matmul(pb[:, 0:D], ident, xn[:, q], start=True, stop=False)
                pe.wait_ge(s_mm, q + 1)
                pe.wait_ge(s_xb[q % 2], 16 * HQ * (q // 2 + 1))
                for a in range(HG):
                    for c in range(C):
                        o = pb[L * c:L * c + L, 0:D].rearrange("p (a g e) -> p g a e", g=HG, e=HD)[:, a]
                        r = xb[:, q % 2, c].rearrange("p (a g e) -> p g a e", g=HG, e=HD)[:, a]
                        last = nc.tensor.matmul(o, mm[:, q % 2, c * HG + a, :], r, start=False, stop=(a == HG - 1))
                last.then_inc(s_yd, 1)

            def turn_y(q):
                pe.wait_ge(s_y, q + 1)
                if q:
                    pe.wait_ge(s_ytl, q)
                else:
                    pe.wait_ge(s_ra, adds(PAIRS - 1))
                for k in range(K2):
                    last = nc.tensor.transpose(bank[4][:, k * P:(k + 1) * P], yy[:, q % 2, k * P:(k + 1) * P], ident)
                last.then_inc(s_yt, 1)

            def project_out(q):
                pe.wait_ge(s_wlo, 2)
                pe.wait_ge(s_ytl, q + 1)
                if q:
                    pe.wait_ge(s_x1, q)
                split3(bank[5][:, 0:D], [((yt_hi[:, q % 2, k * P:(k + 1) * P], yt_lo[:, q % 2, k * P:(k + 1) * P]),
                                         (wcol(w2_hi, "wo", k), wcol(w2_lo, "wo", k))) for k in range(K2)]).then_inc(s_po, 1)

            def turn_x2(q):
                pe.wait_ge(s_xn2, q + 1)
                if not q:
                    pe.wait_ge(s_ra, adds(PAIRS))
                if q:
                    pe.wait_ge(s_x2c, q)
                for k in range(K2):
                    last = nc.tensor.transpose(bank[6][:, k * P:(k + 1) * P], xn2[:, q % 2, k * P:(k + 1) * P], ident)
                last.then_inc(s_x2t, 1)

            def logits(q):
                pe.wait_ge(s_x2c, q + 1)
                if q:
                    pe.wait_ge(s_lgt, q)
                for k in range(K2):
                    last = nc.tensor.matmul(bank[7][:, 0:32], x2t[:, k * P:(k + 1) * P], wcol(w2_raw, "wg", k),
                                            start=(k == 0), stop=(k == K2 - 1))
                last.then_inc(s_lg, 1)

            xs = [(tx_hi[:, k * P:(k + 1) * P], tx_lo[:, k * P:(k + 1) * P]) for k in range(K2)]

            def s_turn_x(k, par, uses):
                pe.wait_ge(s_sx[par], 16 * uses)
                if isinstance(k, int) and k == 0:
                    pe.wait_ge(s_ex, 2 * NT)
                else:
                    pe.wait_ge(s_stxl, k)
                for c in range(K2):
                    last = nc.tensor.transpose(bank[0][:, c * P:(c + 1) * P], xg[:, par, c * P:(c + 1) * P], ident)
                last.then_inc(s_stx, 1)

            for step in range(STEPS):
                for k, stage in ((4, project), (2, transposes), (5, chunk_products), (7, sums), (9, states)):
                    if 0 <= step - k < PAIRS:
                        stage(step - k)
                m = step - MSTART
                for k, stage in ((0, exponents), (2, outputs), (3, turn_y), (4, project_out), (7, logits), (6, turn_x2)):
                    if 0 <= m - k < NT:
                        stage(m - k)
                if m == NT + 5:
                    s_turn_x(0, 0, 1)

            def s_up(k):
                pe.wait_ge(s_stxl, k + 1)
                for c in range(4):
                    if isinstance(k, int) and k == 0:
                        pe.wait_ge(s_rawl, c + 1)
                    elif c % 2 == 0:
                        pe.wait_ge(s_sh, 2 * k)
                    split3(bank[1 + c][:, 0:2 * EI],
                           [(xs[b], up(c, b)) for b in range(K2)]).then_inc(s_sgu, 1)

            def s_turn_h(k):
                pe.wait_ge(s_sh, 2 * k + 2)
                if isinstance(k, int) and k == 0:
                    pe.wait_ge(s_pad, 1)
                else:
                    pe.wait_ge(s_sthl, 2 * k)
                for c in range(6):
                    last = nc.tensor.transpose(bank[5 + c // 4][:, c % 4 * P:(c % 4 + 1) * P], act_h[:, c * P:(c + 1) * P], ident)
                last.then_inc(s_sth, 1)

            def s_down(k):
                pe.wait_ge(s_sthl, 2 * k + 2)
                if isinstance(k, int) and k == 0:
                    pe.wait_ge(s_idx, 1)
                else:
                    pe.wait_ge(s_sacc, k)
                split3(bank[7][:, 0:D], [((th_hi[:, c, :], th_lo[:, c, :]),
                                         down(c // 2, c % 2))
                                         for c in range(6)]).then_inc(s_sdn, 1)

            s_up(0)
            s_turn_x(1, 1, 1)
            pe.wait_ge(s_msk, 1)
            m = msk[:, :, :].rearrange("p e q -> p (e q)")
            nc.tensor.matmul(bank[7][:, 0:E * NT], rconst("before"), m, start=True, stop=True)
            nc.tensor.matmul(bank[7][:, E * NT:2 * E * NT], rconst("ones"), m, start=True, stop=True).then_inc(s_cnt, 1)

            def s_step(k, n, j):
                s_turn_h(k - 1)
                s_up(k)
                if not isinstance(k, int) or k + 1 < NT:
                    s_turn_x(k + 1, (j + 1) % 2, n + (j + 1) // 2 + 1)
                s_down(k - 1)

            for k in (1, 2):
                s_step(k, k // 2, k % 2)
            with pe.Fori(1, (NT - 1) // 2) as i:
                for j in (1, 2):
                    s_step(2 * i + j, i + j // 2, j % 2)
            s_step(NT - 1, (NT - 1) // 2, (NT - 1) % 2)
            s_turn_h(NT - 1)
            s_down(NT - 1)

            packed = pe.alloc_register("packed")

            def read_experts(i):
                pe.reg_load(packed, epack[0:1, bass.ds(i, 1)] if not isinstance(i, int) else epack[0:1, i:i + 1])

            def experts():
                w = pe.snap(packed)
                return [w // E ** j % E for j in range(XG + 2)]

            def e_turn_x(k, slot, uses):
                pe.wait_ge(s_xg[slot], 16 * uses)
                if not isinstance(k, int) or k >= 1:
                    pe.wait_ge(s_etxl, k)
                for c in range(K2):
                    last = nc.tensor.transpose(bank[0][:, c * P:(c + 1) * P], xg[:, slot, c * P:(c + 1) * P], ident)
                last.then_inc(s_etx, 1)

            def e_up(k, par, e):
                pe.wait_ge(s_etxl, k + 1)
                if not isinstance(k, int) or k >= 2:
                    pe.wait_ge(s_eh, k - 1)
                split3(bank[1 + par][:, 0:2 * EI],
                       [((xt2_hi[par][:, b * P:(b + 1) * P], xt2_lo[par][:, b * P:(b + 1) * P]), up(e, b))
                        for b in range(K2)]).then_inc(s_egu, 1)

            def e_turn_h(k, par):
                pe.wait_ge(s_eh, k + 1)
                if not isinstance(k, int) or k >= 1:
                    pe.wait_ge(s_ethl, k)
                for c in range(2):
                    last = nc.tensor.transpose(bank[5][0:EK, c * P:(c + 1) * P], act_h[:, (2 * par + c) * EK:(2 * par + c + 1) * EK], ident)
                last.then_inc(s_eth, 1)

            def e_down(k, par, e):
                pe.wait_ge(s_ethl, k + 1)
                if not isinstance(k, int) or k >= 1:
                    pe.wait_ge(s_ey, k)
                split3(bank[7][:, 0:D], [((et_hi[par][:, c, :], et_lo[par][:, c, :]),
                                         down(e, c, EK))
                                         for c in range(2)]).then_inc(s_edn, 1)

            pe.wait_ge(s_routed, 1)
            e_turn_x(0, 0, 1)
            e_turn_x(1, 1, 1)
            pe.wait_ge(s_ul, E - SH + 5)
            read_experts(0)

            def e_step(k, n, j, ahead, e):
                e_up(k, j % 2, e[j])
                if not isinstance(k, int) or k + 2 < XT:
                    e_turn_x(k + 2, (j + 2) % XG, n + (j + 2) // XG + 1)
                if not isinstance(k, int) or k >= 1:
                    e_turn_h(k - 1, (j - 1) % 2)
                if not isinstance(k, int) or k >= 2:
                    e_down(k - 2, j % 2, e[j - 2])
                if ahead and j == XG:
                    read_experts(n + 1)

            rounds = (XT - 2) // XG
            e = experts()
            for j in range(2):
                e_step(j, 0, j, False, e)
            pe.wait_ge(s_sacc, NT)
            pe.wait_ge(s_ul, E - SH + 8)
            for j in range(2, XG + 2):
                e_step(j, 0, j, True, e)
            with pe.Fori(1, rounds) as i:
                e = experts()
                for j in range(2, XG + 2):
                    e_step(i * XG + j, i, j, True, e)
            e = experts()
            left = XT - rounds * XG
            for j in range(2, left):
                e_step(rounds * XG + j, rounds, j, False, e)
            e_turn_h(XT - 1, (XT - 1) % 2)
            for j in (left - 2, left - 1):
                e_down(rounds * XG + j, j % 2, e[j])


def kernel(**inputs):
    import concourse.bacc as _bacc
    from concourse.bass_utils import run_bass_kernel_spmd as _run

    nc = _bacc.Bacc("TRN2", target_bir_lowering=False, num_devices=1)
    arrays, args = {}, {}
    for name, a in layout(inputs).items():
        a = np.ascontiguousarray(a)
        arrays[f"in_{name}"] = a
        args[name] = nc.dram_tensor(f"in_{name}", a.shape, mybir.dt.from_np(a.dtype), kind="ExternalInput").ap()
    out = nc.dram_tensor("out_0", (BATCH, SEQ, D), F32, kind="ExternalOutput").ap()
    build(nc, out=out, **args)
    r = _run(nc, [arrays], core_ids=[0])
    return r.results[0]["out_0"]


def layout(inputs):
    g = {k: np.asarray(v) for k, v in inputs.items()}

    def blocks(w):
        return w.T.reshape(w.shape[1] // P, P, w.shape[0]).transpose(1, 0, 2)

    cw = g["L0_attn_C_w"]
    router = np.concatenate([g["L0_ffn_gate_w"], g["L0_ffn_shared_gate_vec"], np.zeros((32 - ER, D), np.float32)])
    small = np.concatenate([g["L0_attn_B_w"], g["L0_attn_dt_w"], cw, cw, g["L0_attn_out_w"], router])
    bias = np.zeros((P, 2), np.float32)
    bias[:N, 0] = g["L0_attn_B_b"]
    bias[N:N + H, 0] = g["L0_attn_dt_b"]
    bias[:N, 1] = bias[N:, 1] = g["L0_attn_C_b"]
    units = np.zeros((4 + E, P, WC), np.float32)
    units[:4, :, :WU] = (g["L0_ffn_shared_gate_up"].reshape(4, 2 * EI, K2, P).transpose(0, 3, 2, 1)).reshape(4, P, WU)
    shared_down = np.zeros((6 * P, D), np.float32)
    shared_down[:SI] = g["L0_ffn_shared_down"].T
    units[:3, :, WU:] = shared_down.reshape(3, 2, P, D).transpose(0, 2, 1, 3).reshape(3, P, WD)
    units[4:, :, :WU] = g["L0_ffn_expert_gate_up"].reshape(E, 2 * EI, K2, P).transpose(0, 3, 2, 1).reshape(E, P, WU)
    units[4:, :EK, WU:] = g["L0_ffn_expert_down"].reshape(E, D, 2, EK).transpose(0, 3, 2, 1).reshape(E, EK, WD)
    units[SH:] = np.roll(units[SH:], -SH, axis=0)
    cst, rcst = constants()
    return {
        "x": g["L0_attn_x"], "w_small": blocks(small), "w_bias": bias,
        "a_log": g["L0_attn_A_log"].reshape(1, H), "d_row": g["L0_attn_D"].reshape(1, H),
        "ob_row": g["L0_attn_out_b"].reshape(1, D), "cst_in": cst,
        "rcst_in": rcst, "w_units": units,
    }
```

```python
from contextlib import ExitStack

import numpy as np

import concourse.bass as bass
from concourse import mybir

ALU = mybir.AluOpType
ACT = mybir.ActivationFunctionType
AX = mybir.AxisListType
F32 = mybir.dt.float32
F32R = mybir.dt.float32r
I32 = mybir.dt.int32
U32 = mybir.dt.uint32

P = 128
L = 32
C = P // L
BATCH, SEQ, D = 4, 512, 256
GROUPS = SEQ // P
NT = BATCH * GROUPS
T = NT * P
PAIRS = NT // 2
K2 = D // P
H, HD = 32, 8
HQ, HG = 4, 8
N = 64
E, TOPK, EI, SI = 16, 4, 176, 704
EPS = 1e-5
XT = 80
ROWS = T * TOPK
ER = 17

WU = K2 * 2 * EI
WD = 2 * D
WC = WU + WD
SH = 4
EK = EI // 2
XG = 4

CONSTS = {}
RCONSTS = {}


def constants():
    r = np.arange(P)
    blk, pos = r // L, r % L
    same = blk[:, None] == blk[None, :]
    parts = {
        "ident": np.eye(P),
        "after": same & (pos[:, None] > pos[None, :]),
        "upto": same & (pos[:, None] <= pos[None, :]),
        "spread": pos[:, None] == pos[None, :],
        "tri": pos[:, None] <= np.arange(L)[None, :],
        "chunk": np.repeat(np.arange(C), N)[None, :] == blk[:, None],
    }
    routing = {
        "ones": np.ones((P, P)),
        "before": r[:, None] < r[None, :],
        "iota_e": np.broadcast_to(np.arange(E), (P, E)),
        "edges": np.broadcast_to(np.arange(NT) * P, (P, NT)),
        "keep": np.broadcast_to((np.arange(E * NT) % NT) != 0, (P, E * NT)),
        "tiles": np.broadcast_to(np.arange(XT + XG), (P, XT + XG)),
    }
    arrays = []
    for where, group in ((CONSTS, parts), (RCONSTS, routing)):
        at = 0
        for name, a in group.items():
            where[name] = (at, a.shape[1])
            at += a.shape[1]
        arrays.append(np.concatenate([np.asarray(a, np.float32) for a in group.values()], 1))
    return arrays


constants()
NC = sum(n for _, n in CONSTS.values())
NRC = sum(n for _, n in RCONSTS.values())
WS = {"bd": (0, N + H), "cc": (N + H, 2 * N), "wo": (0, D), "wg": (D, 32)}
NW1, NW2 = N + H + 2 * N, D + 32


def build(nc, x, w_small, w_bias, a_log, d_row, ob_row, cst_in, rcst_in, w_units, out):
    es = ExitStack()
    with es:
        def sem(name):
            return es.enter_context(nc.semaphore(name))

        def sb(name, shape, dt=F32, stack=None):
            return (stack or es).enter_context(nc.sbuf_tensor(name, shape, dt))

        cst = sb("cst", [P, NC])
        res = sb("res", [P, NT, D])
        rcst = sb("rcst", [P, NRC])
        xg = sb("xg", [P, XG, D])
        wgt = sb("wgt", [P, NT, TOPK])
        sig = sb("sig", [P, NT])
        pair = sb("pair", [P, NT * TOPK], I32)
        init = sb("init", [P, XT], I32)
        incl = sb("incl", [P, E])
        ef = sb("ef", [1, 2, XT + XG])
        em = sb("em", [1, XT + XG])
        ep = sb("ep", [1, 2, XT // XG])
        eq = sb("eq", [1, XT // XG])
        slot_i = sb("slot_i", [P, NT * TOPK], I32)
        tab = sb("tab", [P, XT], I32)
        tok = sb("tok", [P, XT], I32)
        epack = sb("epack", [1, XT // XG], I32)
        bank = [es.enter_context(nc.psum_tensor(f"bank{i}", [P, 512], F32)) for i in range(8)]

        def const(name):
            a, n = CONSTS[name]
            return cst[:, a:a + n]

        st = ExitStack()
        w1_raw = sb("w1_raw", [P, K2, NW1], F32, st)
        w1_hi = sb("w1_hi", [P, K2, NW1], F32R, st)
        w1_lo = sb("w1_lo", [P, K2, NW1], F32R, st)
        bias = sb("bias", [P, 2], F32, st)
        a_sb = sb("a_sb", [P, H], F32, st)
        ob_sb = sb("ob_sb", [P, D], F32, st)
        ones_col = sb("ones_col", [P, 1], F32, st)
        stat6 = sb("stat6", [P, 2, 2, 6], F32, st)
        mv = sb("mv", [P, 2, 2, 2], F32, st)
        var = sb("var", [P, 2, 2], F32, st)
        lnv = sb("lnv", [P, 2, 2], F32, st)
        y0 = sb("y0", [P, 2, 2], F32, st)
        ya = sb("ya", [P, 2], F32, st)
        yb = sb("yb", [P, 2], F32, st)
        rs = sb("rs", [P, 2], F32, st)
        xt_hi = sb("xt_hi", [P, 2, K2, 2 * P], F32R, st)
        xt_lo = sb("xt_lo", [P, 2, K2, 2 * P], F32R, st)
        bdf = sb("bdf", [N + H, 2, 2 * P], F32, st)
        bz = sb("bz", [P, 4, 2, N + H], F32, st)
        gmd = sb("gmd", [P, 2, 2 * P], F32, st)
        na = sb("na", [P, 2, H], F32, st)
        sp_e = sb("sp_e", [P, 2, H], F32, st)
        sp_l = sb("sp_l", [P, 2, H], F32, st)
        dt = sb("dt", [P, 2, 2, H], F32, st)
        da = sb("da", [P, 2, 2, H], F32, st)
        daq = sb("daq", [P, 2, 2, C, HG], F32, st)
        dec = sb("dec", [P, 2, 2, H], F32, st)
        dch = sb("dch", [P, 4, C, H], F32, st)
        xdt = sb("xdt", [P, 2, 2, D], F32, st)
        xd = sb("xd", [P, 2, 2, D], F32, st)
        bm = sb("bm", [P, 2, 2, C, N], F32, st)
        tmp_s = sb("tmp_s", [P, D], F32, st)
        state = sb("state", [P, GROUPS, 2, C, D], F32, st)
        lg = sb("lg", [P, 2, BATCH, 32], F32, st)
        mx = sb("mx", [P, BATCH], F32, st)
        shl = sb("shl", [P, BATCH, E], F32, st)
        pe_ = sb("pexp", [P, BATCH, E], F32, st)
        sgx = sb("sgx", [P, BATCH], F32, st)
        sgy = sb("sgy", [P, BATCH], F32, st)
        sm = sb("sm", [P, BATCH], F32, st)
        rc = sb("rc", [P, BATCH], F32, st)
        prob = sb("prob", [P, BATCH, E], F32, st)
        m8 = sb("m8", [P, BATCH, 8], F32, st)
        i8 = sb("i8", [P, BATCH, 8], U32, st)
        sw = sb("sw", [P, BATCH], F32, st)
        rw = sb("rw", [P, BATCH], F32, st)
        idf = sb("idf", [P, NT, TOPK], F32, st)
        xn = sb("xn", [P, NT, D], F32, st)
        ct = sb("ct", [P, NT, P], F32, st)
        gp = sb("gp", [P, NT, P], F32, st)
        d_sb = sb("d_sb", [P, H], F32, st)
        w2 = sb("w2", [P, K2, NW2], F32, st)
        daq_hi = sb("daq_hi", [P, NT, C, HG], F32R, st)
        daq_lo = sb("daq_lo", [P, NT, C, HG], F32R, st)
        ecs = sb("ecs", [P, NT, H], F32, st)
        t1 = sb("t1", [P, D], F32, st)
        yy = sb("yy", [P, 2, D], F32, st)
        yt = sb("yt", [P, 2, D], F32, st)
        stat6b = sb("stat6b", [P, 6], F32, st)
        mvb = sb("mvb", [P, 2], F32, st)
        varb = sb("varb", [P, 1], F32, st)
        lnvb = sb("lnvb", [P, 1], F32, st)
        y0b = sb("y0b", [P, 1], F32, st)
        yab = sb("yab", [P, 1], F32, st)
        ybb = sb("ybb", [P, 1], F32, st)
        rsb = sb("rsb", [P, 1], F32, st)
        xn2 = sb("xn2", [P, 2, D], F32, st)
        x2t = sb("x2t", [P, D], F32, st)
        after_r = sb("after_r", [P, P], F32R, st)
        rr_hi = sb("rr_hi", [P, 2, C * HG, L], F32R, st)
        rr_lo = sb("rr_lo", [P, 2, C * HG, L], F32R, st)
        ex = sb("ex", [P, 2, C * HG, L], F32, st)
        mm = sb("mm", [P, 2, C * HG, L], F32, st)
        xb = sb("xb", [P, 2, C, D], F32, st)
        st.close()

        rw4 = ExitStack()
        sb("under_raw", [P, SH, 2, WC], F32, rw4)
        raw = sb("raw", [P, SH * WC - WD], F32, rw4)
        rw4.close()

        rt = ExitStack()
        sb("under_routing", [P, E - 4, 2, WC], F32, rt)
        oh = sb("oh", [P, NT, TOPK, E], F32, rt)
        msk = sb("msk", [P, E, NT], F32, rt)
        inc = sb("inc", [P, E, NT], F32, rt)
        exc = sb("exc", [P, E, NT], F32, rt)
        gt = sb("gt", [P, E, NT], F32, rt)
        tl = sb("tl", [P, E], F32, rt)
        base = sb("base", [P, E], F32, rt)
        sl = sb("sl", [P, E, NT], F32, rt)
        sl2 = sb("sl2", [P, E, NT], F32, rt)
        so = sb("so", [P, NT, TOPK, E], F32, rt)
        slf = sb("slf", [P, NT * TOPK], F32, rt)
        si = sb("si", [P, NT * TOPK], I32, rt)
        s_hi7 = sb("s_hi7", [P, NT * TOPK], I32, rt)
        s_lo7 = sb("s_lo7", [P, NT * TOPK], I32, rt)
        rt.close()

        fin = ExitStack()
        yl = sb("yl", [P, NT, TOPK * D], F32, fin)
        fin.close()

        pl = ExitStack()
        sb("under_places", [P, 2, 2, WC], F32, pl)
        place23 = sb("place23", [P, 2, 2, WC], F32, pl)
        pl.close()

        wu = sb("wu", [P, E, 2, WC], F32R)
        stage_w = sb("stage_w", [P, 2, WC])
        tx_hi = sb("tx_hi", [P, D], F32R)
        tx_lo = sb("tx_lo", [P, D], F32R)
        act_s = sb("act_s", [P, SI])
        act_h = sb("act_h", [P, 6 * P])
        th_hi = sb("th_hi", [P, 6, P], F32R)
        th_lo = sb("th_lo", [P, 6, P], F32R)
        y_sb = sb("y_sb", [P, 2, D])
        xt2_hi = [tx_hi[:, :], th_hi[:, 2:4, :].rearrange("p c t -> p (c t)")]
        xt2_lo = [tx_lo[:, :], th_lo[:, 2:4, :].rearrange("p c t -> p (c t)")]
        et_hi = [th_hi[0:EK, 4 * h:4 * h + 2, :] for h in range(2)]
        et_lo = [th_lo[0:EK, 4 * h:4 * h + 2, :] for h in range(2)]
        stage_d = y_sb[:, :, :].rearrange("p a d -> p (a d)")

        table_d = nc.dram_tensor("table_dram", (P * XT, 1), I32, kind="Internal").ap()
        y_d = nc.dram_tensor("y_dram", (ROWS + P * XT, D), F32, kind="Internal").ap()
        out_v = out.rearrange("b (g p) d -> g b p d", p=P)

        xdt_d = nc.dram_tensor("xdt_dram", (NT, P, D), F32, kind="Internal").ap()
        xn2_d = nc.dram_tensor("xn2_dram", (T, D), F32, kind="Internal").ap()
        x_v = x.rearrange("b (g p) d -> g p b d", p=P)

        consts_in = sem("consts_in")
        x_in = [sem(f"x_in{g}") for g in range(GROUPS)]
        w1_in = sem("w1_in")
        w2_in = sem("w2_in")
        small_in = sem("small_in")
        w1_hi_made = sem("w1_hi_made")
        w1_lo_made = sem("w1_lo_made")
        zeroed = sem("zeroed")
        a_exp_made = sem("a_exp_made")
        stats_made = sem("stats_made")
        mean_var_made = sem("mean_var_made")
        var_made = sem("var_made")
        ln_var_made = sem("ln_var_made")
        rstd_guessed = sem("rstd_guessed")
        newton_steps = sem("newton_steps")
        x_normalised = sem("x_normalised")
        x_turned = sem("x_turned")
        xt_hi_made = sem("xt_hi_made")
        xt_lo_made = sem("xt_lo_made")
        x_projected = sem("x_projected")
        bdf_made = sem("bdf_made")
        ct_made = sem("ct_made")
        bc_products_made = sem("bc_products_made")
        bz_made = sem("bz_made")
        gmd_made = sem("gmd_made")
        minus_abs_made = sem("minus_abs_made")
        softplus_exp_made = sem("softplus_exp_made")
        softplus_log_made = sem("softplus_log_made")
        dt_made = sem("dt_made")
        da_made = sem("da_made")
        daq_made = sem("daq_made")
        daq_hi_made = sem("daq_hi_made")
        daq_lo_made = sem("daq_lo_made")
        after_made = sem("after_made")
        decay_sums_made = sem("decay_sums_made")
        gp_sums_made = sem("gp_sums_made")
        decays_made = sem("decays_made")
        gp_made = sem("gp_made")
        xdt_made = sem("xdt_made")
        xd_made = sem("xd_made")
        bm_made = sem("bm_made")
        xdt_stored = [sem("xdt_stored0"), sem("xdt_stored1")]
        chunk_states_made = sem("chunk_states_made")
        state_decayed = sem("state_decayed")
        states_ready = sem("states_ready")
        increments_ready = sem("increments_ready")
        low_increments_ready = sem("low_increments_ready")
        exponents_made = sem("exponents_made")
        exp_made = sem("exp_made")
        mm_made = sem("mm_made")
        xb_in = [sem("xb_in0"), sem("xb_in1")]
        skip_made = sem("skip_made")
        bias_added = sem("bias_added")
        scan_made = sem("scan_made")
        t1_made = sem("t1_made")
        y_made = sem("y_made")
        y_turned = sem("y_turned")
        yt_made = sem("yt_made")
        projected_out = sem("projected_out")
        residual_made = sem("residual_made")
        stats2_made = sem("stats2_made")
        mean_var2_made = sem("mean_var2_made")
        var2_made = sem("var2_made")
        ln_var2_made = sem("ln_var2_made")
        rstd2_guessed = sem("rstd2_guessed")
        xn2_made = sem("xn2_made")
        xn2_stored = [sem("xn2_stored0"), sem("xn2_stored1")]
        x2_turned = sem("x2_turned")
        x2t_made = sem("x2t_made")
        logits_made = sem("logits_made")
        logits_copied = sem("logits_copied")
        out_stored = [sem("out_stored0"), sem("out_stored1")]
        logits_shifted = sem("logits_shifted")
        gate_exps_made = sem("gate_exps_made")
        routed_groups = sem("routed_groups")
        rconsts_in = sem("rconsts_in")
        pairs_made = sem("pairs_made")
        table_cleared = sem("table_cleared")
        routing_steps = sem("routing_steps")
        counts_made = sem("counts_made")
        choices_marked = sem("choices_marked")
        places_made = sem("places_made")
        table_written = sem("table_written")
        table_in = sem("table_in")
        tokens_known = sem("tokens_known")
        tile_experts_known = sem("tile_experts_known")
        raw_in = sem("raw_in")
        raw_hi_made = sem("raw_hi_made")
        raw_lo_made = sem("raw_lo_made")
        last_in = [sem(f"last_in{i}") for i in range(4)]
        unit_in = [sem("unit_in0"), sem("unit_in1")]
        unit_hi_made = sem("unit_hi_made")
        unit_lo_made = sem("unit_lo_made")
        rows_in = [sem("rows_in0"), sem("rows_in1")]
        s_x_turned = sem("s_x_turned")
        s_xt_hi_made = sem("s_xt_hi_made")
        s_xt_lo_made = sem("s_xt_lo_made")
        s_up_made = sem("s_up_made")
        s_silu_made = sem("s_silu_made")
        s_gated_made = sem("s_gated_made")
        s_h_turned = sem("s_h_turned")
        s_th_hi_made = sem("s_th_hi_made")
        s_th_lo_made = sem("s_th_lo_made")
        s_down_made = sem("s_down_made")
        s_added = sem("s_added")
        gathered = [sem(f"gathered{i}") for i in range(XG)]
        e_x_turned = sem("e_x_turned")
        e_xt_hi_made = sem("e_xt_hi_made")
        e_xt_lo_made = sem("e_xt_lo_made")
        e_up_made = sem("e_up_made")
        e_silu_made = sem("e_silu_made")
        e_gated_made = sem("e_gated_made")
        e_h_turned = sem("e_h_turned")
        e_th_hi_made = sem("e_th_hi_made")
        e_th_lo_made = sem("e_th_lo_made")
        e_down_made = sem("e_down_made")
        e_y_made = sem("e_y_made")
        scattered = [sem("scattered0"), sem("scattered1")]
        y_in = [sem(f"y_in{q}") for q in range(NT)]
        sum_made = sem("sum_made")
        pad_zeroed = sem("pad_zeroed")
        tile_steps = sem("tile_steps")

        def rconst(name):
            a, n = RCONSTS[name]
            return rcst[:, a:a + n]

        def last_part(place, up_part):
            cols = slice(0, WU) if up_part else slice(WU, WC)
            if place < 2:
                return place, cols, stage_w[:, place, cols], unit_in[place], 16 * (E - SH + 2) // 2
            if place == 2 and not up_part:
                return place, cols, stage_d, last_in[0], 16
            return place, cols, place23[:, place - 2, 1, cols], last_in[place if up_part else 1], 16

        LAST = [last_part(3, False), last_part(0, True), last_part(1, True), last_part(2, True), last_part(3, True),
                last_part(0, False), last_part(1, False), last_part(2, False)]

        def unit_width(u):
            return WC if u < SH - 1 else WU

        def up(slot, k):
            return [wu[:, slot, i, k * 2 * EI:(k + 1) * 2 * EI] for i in range(2)]

        def down(slot, k, rows=P):
            return [wu[0:rows, slot, i, WU + k * D:WU + (k + 1) * D] for i in range(2)]

        def expert_tiles(eng, step):
            rounds = (XT - 2) // XG
            for k in range(1, XG + 2):
                step(k, k // XG, k % XG)
            with eng.Fori(1, rounds) as i:
                for j in range(2, XG + 2):
                    step(i * XG + j, i + j // XG, j % XG)
            for k in range(rounds * XG + 2, XT):
                step(k, k // XG, k % XG)

        def split3(out_ap, pairs):
            n = 3 * len(pairs)
            i = 0
            for (lh, ll), (rh, rl) in pairs:
                for a, b in ((lh, rl), (ll, rh), (lh, rh)):
                    last = nc.tensor.matmul(out_ap, a, b, start=(i == 0), stop=(i == n - 1))
                    i += 1
            return last

        MSTART = 13
        STEPS = MSTART + NT + 10
        ROUTE = 11
        EARLY = 4
        SPLIT = NT - 3

        def adds(u):
            return 1 + C * u - max(0, u - (PAIRS - 2))

        def wcol(w, name, k):
            a, n = WS[name]
            return w[:, k, a:a + n]

        def by_head(ap):
            return ap.rearrange("p (h e) -> p h e", e=HD)

        def shared_rows(eng, k, par):
            eng.dma_start(xg[:, par, :], xn2_d.rearrange("(q p) d -> q p d", p=P)[k]).then_inc(rows_in[par], 16)

        def masked(eng, part, of, q):
            return eng.tensor_tensor(part[:, q % 2], of[:, q].rearrange("p c a -> p (c a)").unsqueeze(2).to_broadcast([P, C * HG, L]),
                                     const("tri").unsqueeze(1).to_broadcast([P, C * HG, L]), ALU.mult)

        block = es.enter_context(nc.Block())

        @block.sync
        def _(sp):
            for g in range(GROUPS):
                sp.dma_start(res[:, g * BATCH:(g + 1) * BATCH, :], x_v[g]).then_inc(x_in[g], 16)
                if g == 0:
                    sp.dma_start(cst[:, :], cst_in).then_inc(consts_in, 16)
            sp.dma_start(rcst[:, :], rcst_in).then_inc(rconsts_in, 16)
            sp.wait_ge(pairs_made, 2)
            sp.dma_start(table_d.rearrange("(p t) o -> p (t o)", t=XT), init[:, :]).then_inc(table_cleared, 16)
            for step in range(-PAIRS, NT + 5):
                u = step + PAIRS
                if u < PAIRS:
                    sp.wait_ge(xdt_made, u + 1)
                    sp.dma_start(xdt_d[2 * u:2 * u + 2].rearrange("b p d -> p b d"),
                                 xdt[:, u % 2]).then_inc(xdt_stored[u % 2], 16)
                q = step
                if 0 <= q < NT:
                    u = q // 2
                    sp.wait_ge(xdt_stored[u % 2], 16 * (u // 2 + 1))
                    if q >= 2:
                        sp.wait_ge(scan_made, q - 1)
                    else:
                        sp.wait_ge(zeroed, 3)
                    for a in range(HQ):
                        src = xdt_d[q].rearrange("(c s) (a e) -> a s c e", c=C, a=HQ)[a]
                        sp.dma_start(xb[L * a:L * a + L, q % 2, :, a * N:(a + 1) * N], src).then_inc(xb_in[q % 2], 16)
                q = step - 5
                if step == 2 * BATCH + 2:
                    sp.wait_ge(scan_made, 2 * BATCH)
                    sp.wait_ge(states_ready, adds(PAIRS))
                    sp.wait_ge(daq_lo_made, PAIRS)
                    sp.wait_ge(xdt_stored[1], 16 * PAIRS // 2)
                    for u in range(SH):
                        n = unit_width(u)
                        sp.dma_start(raw[:, u * WC:u * WC + n], w_units[u, :, 0:n]).then_inc(raw_in, 16)
                if 0 <= q < NT:
                    sp.wait_ge(xn2_made, q + 1)
                    sp.dma_start(xn2_d[q * P:(q + 1) * P, :], xn2[:, q % 2, :]).then_inc(xn2_stored[q % 2], 16)
                if q == NT - 2:
                    for k in range(2):
                        shared_rows(sp, k, k)
            def load_unit(n, par):
                sp.dma_start(stage_w[:, par, :], w_units[n + SH]).then_inc(unit_in[par], 16)

            sp.wait_ge(scan_made, NT)
            load_unit(0, 0)
            load_unit(1, 1)
            with sp.Fori(0, (E - SH) // 2) as i:
                for j in range(2):
                    k = 2 * i + j + 2
                    sp.wait_ge(unit_lo_made, k - 1)
                    load_unit(k, j)
            sp.dma_start(stage_d, w_units[SH + E - 2, :, WU:WC]).then_inc(last_in[0], 16)
            sp.dma_start(place23[:, 1, 1, WU:WC], w_units[SH + E - 1, :, WU:WC]).then_inc(last_in[1], 16)
            sp.wait_ge(table_written, 16 * NT * TOPK)
            sp.dma_start(tab[:, :], table_d.rearrange("(p t) o -> p (t o)", t=XT)).then_inc(table_in, 16)
            sp.wait_ge(s_up_made, 4 * NT)
            for i in range(2):
                sp.dma_start(place23[:, i, 1, 0:WU], w_units[SH + E - 2 + i, :, 0:WU]).then_inc(last_in[2 + i], 16)

            y_v = y_d[0:ROWS, :].rearrange("(q p j) d -> q p (j d)", p=P, j=TOPK)
            sp.wait_ge(e_down_made, XT)
            for i in range(2):
                sp.wait_ge(scattered[i], 16 * XT // 2)
            for q in range(NT):
                sp.dma_start(yl[:, q, :], y_v[q]).then_inc(y_in[q], 16)
            for q in range(NT):
                sp.wait_ge(sum_made, q + 1)
                sp.dma_start(out_v[q // BATCH, q % BATCH], res[:, q, :]).then_inc(out_stored[q % 2], 16)
            for i in range(2):
                sp.wait_ge(out_stored[i], 16 * NT // 2)

        @block.gpsimd
        def _(pool):
            nc.gpsimd.iota(pair[:, :], [[TOPK * P, NT], [1, TOPK]], base=0, channel_multiplier=TOPK).then_inc(pairs_made, 1)
            nc.gpsimd.iota(init[:, :], [[1, XT]], base=ROWS, channel_multiplier=XT).then_inc(pairs_made, 1)
            nc.gpsimd.memset(ones_col[:, :], 1.0).then_inc(zeroed, 1)
            nc.gpsimd.memset(xb[:, 0], 0.0).then_inc(zeroed, 1)
            nc.gpsimd.memset(xb[:, 1], 0.0).then_inc(zeroed, 1)
            nc.gpsimd.memset(bm[:, :, :, :, :], 0.0).then_inc(bm_made, 1)
            pool.wait_ge(consts_in, 16)
            nc.gpsimd.tensor_copy(after_r[:, :], const("after")).then_inc(after_made, 1)
            pool.wait_ge(small_in, 64)

            def with_bias(u):
                pool.wait_ge(x_normalised, 2 * (u + 1))
                nc.gpsimd.tensor_tensor(res[:, 2 * u:2 * u + 2], res[:, 2 * u:2 * u + 2],
                                        ob_sb[:, :].unsqueeze(1).to_broadcast([P, 2, D]), ALU.add).then_inc(bias_added, 1)

            def inputs(u):
                if u >= 2:
                    pool.wait_ge(xdt_stored[u % 2], 16 * (u // 2))
                pool.wait_ge(dt_made, u + 1)
                for j in range(2):
                    i = nc.gpsimd.tensor_tensor(by_head(xdt[:, u % 2, j]), by_head(xn[:, 2 * u + j]),
                                                dt[:, u % 2, j].unsqueeze(2).to_broadcast([P, H, HD]), ALU.mult)
                i.then_inc(xdt_made, 1)
                if u >= 2:
                    pool.wait_ge(chunk_states_made, u - 1)
                pool.wait_ge(xdt_made, u + 1)
                pool.wait_ge(decays_made, 3 * u + 1)
                for j in range(2):
                    i = nc.gpsimd.tensor_tensor(by_head(xd[:, u % 2, j]), by_head(xdt[:, u % 2, j]),
                                                dec[:, u % 2, j].unsqueeze(2).to_broadcast([P, H, HD]), ALU.mult)
                i.then_inc(xd_made, 1)
                pool.wait_ge(daq_made, C * HQ * (u + 1))
                dq = slice(2 * u, 2 * u + 2)
                nc.gpsimd.tensor_copy(daq_hi[:, dq], daq[:, u % 2]).then_inc(daq_hi_made, 1)
                pool.wait_ge(daq_hi_made, u + 1)
                nc.gpsimd.tensor_tensor(daq_lo[:, dq], daq[:, u % 2], daq_hi[:, dq], ALU.subtract).then_inc(daq_lo_made, 1)

            def skip_part(u):
                for j in range(2):
                    i = nc.gpsimd.tensor_tensor(by_head(xn[:, 2 * u + j]), by_head(xn[:, 2 * u + j]),
                                                d_sb[:, :].unsqueeze(2).to_broadcast([P, H, HD]), ALU.mult)
                i.then_inc(skip_made, 1)

            def increments(q):
                if q >= 2:
                    pool.wait_ge(exponents_made, q - 1)
                pool.wait_ge(daq_lo_made, q // 2 + 1)
                last = masked(nc.gpsimd, rr_hi, daq_hi, q)
                if q >= EARLY:
                    last = masked(nc.gpsimd, rr_lo, daq_lo, q)
                last.then_inc(increments_ready, 1)

            for step in range(STEPS):
                for u, stage in ((step - 8, inputs), (step - 2, with_bias)):
                    if 0 <= u < PAIRS:
                        stage(u)
                m = step - MSTART
                if 0 <= m < NT:
                    increments(m)
                    if m % 2 == 1:
                        skip_part(m // 2)
            for u in range(SH):
                pool.wait_ge(raw_hi_made, u + 1)
                n = unit_width(u)
                nc.gpsimd.tensor_tensor(wu[:, u, 1, 0:n], raw[:, u * WC:u * WC + n], wu[:, u, 0, 0:n],
                                        ALU.subtract).then_inc(raw_lo_made, 1)
            pool.wait_ge(pairs_made, 2)
            pool.wait_ge(table_cleared, 16)
            pool.wait_ge(places_made, 1)
            for i in range(NT * TOPK):
                pool.indirect_dma_start(out=table_d, out_offset=bass.IndirectOffsetOnAxis(ap=slot_i[:, i:i + 1], axis=0),
                                        in_=pair[:, i:i + 1], in_offset=None).then_inc(table_written, 16)

            pool.wait_ge(rconsts_in, 16)
            n_ef = [0]

            def small(ins):
                ins.then_inc(tile_steps, 1)
                n_ef[0] += 1
                pool.wait_ge(tile_steps, n_ef[0])

            small(nc.gpsimd.tensor_scalar(ef[:, 0, :], rconst("tiles")[0:1, :], incl[0:1, 0:1], None, ALU.is_ge))
            for e in range(1, E):
                small(nc.gpsimd.tensor_scalar(em[:, :], rconst("tiles")[0:1, :], incl[0:1, e:e + 1], None, ALU.is_ge))
                small(nc.gpsimd.tensor_tensor(ef[:, e % 2, :], ef[:, (e - 1) % 2, :], em[:, :], ALU.add))
            small(nc.gpsimd.tensor_scalar(em[:, :], ef[:, (E - 1) % 2, :], float(E - 1), None, ALU.min))
            e4 = em[:, :].rearrange("o (i j) -> o i j", j=XG)
            np_ = XT // XG
            for j in range(1, XG + 2):
                src = e4[:, j // XG:np_ + j // XG, j % XG]
                low = ep[:, (j - 1) % 2, :] if j > 1 else e4[:, 0:np_, 0]
                small(nc.gpsimd.tensor_scalar(eq[:, :], src, float(E ** j), None, ALU.mult))
                small(nc.gpsimd.tensor_tensor(ep[:, j % 2, :], eq[:, :], low, ALU.add))
            nc.gpsimd.tensor_copy(epack[:, :], ep[:, (XG + 1) % 2, :]).then_inc(tile_experts_known, 1)

            def gather(k):
                if k >= XG:
                    pool.wait_ge(e_x_turned, k - XG + 1)
                pool.indirect_dma_start(out=xg[:, k % XG, :], out_offset=None, in_=xn2_d,
                                        in_offset=bass.IndirectOffsetOnAxis(ap=tok[:, k:k + 1], axis=0)).then_inc(gathered[k % XG], 16)

            pool.wait_ge(tokens_known, 1)
            pool.wait_ge(s_x_turned, NT)
            for k in range(XG):
                gather(k)
            for k in range(XT + 2):
                if k + XG < XT:
                    gather(k + XG)
                if k >= 2:
                    pool.wait_ge(e_y_made, k - 1)
                    pool.indirect_dma_start(out=y_d, out_offset=bass.IndirectOffsetOnAxis(ap=tab[:, k - 2:k - 1], axis=0),
                                            in_=y_sb[:, k % 2, :], in_offset=None).then_inc(scattered[k % 2], 16)

        @block.scalar
        def _(act):
            nc.scalar.preload_act_table_set("natural_log_exp_and_others")
            act.dma_start(w1_raw[:, :, :], w_small[:, :, 0:NW1]).then_inc(w1_in, 16)
            act.dma_start(bias[:, :], w_bias).then_inc(small_in, 16)
            act.dma_start(a_sb[:, :], a_log.to_broadcast([P, H])).then_inc(small_in, 16)
            act.dma_start(d_sb[:, :], d_row.to_broadcast([P, H])).then_inc(small_in, 16)
            act.dma_start(ob_sb[:, :], ob_row.to_broadcast([P, D])).then_inc(small_in, 16)
            act.dma_start(w2[:, :, :], w_small[:, :, NW1:NW1 + NW2]).then_inc(w2_in, 16)
            act.wait_ge(w1_in, 16)
            nc.scalar.copy(w1_hi[:, :, :], w1_raw[:, :, :]).then_inc(w1_hi_made, 1)
            act.wait_ge(zeroed, 1)

            def rstd_guess(u):
                act.wait_ge(var_made, u + 1)
                nc.scalar.activation(lnv[:, u % 2], var[:, u % 2], ACT.Ln).then_inc(ln_var_made, 1)
                act.wait_ge(ln_var_made, u + 1)
                nc.scalar.activation(y0[:, u % 2], lnv[:, u % 2], ACT.Exp, scale=-0.5).then_inc(rstd_guessed, 1)

            def high_parts(u):
                act.wait_ge(x_turned, u + 1)
                if u >= 2:
                    act.wait_ge(x_projected, u - 1)
                nc.scalar.copy(xt_hi[:, u % 2].rearrange("p k t -> p (k t)"), bank[0][:, :]).then_inc(xt_hi_made, 1)

            def projected(u):
                act.wait_ge(x_projected, u + 1)
                if u == 0:
                    act.wait_ge(small_in, 64)
                if u >= 2:
                    act.wait_ge(bc_products_made, u - 1)
                nc.scalar.activation(bdf[:, u % 2], bank[1][0:N + H, 0:2 * P], ACT.Identity,
                                     bias=bias[0:N + H, 0:1]).then_inc(bdf_made, 1)
                nc.scalar.activation(ct[:, 2 * u:2 * u + 2, :].rearrange("p b t -> p (b t)"), bank[1][:, 2 * P:4 * P],
                                     ACT.Identity, bias=bias[:, 1:2]).then_inc(ct_made, 1)

            def token_major(u):
                act.wait_ge(bc_products_made, u + 1)
                if u >= 4:
                    act.wait_ge(bm_made, u - 2)
                    act.wait_ge(dt_made, u - 3)
                nc.scalar.copy(bz[:, u % 4].rearrange("p b j -> p (b j)"), bank[2][:, 0:2 * (N + H)]).then_inc(bz_made, 1)

            def softplus(u):
                act.wait_ge(minus_abs_made, u + 1)
                nc.scalar.activation(sp_e[:, :, :], na[:, :, :], ACT.Exp).then_inc(softplus_exp_made, 1)
                act.wait_ge(softplus_exp_made, u + 1)
                if u:
                    act.wait_ge(dt_made, u)
                nc.scalar.activation(sp_l[:, :, :], sp_e[:, :, :], ACT.Ln, bias=ones_col[:, 0:1]).then_inc(softplus_log_made, 1)

            def blocks(u):
                if u >= 2:
                    act.wait_ge(chunk_states_made, u - 1)
                act.wait_ge(bm_made, u + 1)
                for c in range(C):
                    i = nc.scalar.copy(bm[L * c:L * c + L, u % 2, :, c, :], bz[L * c:L * c + L, u % 4, :, 0:N])
                i.then_inc(bm_made, 1)

            def by_quarter(u):
                act.wait_ge(da_made, u + 1)
                if u >= 2:
                    act.wait_ge(daq_lo_made, u - 1)
                for a in range(HQ):
                    for c in range(C):
                        nc.scalar.copy(daq[L * a:L * a + L, u % 2, :, c, :],
                                       da[L * c:L * c + L, u % 2, :, a * HG:(a + 1) * HG]).then_inc(daq_made, 1)

            def decays(u):
                act.wait_ge(decay_sums_made, u + 1)
                if u >= 2:
                    act.wait_ge(xd_made, u - 1)
                if u >= 4:
                    act.wait_ge(states_ready, adds(u - 3))
                nc.scalar.activation(dec[:, u % 2].rearrange("p b h -> p (b h)"), bank[3][:, 0:2 * H], ACT.Exp).then_inc(decays_made, 1)
                nc.scalar.activation(ecs[:, 2 * u:2 * u + 2, :].rearrange("p b h -> p (b h)"),
                                     bank[3][:, 2 * H:4 * H], ACT.Exp).then_inc(decays_made, 1)
                nc.scalar.activation(dch[:, u % 4].rearrange("p c h -> p (c h)"), bank[3][:, 4 * H:4 * H + C * H],
                                     ACT.Exp).then_inc(decays_made, 1)
                nc.scalar.copy(gp[:, 2 * u:2 * u + 2, :].rearrange("p b t -> p (b t)"), bank[3][:, 2 * P:4 * P]).then_inc(gp_made, 1)

            def expo(q):
                act.wait_ge(exponents_made, q + 1)
                if q >= 2:
                    act.wait_ge(mm_made, q - 1)
                for i in range(2):
                    nc.scalar.activation(ex[:, q % 2, 16 * i:16 * i + 16, :].rearrange("p a l -> p (a l)"),
                                         bank[i][:, :], ACT.Exp).then_inc(exp_made, 1)

            def y_copy(q):
                act.wait_ge(y_turned, q + 1)
                if q >= 2:
                    act.wait_ge(projected_out, q - 1)
                nc.scalar.copy(yt[:, q % 2], bank[4][:, 0:D]).then_inc(yt_made, 1)

            def rstd2(q):
                act.wait_ge(var2_made, q + 1)
                nc.scalar.activation(lnvb[:, :], varb[:, :], ACT.Ln).then_inc(ln_var2_made, 1)
                act.wait_ge(ln_var2_made, q + 1)
                nc.scalar.activation(y0b[:, :], lnvb[:, :], ACT.Exp, scale=-0.5).then_inc(rstd2_guessed, 1)

            def x2_copy(q):
                act.wait_ge(x2_turned, q + 1)
                if q:
                    act.wait_ge(logits_made, q)
                nc.scalar.copy(x2t[:, :], bank[6][:, 0:D]).then_inc(x2t_made, 1)

            def logits_copy(q):
                act.wait_ge(logits_made, q + 1)
                g = q // BATCH
                if g >= 2:
                    act.wait_ge(routed_groups, g - 1)
                nc.scalar.copy(lg[:, g % 2, q % BATCH, :], bank[7][:, 0:32]).then_inc(logits_copied, 1)

            def gate_exps(g):
                act.wait_ge(logits_copied, BATCH * (g + 1))
                if g:
                    act.wait_ge(routed_groups, g)
                nc.scalar.activation(sgx[:, :], lg[:, g % 2, :, E], ACT.Exp, scale=-1.0).then_inc(gate_exps_made, 1)
                act.wait_ge(logits_shifted, g + 1)
                nc.scalar.activation(pe_[:, :, :].rearrange("p q e -> p (q e)"), shl[:, :, :].rearrange("p q e -> p (q e)"),
                                     ACT.Exp).then_inc(gate_exps_made, 1)

            def raw_high(u):
                act.wait_ge(raw_in, 16 * SH)
                n = unit_width(u)
                nc.scalar.copy(wu[:, u, 0, 0:n], raw[:, u * WC:u * WC + n]).then_inc(raw_hi_made, 1)

            def s_xhigh(k):
                act.wait_ge(s_x_turned, k + 1)
                if not isinstance(k, int) or k >= 1:
                    act.wait_ge(s_up_made, 4 * k)
                nc.scalar.copy(tx_hi[:, :], bank[0][:, 0:D]).then_inc(s_xt_hi_made, 1)

            for step in range(STEPS):
                for k, stage in ((1, rstd_guess), (2, high_parts), (4, projected), (5, token_major), (6, softplus),
                                 (7, decays), (7, by_quarter), (8, blocks)):
                    if 0 <= step - k < PAIRS:
                        stage(step - k)
                if step == 5:
                    act.wait_ge(small_in, 64)
                    nc.scalar.activation(a_sb[:, :], a_sb[:, :], ACT.Exp).then_inc(a_exp_made, 1)
                m = step - MSTART
                for k, stage in ((0, expo), (5, rstd2), (3, y_copy), (7, logits_copy), (6, x2_copy)):
                    if 0 <= m - k < NT:
                        stage(m - k)
                if m >= ROUTE and (m - ROUTE) % BATCH == 0:
                    gate_exps((m - ROUTE) // BATCH)
                if 0 <= m - SPLIT < SH:
                    raw_high(m - SPLIT)
                if m == NT + 5:
                    s_xhigh(0)

            def split_high(slot, n, par, uses):
                act.wait_ge(unit_in[par], 16 * uses)
                nc.scalar.copy(wu[:, slot, 0, :], stage_w[:, par, :]).then_inc(unit_hi_made, 1)

            def s_thigh(k):
                act.wait_ge(s_h_turned, k + 1)
                if not isinstance(k, int) or k >= 1:
                    act.wait_ge(s_down_made, k)
                nc.scalar.copy(th_hi[:, 0:4, :].rearrange("p c t -> p (c t)"), bank[5][:, :]).then_inc(s_th_hi_made, 1)
                nc.scalar.copy(th_hi[:, 4:6, :].rearrange("p c t -> p (c t)"), bank[6][:, 0:2 * P]).then_inc(s_th_hi_made, 1)

            def s_silu(k):
                for c in range(2):
                    act.wait_ge(s_up_made, 4 * k + c + 1)
                    if not isinstance(k, int) or k >= 1:
                        act.wait_ge(s_gated_made, 2 * k + c - 1)
                    nc.scalar.activation(act_s[:, c * 352:(c + 1) * 352], bank[1 + c][:, 0:352], ACT.Silu).then_inc(s_silu_made, 1)

            for i in range(2):
                act.wait_ge(xn2_stored[i], 16 * NT // 2)
            shared_rows(act, 2, 0)
            s_silu(0)
            s_xhigh(1)
            shared_rows(act, 3, 1)
            def s_step(i, j):
                k = 2 * i + j + 1
                s_thigh(k - 1)
                s_silu(k)
                s_xhigh(k + 1)
                shared_rows(act, k + 3, j)
                split_high(k + 3, k - 1, j, i + 1)

            for j in range(2):
                s_step(0, j)
            with act.Fori(1, (E - SH) // 2) as i:
                for j in range(2):
                    s_step(i, j)
            def last_high(i):
                place, cols, src, loaded, n = LAST[i]
                act.wait_ge(loaded, n)
                if i >= 5:
                    act.wait_ge(s_down_made, NT)
                elif i >= 1:
                    act.wait_ge(s_up_made, 4 * NT)
                nc.scalar.copy(wu[:, place, 0, cols], src).then_inc(unit_hi_made, 1)

            for k in range(E - SH + 1, NT):
                s_thigh(k - 1)
                s_silu(k)
                if k + 1 < NT:
                    s_xhigh(k + 1)
            for i in range(3):
                last_high(i)
            s_thigh(NT - 1)
            for i in range(3, 5):
                last_high(i)
            def e_thigh(k, par):
                act.wait_ge(e_h_turned, k + 1)
                if not isinstance(k, int) or k >= 2:
                    act.wait_ge(e_down_made, k - 1)
                nc.scalar.copy(et_hi[par].rearrange("p c t -> p (c t)"), bank[5][0:EK, 0:2 * P]).then_inc(e_th_hi_made, 1)

            def e_silu(k, par):
                act.wait_ge(e_up_made, k + 1)
                if not isinstance(k, int) or k >= 1:
                    act.wait_ge(e_gated_made, k)
                nc.scalar.activation(act_s[:, 0:EI], bank[1 + par][:, 0:EI], ACT.Silu).then_inc(e_silu_made, 1)

            def e_xhigh(k, par):
                act.wait_ge(e_x_turned, k + 1)
                if not isinstance(k, int) or k >= 2:
                    act.wait_ge(e_up_made, k - 1)
                nc.scalar.copy(xt2_hi[par], bank[0][:, 0:D]).then_inc(e_xt_hi_made, 1)

            def e_result(k, par, uses):
                act.wait_ge(e_down_made, k + 1)
                if not isinstance(uses, int) or uses >= 1:
                    act.wait_ge(scattered[par], 16 * uses)
                nc.scalar.copy(y_sb[:, par, :], bank[7][:, 0:D]).then_inc(e_y_made, 1)

            act.wait_ge(s_th_lo_made, 2 * NT)
            e_xhigh(0, 0)
            for i in range(5, 8):
                last_high(i)
            e_xhigh(1, 1)
            e_silu(0, 0)
            e_xhigh(2, 0)

            def e_step(k, n, j):
                e_silu(k, j % 2)
                if not isinstance(k, int) or k + 2 < XT:
                    e_xhigh(k + 2, j % 2)
                e_thigh(k - 1, (j - 1) % 2)
                if not isinstance(k, int) or k >= 2:
                    e_result(k - 2, j % 2, n * (XG // 2) + j // 2 - 1)

            expert_tiles(act, e_step)
            e_thigh(XT - 1, (XT - 1) % 2)
            for k in (XT - 2, XT - 1):
                e_result(k, k % 2, k // 2)

        @block.vector
        def _(dve):
            dve.wait_ge(w1_hi_made, 1)
            nc.vector.tensor_tensor(w1_lo[:, :, :], w1_raw[:, :, :], w1_hi[:, :, :], ALU.subtract).then_inc(w1_lo_made, 1)
            nc.vector.memset(state[:, 0, :, 0, :], 0.0).then_inc(states_ready, 1)
            nw = [0]

            def newton(v, y, a, b, r):
                ops = (lambda: nc.vector.tensor_tensor(a, y, y, ALU.mult),
                       lambda: nc.vector.scalar_tensor_tensor(out=b, in0=a, scalar=-0.5, in1=v, op0=ALU.mult, op1=ALU.mult),
                       lambda: nc.vector.scalar_tensor_tensor(out=r, in0=b, scalar=1.5, in1=y, op0=ALU.add, op1=ALU.mult))
                for op in ops:
                    op().then_inc(newton_steps, 1)
                    nw[0] += 1
                    dve.wait_ge(newton_steps, nw[0])

            def stats(u):
                if u % 2 == 0:
                    dve.wait_ge(x_in[u // 2], 16)
                for j in range(2):
                    nc.vector.bn_stats(stat6[:, u % 2, j], res[:, 2 * u + j]).then_inc(stats_made, 1)
                for j in range(2):
                    dve.wait_ge(stats_made, 2 * u + j + 1)
                    nc.vector.bn_aggr(mv[:, u % 2, j], stat6[:, u % 2, j]).then_inc(mean_var_made, 1)
                dve.wait_ge(mean_var_made, 2 * (u + 1))
                nc.vector.tensor_scalar(var[:, u % 2], mv[:, u % 2, :, 1], EPS, None, ALU.add).then_inc(var_made, 1)

            def normalise(u):
                dve.wait_ge(rstd_guessed, u + 1)
                newton(var[:, u % 2], y0[:, u % 2], ya[:, :], yb[:, :], rs[:, :])
                for j in range(2):
                    nc.vector.tensor_scalar(xn[:, 2 * u + j], res[:, 2 * u + j], mv[:, u % 2, j, 0:1],
                                            rs[:, j:j + 1], ALU.subtract, ALU.mult).then_inc(x_normalised, 1)

            def low_parts(u):
                dve.wait_ge(xt_hi_made, u + 1)
                if u >= 2:
                    dve.wait_ge(x_projected, u - 1)
                nc.vector.tensor_tensor(xt_lo[:, u % 2].rearrange("p k t -> p (k t)"), bank[0][:, :],
                                        xt_hi[:, u % 2].rearrange("p k t -> p (k t)"), ALU.subtract).then_inc(xt_lo_made, 1)

            def masks(u):
                dve.wait_ge(bz_made, u + 1)
                if u >= 2:
                    dve.wait_ge(gp_sums_made, u - 1)
                nc.vector.tensor_tensor(gmd[:, u % 2].rearrange("p (b t) -> p b t", b=2),
                                        bank[2][:, 2 * P:4 * P].rearrange("p (b t) -> p b t", b=2),
                                        const("upto").unsqueeze(1).to_broadcast([P, 2, P]), ALU.mult).then_inc(gmd_made, 1)
                z = bz[:, u % 4, :, N:N + H]
                nc.vector.scalar_tensor_tensor(out=na[:, :, :], in0=z, scalar=-1.0, in1=z, op0=ALU.mult,
                                               op1=ALU.min).then_inc(minus_abs_made, 1)

            def steps(u):
                dve.wait_ge(softplus_log_made, u + 1)
                if u >= 2:
                    dve.wait_ge(xdt_made, u - 1)
                nc.vector.scalar_tensor_tensor(out=dt[:, u % 2], in0=bz[:, u % 4, :, N:N + H], scalar=0.0, in1=sp_l[:, :, :],
                                               op0=ALU.max, op1=ALU.add).then_inc(dt_made, 1)
                dve.wait_ge(dt_made, u + 1)
                dve.wait_ge(a_exp_made, 1)
                if u >= 2:
                    dve.wait_ge(decay_sums_made, u - 1)
                    dve.wait_ge(daq_made, C * HQ * (u - 1))
                nc.vector.scalar_tensor_tensor(out=da[:, u % 2], in0=dt[:, u % 2], scalar=-1.0,
                                               in1=a_sb[:, :].unsqueeze(1).to_broadcast([P, 2, H]),
                                               op0=ALU.mult, op1=ALU.mult).then_inc(da_made, 1)

            def recur(u):
                g, i = u // 2, u % 2
                dve.wait_ge(chunk_states_made, u + 1)
                dve.wait_ge(decays_made, 3 * u + 3)
                for c in range(C):
                    if (g, c) == (GROUPS - 1, C - 1):
                        continue
                    dve.wait_ge(states_ready, adds(u) + c)
                    nc.vector.tensor_tensor(by_head(tmp_s[:, :]), by_head(state[:, g, i, c]),
                                            dch[:, u % 4, c].unsqueeze(2).to_broadcast([P, H, HD]), ALU.mult).then_inc(state_decayed, 1)
                    dve.wait_ge(state_decayed, adds(u) + c)
                    nxt = (g, c + 1) if c + 1 < C else (g + 1, 0)
                    nc.vector.tensor_tensor(state[:, nxt[0], i, nxt[1]], tmp_s[:, :],
                                            bank[4 + 2 * i + c // 2][:, D * (c % 2):D * (c % 2) + D],
                                            ALU.add).then_inc(states_ready, 1)

            def weigh(q):
                dve.wait_ge(exp_made, 2 * (q + 1))
                if q >= 2:
                    dve.wait_ge(scan_made, q - 1)
                dve.wait_ge(gp_made, q // 2 + 1)
                g4 = gp[:, q].rearrange("p (c l) -> p c l", c=C)
                nc.vector.tensor_tensor(mm[:, q % 2].rearrange("p (c a) l -> p c a l", c=C),
                                        ex[:, q % 2].rearrange("p (c a) l -> p c a l", c=C),
                                        g4.unsqueeze(2).to_broadcast([P, C, HG, L]), ALU.mult).then_inc(mm_made, 1)

            def combine(q):
                pb = bank[2 + q % 2]
                dve.wait_ge(scan_made, q + 1)
                nc.vector.tensor_tensor(by_head(t1[:, :]), by_head(pb[:, D:2 * D]),
                                        ecs[:, q].unsqueeze(2).to_broadcast([P, H, HD]), ALU.mult).then_inc(t1_made, 1)
                dve.wait_ge(t1_made, q + 1)
                if q >= 2:
                    dve.wait_ge(y_turned, q - 1)
                nc.vector.tensor_tensor(yy[:, q % 2], t1[:, :], pb[:, 0:D], ALU.add).then_inc(y_made, 1)

            def low_increments(q):
                if q >= 2:
                    dve.wait_ge(exponents_made, q - 1)
                dve.wait_ge(daq_lo_made, q // 2 + 1)
                dve.wait_ge(consts_in, 16)
                masked(nc.vector, rr_lo, daq_lo, q).then_inc(low_increments_ready, 1)

            def residual(q):
                dve.wait_ge(projected_out, q + 1)
                dve.wait_ge(bias_added, q // 2 + 1)
                nc.vector.tensor_tensor(res[:, q], bank[5][:, 0:D], res[:, q], ALU.add).then_inc(residual_made, 1)
                dve.wait_ge(residual_made, q + 1)
                nc.vector.bn_stats(stat6b[:, :], res[:, q]).then_inc(stats2_made, 1)
                dve.wait_ge(stats2_made, q + 1)
                nc.vector.bn_aggr(mvb[:, :], stat6b[:, :]).then_inc(mean_var2_made, 1)
                dve.wait_ge(mean_var2_made, q + 1)
                nc.vector.tensor_scalar(varb[:, :], mvb[:, 1:2], EPS, None, ALU.add).then_inc(var2_made, 1)

            def normalise2(q):
                dve.wait_ge(rstd2_guessed, q + 1)
                newton(varb[:, :], y0b[:, :], yab[:, :], ybb[:, :], rsb[:, :])
                if q >= 2:
                    dve.wait_ge(xn2_stored[q % 2], 16 * (q // 2))
                    dve.wait_ge(x2_turned, q - 1)
                nc.vector.tensor_scalar(xn2[:, q % 2], res[:, q], mvb[:, 0:1], rsb[:, 0:1], ALU.subtract,
                                        ALU.mult).then_inc(xn2_made, 1)

            nr = [0]

            def r_(ins):
                ins.then_inc(routing_steps, 1)
                nr[0] += 1
                dve.wait_ge(routing_steps, nr[0])

            def wide(ap, n):
                return ap.unsqueeze(2).to_broadcast([P, ap.shape[1], n])

            def shifted(g):
                dve.wait_ge(logits_copied, BATCH * (g + 1))
                r_(nc.vector.tensor_reduce(mx[:, :], lg[:, g % 2, :, 0:E], AX.X, ALU.max))
                nc.vector.tensor_tensor(shl[:, :, :], lg[:, g % 2, :, 0:E], wide(mx[:, :], E), ALU.subtract).then_inc(logits_shifted, 1)

            def choose(g):
                qs = slice(g * BATCH, (g + 1) * BATCH)
                dve.wait_ge(gate_exps_made, 2 * (g + 1))
                r_(nc.vector.tensor_reduce(sm[:, :], pe_[:, :, :], AX.X, ALU.add))
                r_(nc.vector.reciprocal(rc[:, :], sm[:, :]))
                r_(nc.vector.tensor_tensor(prob[:, :, :], pe_[:, :, :], wide(rc[:, :], E), ALU.mult))
                for b in range(BATCH):
                    last = nc.vector.max(m8[:, b, :], prob[:, b, :])
                r_(last)
                for b in range(BATCH):
                    last = nc.vector.max_index(i8[:, b, :], m8[:, b, :], prob[:, b, :])
                nc.vector.tensor_scalar(sgy[:, :], sgx[:, :], 1.0, None, ALU.add).then_inc(routed_groups, 1)
                r_(nc.vector.tensor_reduce(sw[:, :], m8[:, :, 0:TOPK], AX.X, ALU.add))
                dve.wait_ge(routed_groups, g + 1)
                nc.vector.reciprocal(sig[:, qs], sgy[:, :])
                r_(nc.vector.reciprocal(rw[:, :], sw[:, :]))
                nc.vector.tensor_tensor(wgt[:, qs, :], m8[:, :, 0:TOPK], wide(rw[:, :], TOPK), ALU.mult)
                r_(nc.vector.tensor_copy(idf[:, qs, :], i8[:, :, 0:TOPK]))

            def s_xlow(k):
                dve.wait_ge(s_xt_hi_made, k + 1)
                if not isinstance(k, int) or k >= 1:
                    dve.wait_ge(s_up_made, 4 * k)
                nc.vector.tensor_tensor(tx_lo[:, :], bank[0][:, 0:D], tx_hi[:, :], ALU.subtract).then_inc(s_xt_lo_made, 1)

            for step in range(STEPS):
                for k, stage in ((3, low_parts), (7, steps), (6, masks), (10, recur), (1, normalise), (0, stats)):
                    if 0 <= step - k < PAIRS:
                        stage(step - k)
                m = step - MSTART
                for k, stage in ((5, residual), (1, weigh), (5, normalise2), (2, combine)):
                    if 0 <= m - k < NT:
                        stage(m - k)
                if 0 <= m + 1 < EARLY:
                    low_increments(m + 1)
                if m > ROUTE and (m - ROUTE) % BATCH == 1:
                    choose((m - ROUTE) // BATCH)
                if m >= ROUTE and (m - ROUTE) % BATCH == 0:
                    shifted((m - ROUTE) // BATCH)
                if m == NT + 5:
                    s_xlow(0)

            def s_gated(k):
                for c in range(2):
                    dve.wait_ge(s_silu_made, 2 * k + c + 1)
                    dve.wait_ge(s_up_made, 4 * k + c + 3)
                    if not isinstance(k, int) or k >= 1:
                        dve.wait_ge(s_h_turned, k)
                    nc.vector.tensor_tensor(act_h[:, c * 352:(c + 1) * 352], act_s[:, c * 352:(c + 1) * 352],
                                            bank[3 + c][:, 0:352], ALU.mult).then_inc(s_gated_made, 1)

            for i in range(2):
                dve.wait_ge(xn2_stored[i], 16 * NT // 2)
            dve.wait_ge(logits_made, NT)
            dve.wait_ge(rconsts_in, 16)
            r_(nc.vector.tensor_tensor(oh[:, :, :, :].rearrange("p q j e -> p (q j) e"),
                                       wide(idf[:, :, :].rearrange("p q j -> p (q j)"), E),
                                       rconst("iota_e").unsqueeze(1).to_broadcast([P, NT * TOPK, E]), ALU.is_equal))
            nc.vector.tensor_reduce(msk[:, :, :].rearrange("p e q -> p q e"), oh[:, :, :, :].rearrange("p q j e -> p q e j"),
                                    AX.X, ALU.add).then_inc(choices_marked, 1)
            nc.vector.memset(act_h[:, SI:6 * P], 0.0).then_inc(pad_zeroed, 1)
            s_gated(0)
            s_xlow(1)
            dve.wait_ge(counts_made, 1)
            rank, tot = bank[7][:, 0:E * NT], bank[7][:, E * NT:2 * E * NT]
            flat = lambda t: t[:, :, :].rearrange("p e q -> p (e q)")
            r_(nc.vector.tensor_tensor_scan(flat(inc), rconst("keep"), tot, 0.0, ALU.mult, ALU.add))
            r_(nc.vector.tensor_tensor(flat(exc), flat(inc), tot, ALU.subtract))
            r_(nc.vector.tensor_tensor(gt[:, :, :], inc[:, :, NT - 1].unsqueeze(2).to_broadcast([P, E, NT]),
                                       rconst("edges").unsqueeze(1).to_broadcast([P, E, NT]), ALU.is_gt))
            r_(nc.vector.tensor_reduce(tl[:, :], gt[:, :, :], AX.X, ALU.add))
            r_(nc.vector.tensor_tensor_scan(incl[:, :], rconst("ones")[:, 0:E], tl[:, :], 0.0, ALU.mult, ALU.add))
            r_(nc.vector.tensor_tensor(base[:, :], incl[:, :], tl[:, :], ALU.subtract))
            r_(nc.vector.tensor_tensor(flat(sl), flat(exc), rank, ALU.add))
            r_(nc.vector.scalar_tensor_tensor(out=sl2[:, :, :], in0=wide(base[:, :], NT), scalar=float(P), in1=sl[:, :, :],
                                              op0=ALU.mult, op1=ALU.add))
            r_(nc.vector.tensor_tensor(so[:, :, :, :], oh[:, :, :, :],
                                       sl2[:, :, :].rearrange("p e q -> p q e").unsqueeze(2).to_broadcast([P, NT, TOPK, E]), ALU.mult))
            r_(nc.vector.tensor_reduce(slf[:, :], so[:, :, :, :].rearrange("p q j e -> p (q j) e"), AX.X, ALU.add))
            r_(nc.vector.tensor_copy(si[:, :], slf[:, :]))
            r_(nc.vector.tensor_scalar(s_hi7[:, :], si[:, :], 7, None, ALU.logical_shift_right))
            r_(nc.vector.tensor_scalar(s_lo7[:, :], si[:, :], P - 1, None, ALU.bitwise_and))
            nc.vector.scalar_tensor_tensor(out=slot_i[:, :], in0=s_lo7[:, :], scalar=float(XT), in1=s_hi7[:, :],
                                           op0=ALU.mult, op1=ALU.add).then_inc(places_made, 1)

            def split_low(slot, n, par):
                dve.wait_ge(unit_hi_made, n + 1)
                nc.vector.tensor_tensor(wu[:, slot, 1, :], stage_w[:, par, :], wu[:, slot, 0, :], ALU.subtract).then_inc(unit_lo_made, 1)

            def s_tlow(k):
                dve.wait_ge(s_th_hi_made, 2 * k + 2)
                if not isinstance(k, int) or k >= 1:
                    dve.wait_ge(s_down_made, k)
                nc.vector.tensor_tensor(th_lo[:, 0:4, :].rearrange("p c t -> p (c t)"), bank[5][:, :],
                                        th_hi[:, 0:4, :].rearrange("p c t -> p (c t)"), ALU.subtract).then_inc(s_th_lo_made, 1)
                nc.vector.tensor_tensor(th_lo[:, 4:6, :].rearrange("p c t -> p (c t)"), bank[6][:, 0:2 * P],
                                        th_hi[:, 4:6, :].rearrange("p c t -> p (c t)"), ALU.subtract).then_inc(s_th_lo_made, 1)

            def s_add(k):
                dve.wait_ge(s_down_made, k + 1)
                nc.vector.scalar_tensor_tensor(out=res[:, k, :], in0=bank[7][:, 0:D], scalar=sig[:, bass.ds(k, 1)],
                                               in1=res[:, k, :], op0=ALU.mult, op1=ALU.add).then_inc(s_added, 1)

            def s_step(i, j):
                k = 2 * i + j + 1
                s_tlow(k - 1)
                s_gated(k)
                s_xlow(k + 1)
                s_add(k - 1)
                split_low(k + 3, k - 1, j)

            for j in range(2):
                s_step(0, j)
            with dve.Fori(1, (E - SH) // 2) as i:
                for j in range(2):
                    s_step(i, j)
            for k in range(E - SH + 1, NT):
                s_tlow(k - 1)
                s_gated(k)
                if k + 1 < NT:
                    s_xlow(k + 1)
                s_add(k - 1)
            def last_low(i):
                place, cols, src, _, _ = LAST[i]
                dve.wait_ge(unit_hi_made, E - SH + 1 + i)
                nc.vector.tensor_tensor(wu[:, place, 1, cols], src, wu[:, place, 0, cols], ALU.subtract).then_inc(unit_lo_made, 1)

            dve.wait_ge(table_in, 16)
            nc.vector.tensor_scalar(tok[:, :], tab[:, :], 2, T - 1, ALU.logical_shift_right, ALU.bitwise_and).then_inc(tokens_known, 1)
            last_low(0)
            s_tlow(NT - 1)
            for i in range(1, 5):
                last_low(i)
            s_add(NT - 1)

            def e_tlow(k, par):
                dve.wait_ge(e_th_hi_made, k + 1)
                if not isinstance(k, int) or k >= 2:
                    dve.wait_ge(e_down_made, k - 1)
                nc.vector.tensor_tensor(et_lo[par].rearrange("p c t -> p (c t)"), bank[5][0:EK, 0:2 * P],
                                        et_hi[par].rearrange("p c t -> p (c t)"), ALU.subtract).then_inc(e_th_lo_made, 1)

            def e_gated(k, par):
                dve.wait_ge(e_silu_made, k + 1)
                if not isinstance(k, int) or k >= 2:
                    dve.wait_ge(e_h_turned, k - 1)
                nc.vector.tensor_tensor(act_h[:, par * EI:(par + 1) * EI], act_s[:, 0:EI], bank[1 + par][:, EI:2 * EI], ALU.mult).then_inc(e_gated_made, 1)

            def e_xlow(k, par):
                dve.wait_ge(e_xt_hi_made, k + 1)
                if not isinstance(k, int) or k >= 2:
                    dve.wait_ge(e_up_made, k - 1)
                nc.vector.tensor_tensor(xt2_lo[par], bank[0][:, 0:D], xt2_hi[par], ALU.subtract).then_inc(e_xt_lo_made, 1)

            e_xlow(0, 0)
            for i in range(5, 8):
                last_low(i)
            e_xlow(1, 1)
            e_gated(0, 0)
            e_xlow(2, 0)

            def e_step(k, n, j):
                e_gated(k, j % 2)
                if not isinstance(k, int) or k + 2 < XT:
                    e_xlow(k + 2, j % 2)
                e_tlow(k - 1, (j - 1) % 2)

            expert_tiles(dve, e_step)
            e_tlow(XT - 1, (XT - 1) % 2)

            dve.wait_ge(s_added, NT)
            summed = {}

            def join(q, j):
                dve.wait_ge(y_in[q], 16) if j == 0 else dve.wait_ge(routing_steps, summed[q])
                ins = nc.vector.scalar_tensor_tensor(out=res[:, q, :], in0=yl[:, q, j * D:(j + 1) * D],
                                                     scalar=wgt[:, q, j:j + 1], in1=res[:, q, :],
                                                     op0=ALU.mult, op1=ALU.add)
                if j == TOPK - 1:
                    ins.then_inc(sum_made, 1)
                else:
                    ins.then_inc(routing_steps, 1)
                    nr[0] += 1
                    summed[q] = nr[0]

            for q in range(NT + 1):
                for j in range(TOPK // 2):
                    if q >= 1:
                        join(q - 1, TOPK // 2 + j)
                    if q < NT:
                        join(q, j)

        @block.tensor
        def _(pe):
            pe.wait_ge(consts_in, 16)
            ident = const("ident")

            def transposes(u):
                if u:
                    pe.wait_ge(xt_lo_made, u)
                for j in range(2):
                    pe.wait_ge(x_normalised, 2 * u + j + 1)
                    for k in range(K2):
                        last = nc.tensor.transpose(bank[0][:, (2 * k + j) * P:(2 * k + j + 1) * P],
                                                   xn[:, 2 * u + j, k * P:(k + 1) * P], ident)
                last.then_inc(x_turned, 1)

            def project(u):
                pe.wait_ge(w1_lo_made, 1)
                pe.wait_ge(xt_lo_made, u + 1)
                if u:
                    pe.wait_ge(bdf_made, u)
                    pe.wait_ge(ct_made, u)
                xs = [(xt_hi[:, u % 2, k], xt_lo[:, u % 2, k]) for k in range(K2)]
                split3(bank[1][0:N + H, 0:2 * P], [((wcol(w1_hi, "bd", k), wcol(w1_lo, "bd", k)), xs[k]) for k in range(K2)])
                split3(bank[1][:, 2 * P:4 * P], [((wcol(w1_hi, "cc", k), wcol(w1_lo, "cc", k)), xs[k])
                                                 for k in range(K2)]).then_inc(x_projected, 1)

            def chunk_products(u):
                pe.wait_ge(bdf_made, u + 1)
                pe.wait_ge(ct_made, u + 1)
                if u:
                    pe.wait_ge(bz_made, u)
                    pe.wait_ge(gmd_made, u)
                for j in range(2):
                    nc.tensor.transpose(bank[2][:, j * (N + H):(j + 1) * (N + H)], bdf[:, u % 2, j * P:(j + 1) * P],
                                        const("ident")[0:N + H, 0:N + H])
                for j in range(2):
                    last = nc.tensor.matmul(bank[2][:, (2 + j) * P:(3 + j) * P], bdf[0:N, u % 2, j * P:(j + 1) * P],
                                            ct[0:N, 2 * u + j, :], start=True, stop=True)
                last.then_inc(bc_products_made, 1)

            def sums(u):
                pe.wait_ge(gmd_made, u + 1)
                if u:
                    pe.wait_ge(decays_made, 3 * u)
                    pe.wait_ge(gp_made, u)
                nc.tensor.matmul(bank[3][:, 2 * P:4 * P], const("spread"), gmd[:, u % 2], start=True, stop=True).then_inc(gp_sums_made, 1)
                pe.wait_ge(da_made, u + 1)
                d2 = da[:, u % 2].rearrange("p b h -> p (b h)")
                nc.tensor.matmul(bank[3][:, 0:2 * H], const("after"), d2, start=True, stop=True)
                nc.tensor.matmul(bank[3][:, 2 * H:4 * H], const("upto"), d2, start=True, stop=True)
                for c in range(C):
                    for j in range(2):
                        col = (4 + c) * H
                        last = nc.tensor.matmul(bank[3][N * j:N * j + N, col:col + H],
                                                const("chunk")[:, c * N:(c + 1) * N], da[:, u % 2, j, :],
                                                start=True, stop=True)
                last.then_inc(decay_sums_made, 1)

            def states(u):
                pe.wait_ge(xd_made, u + 1)
                pe.wait_ge(bm_made, u + 2)
                if u >= 2:
                    pe.wait_ge(states_ready, adds(u - 1))
                for c in range(C):
                    if u >= PAIRS - 2 and c == C - 1:
                        continue
                    for j in range(2):
                        last = nc.tensor.matmul(bank[4 + 2 * (u % 2) + c // 2][N * j:N * j + N, D * (c % 2):D * (c % 2) + D],
                                                bm[:, u % 2, j, c, :], xd[:, u % 2, j, :], start=True, stop=True)
                last.then_inc(chunk_states_made, 1)

            def exponents(q):
                pe.wait_ge(increments_ready, q + 1)
                if q < EARLY:
                    pe.wait_ge(low_increments_ready, q + 1)
                pe.wait_ge(after_made, 1)
                if q >= 1:
                    pe.wait_ge(exp_made, 2 * q)
                else:
                    pe.wait_ge(ct_made, PAIRS)
                for i in range(2):
                    for part in (rr_lo, rr_hi):
                        last = nc.tensor.matmul(bank[i][:, :], after_r[:, :],
                                                part[:, q % 2, 16 * i:16 * i + 16, :].rearrange("p a l -> p (a l)"),
                                                start=(part is rr_lo), stop=(part is rr_hi))
                last.then_inc(exponents_made, 1)

            def outputs(q):
                g, i, j = q // BATCH, q % BATCH // 2, q % 2
                pb = bank[2 + q % 2]
                if q >= 2:
                    pe.wait_ge(y_made, q - 1)
                elif q == 0:
                    pe.wait_ge(gmd_made, PAIRS)
                    pe.wait_ge(bz_made, PAIRS)
                else:
                    pe.wait_ge(decays_made, 3 * PAIRS)
                    pe.wait_ge(gp_made, PAIRS)
                pe.wait_ge(states_ready, adds(q // 2 + 1))
                for c in range(C):
                    nc.tensor.matmul(pb[L * c:L * c + L, D:2 * D], ct[N * j:N * j + N, q, L * c:L * c + L],
                                     state[N * j:N * j + N, g, i, c, :], start=True, stop=True)
                pe.wait_ge(skip_made, q // 2 + 1)
                nc.tensor.matmul(pb[:, 0:D], ident, xn[:, q], start=True, stop=False)
                pe.wait_ge(mm_made, q + 1)
                pe.wait_ge(xb_in[q % 2], 16 * HQ * (q // 2 + 1))
                for a in range(HG):
                    for c in range(C):
                        o = pb[L * c:L * c + L, 0:D].rearrange("p (a g e) -> p g a e", g=HG, e=HD)[:, a]
                        r = xb[:, q % 2, c].rearrange("p (a g e) -> p g a e", g=HG, e=HD)[:, a]
                        last = nc.tensor.matmul(o, mm[:, q % 2, c * HG + a, :], r, start=False, stop=(a == HG - 1))
                last.then_inc(scan_made, 1)

            def turn_y(q):
                pe.wait_ge(y_made, q + 1)
                if q:
                    pe.wait_ge(yt_made, q)
                else:
                    pe.wait_ge(states_ready, adds(PAIRS - 1))
                for k in range(K2):
                    last = nc.tensor.transpose(bank[4][:, k * P:(k + 1) * P], yy[:, q % 2, k * P:(k + 1) * P], ident)
                last.then_inc(y_turned, 1)

            def project_out(q):
                if q:
                    pe.wait_ge(residual_made, q)
                else:
                    pe.wait_ge(w2_in, 16)
                pe.wait_ge(yt_made, q + 1)
                for k in range(K2):
                    last = nc.tensor.matmul(bank[5][:, 0:D], yt[:, q % 2, k * P:(k + 1) * P], wcol(w2, "wo", k),
                                            start=(k == 0), stop=(k == K2 - 1))
                last.then_inc(projected_out, 1)

            def turn_x2(q):
                pe.wait_ge(xn2_made, q + 1)
                if not q:
                    pe.wait_ge(states_ready, adds(PAIRS))
                if q:
                    pe.wait_ge(x2t_made, q)
                for k in range(K2):
                    last = nc.tensor.transpose(bank[6][:, k * P:(k + 1) * P], xn2[:, q % 2, k * P:(k + 1) * P], ident)
                last.then_inc(x2_turned, 1)

            def logits(q):
                pe.wait_ge(x2t_made, q + 1)
                if q:
                    pe.wait_ge(logits_copied, q)
                for k in range(K2):
                    last = nc.tensor.matmul(bank[7][:, 0:32], x2t[:, k * P:(k + 1) * P], wcol(w2, "wg", k),
                                            start=(k == 0), stop=(k == K2 - 1))
                last.then_inc(logits_made, 1)

            xs = [(tx_hi[:, k * P:(k + 1) * P], tx_lo[:, k * P:(k + 1) * P]) for k in range(K2)]

            def s_turn_x(k, par, uses):
                pe.wait_ge(rows_in[par], 16 * uses)
                if isinstance(k, int) and k == 0:
                    pe.wait_ge(exp_made, 2 * NT)
                else:
                    pe.wait_ge(s_xt_lo_made, k)
                for c in range(K2):
                    last = nc.tensor.transpose(bank[0][:, c * P:(c + 1) * P], xg[:, par, c * P:(c + 1) * P], ident)
                last.then_inc(s_x_turned, 1)

            for step in range(STEPS):
                for k, stage in ((4, project), (2, transposes), (5, chunk_products), (7, sums), (9, states)):
                    if 0 <= step - k < PAIRS:
                        stage(step - k)
                m = step - MSTART
                for k, stage in ((0, exponents), (2, outputs), (3, turn_y), (4, project_out), (7, logits), (6, turn_x2)):
                    if 0 <= m - k < NT:
                        stage(m - k)
                if m == NT + 5:
                    s_turn_x(0, 0, 1)

            def s_up(k):
                pe.wait_ge(s_xt_lo_made, k + 1)
                for c in range(4):
                    if isinstance(k, int) and k == 0:
                        pe.wait_ge(raw_lo_made, c + 1)
                    elif c % 2 == 0:
                        pe.wait_ge(s_gated_made, 2 * k)
                    split3(bank[1 + c][:, 0:2 * EI],
                           [(xs[b], up(c, b)) for b in range(K2)]).then_inc(s_up_made, 1)

            def s_turn_h(k):
                pe.wait_ge(s_gated_made, 2 * k + 2)
                if isinstance(k, int) and k == 0:
                    pe.wait_ge(pad_zeroed, 1)
                else:
                    pe.wait_ge(s_th_lo_made, 2 * k)
                for c in range(6):
                    last = nc.tensor.transpose(bank[5 + c // 4][:, c % 4 * P:(c % 4 + 1) * P], act_h[:, c * P:(c + 1) * P], ident)
                last.then_inc(s_h_turned, 1)

            def s_down(k):
                pe.wait_ge(s_th_lo_made, 2 * k + 2)
                if isinstance(k, int) and k == 0:
                    pe.wait_ge(places_made, 1)
                else:
                    pe.wait_ge(s_added, k)
                split3(bank[7][:, 0:D], [((th_hi[:, c, :], th_lo[:, c, :]),
                                         down(c // 2, c % 2))
                                         for c in range(6)]).then_inc(s_down_made, 1)

            s_up(0)
            s_turn_x(1, 1, 1)
            pe.wait_ge(choices_marked, 1)
            m = msk[:, :, :].rearrange("p e q -> p (e q)")
            nc.tensor.matmul(bank[7][:, 0:E * NT], rconst("before"), m, start=True, stop=True)
            nc.tensor.matmul(bank[7][:, E * NT:2 * E * NT], rconst("ones"), m, start=True, stop=True).then_inc(counts_made, 1)

            def s_step(k, n, j):
                s_turn_h(k - 1)
                s_up(k)
                if not isinstance(k, int) or k + 1 < NT:
                    s_turn_x(k + 1, (j + 1) % 2, n + (j + 1) // 2 + 1)
                s_down(k - 1)

            for k in (1, 2):
                s_step(k, k // 2, k % 2)
            with pe.Fori(1, (NT - 1) // 2) as i:
                for j in (1, 2):
                    s_step(2 * i + j, i + j // 2, j % 2)
            s_step(NT - 1, (NT - 1) // 2, (NT - 1) % 2)
            s_turn_h(NT - 1)
            s_down(NT - 1)

            packed = pe.alloc_register("packed")

            def read_experts(i):
                pe.reg_load(packed, epack[0:1, bass.ds(i, 1)] if not isinstance(i, int) else epack[0:1, i:i + 1])

            def experts():
                w = pe.snap(packed)
                return [w // E ** j % E for j in range(XG + 2)]

            def e_turn_x(k, slot, uses):
                pe.wait_ge(gathered[slot], 16 * uses)
                if not isinstance(k, int) or k >= 1:
                    pe.wait_ge(e_xt_lo_made, k)
                for c in range(K2):
                    last = nc.tensor.transpose(bank[0][:, c * P:(c + 1) * P], xg[:, slot, c * P:(c + 1) * P], ident)
                last.then_inc(e_x_turned, 1)

            def e_up(k, par, e):
                pe.wait_ge(e_xt_lo_made, k + 1)
                if not isinstance(k, int) or k >= 2:
                    pe.wait_ge(e_gated_made, k - 1)
                split3(bank[1 + par][:, 0:2 * EI],
                       [((xt2_hi[par][:, b * P:(b + 1) * P], xt2_lo[par][:, b * P:(b + 1) * P]), up(e, b))
                        for b in range(K2)]).then_inc(e_up_made, 1)

            def e_turn_h(k, par):
                pe.wait_ge(e_gated_made, k + 1)
                if not isinstance(k, int) or k >= 1:
                    pe.wait_ge(e_th_lo_made, k)
                for c in range(2):
                    last = nc.tensor.transpose(bank[5][0:EK, c * P:(c + 1) * P], act_h[:, (2 * par + c) * EK:(2 * par + c + 1) * EK], ident)
                last.then_inc(e_h_turned, 1)

            def e_down(k, par, e):
                pe.wait_ge(e_th_lo_made, k + 1)
                if not isinstance(k, int) or k >= 1:
                    pe.wait_ge(e_y_made, k)
                split3(bank[7][:, 0:D], [((et_hi[par][:, c, :], et_lo[par][:, c, :]),
                                         down(e, c, EK))
                                         for c in range(2)]).then_inc(e_down_made, 1)

            pe.wait_ge(tile_experts_known, 1)
            e_turn_x(0, 0, 1)
            e_turn_x(1, 1, 1)
            pe.wait_ge(unit_lo_made, E - SH + 5)
            read_experts(0)

            def e_step(k, n, j, ahead, e):
                e_up(k, j % 2, e[j])
                if not isinstance(k, int) or k + 2 < XT:
                    e_turn_x(k + 2, (j + 2) % XG, n + (j + 2) // XG + 1)
                if not isinstance(k, int) or k >= 1:
                    e_turn_h(k - 1, (j - 1) % 2)
                if not isinstance(k, int) or k >= 2:
                    e_down(k - 2, j % 2, e[j - 2])
                if ahead and j == XG:
                    read_experts(n + 1)

            rounds = (XT - 2) // XG
            e = experts()
            for j in range(2):
                e_step(j, 0, j, False, e)
            pe.wait_ge(s_added, NT)
            pe.wait_ge(unit_lo_made, E - SH + 8)
            for j in range(2, XG + 2):
                e_step(j, 0, j, True, e)
            with pe.Fori(1, rounds) as i:
                e = experts()
                for j in range(2, XG + 2):
                    e_step(i * XG + j, i, j, True, e)
            e = experts()
            left = XT - rounds * XG
            for j in range(2, left):
                e_step(rounds * XG + j, rounds, j, False, e)
            e_turn_h(XT - 1, (XT - 1) % 2)
            for j in (left - 2, left - 1):
                e_down(rounds * XG + j, j % 2, e[j])


def kernel(**inputs):
    import concourse.bacc as _bacc
    from concourse.bass_utils import run_bass_kernel_spmd as _run

    nc = _bacc.Bacc("TRN2", target_bir_lowering=False, num_devices=1)
    arrays, args = {}, {}
    for name, a in layout(inputs).items():
        a = np.ascontiguousarray(a)
        arrays[f"in_{name}"] = a
        args[name] = nc.dram_tensor(f"in_{name}", a.shape, mybir.dt.from_np(a.dtype), kind="ExternalInput").ap()
    out = nc.dram_tensor("out_0", (BATCH, SEQ, D), F32, kind="ExternalOutput").ap()
    build(nc, out=out, **args)
    r = _run(nc, [arrays], core_ids=[0])
    return r.results[0]["out_0"]


def layout(inputs):
    g = {k: np.asarray(v) for k, v in inputs.items()}

    def blocks(w):
        return w.T.reshape(w.shape[1] // P, P, w.shape[0]).transpose(1, 0, 2)

    cw = g["L0_attn_C_w"]
    router = np.concatenate([g["L0_ffn_gate_w"], g["L0_ffn_shared_gate_vec"], np.zeros((32 - ER, D), np.float32)])
    small = np.concatenate([g["L0_attn_B_w"], g["L0_attn_dt_w"], cw, cw, g["L0_attn_out_w"], router])
    bias = np.zeros((P, 2), np.float32)
    bias[:N, 0] = g["L0_attn_B_b"]
    bias[N:N + H, 0] = g["L0_attn_dt_b"]
    bias[:N, 1] = bias[N:, 1] = g["L0_attn_C_b"]
    units = np.zeros((4 + E, P, WC), np.float32)
    units[:4, :, :WU] = (g["L0_ffn_shared_gate_up"].reshape(4, 2 * EI, K2, P).transpose(0, 3, 2, 1)).reshape(4, P, WU)
    shared_down = np.zeros((6 * P, D), np.float32)
    shared_down[:SI] = g["L0_ffn_shared_down"].T
    units[:3, :, WU:] = shared_down.reshape(3, 2, P, D).transpose(0, 2, 1, 3).reshape(3, P, WD)
    units[4:, :, :WU] = g["L0_ffn_expert_gate_up"].reshape(E, 2 * EI, K2, P).transpose(0, 3, 2, 1).reshape(E, P, WU)
    units[4:, :EK, WU:] = g["L0_ffn_expert_down"].reshape(E, D, 2, EK).transpose(0, 3, 2, 1).reshape(E, EK, WD)
    units[SH:] = np.roll(units[SH:], -SH, axis=0)
    cst, rcst = constants()
    return {
        "x": g["L0_attn_x"], "w_small": blocks(small), "w_bias": bias,
        "a_log": g["L0_attn_A_log"].reshape(1, H), "d_row": g["L0_attn_D"].reshape(1, H),
        "ob_row": g["L0_attn_out_b"].reshape(1, D), "cst_in": cst,
        "rcst_in": rcst, "w_units": units,
    }
```
